# Optimizing a Trainium2 kernel written in Bass

```python
import numpy as np
import jax
import jax.numpy as jnp

def _softmax(x, axis=-1):
    return jax.nn.softmax(x, axis=axis)

def _gelu(x):
    return jax.nn.gelu(x, approximate=True)

def _silu(x):
    return jax.nn.silu(x)

def _sigmoid(x):
    return jax.nn.sigmoid(x)

def _layernorm(x, axis=-1, eps=1e-05):
    m = jnp.mean(x, axis=axis, keepdims=True)
    v = jnp.var(x, axis=axis, keepdims=True)
    return (x - m) / jnp.sqrt(v + eps)

def _scatter_add(tgt, idx, src, axis=0):
    return tgt.at[idx].add(src)

def _segment_sum(src, seg, n):
    return jax.ops.segment_sum(src, seg, n)
kernel_name = 'mk_conv_preact_d2_conv_nchw512_r2_d25f9b'

def setup_inputs(seed: int=0):
    np.random.seed(seed)
    _w = jnp.asarray

    def _rec_inputs():
        import jax
        import jax.numpy as jnp
        _gk = jax.random.key(seed)
        x = -0.0001546 + 1 * jax.random.normal(jax.random.fold_in(_gk, 1), (8, 256, 64, 64), jnp.float32)
        return x
    x = _rec_inputs()

    def _L0_conv_setup():
        import jax, jax.numpy as jnp
        import numpy as np
        WS = 8
        SHIFT = 4
        HEADS = 16
        key = jax.random.key(seed)
        k1, k2, k3 = jax.random.split(key, 3)
        x = jax.random.normal(k1, (16, 256, 64, 64), dtype=jnp.float32)
        w = jax.random.normal(k2, (HEADS, WS * WS, WS * WS), dtype=jnp.float32) * 0.02
        b = jax.random.normal(k3, (HEADS, WS * WS), dtype=jnp.float32) * 0.02
        return {'x': x, 'w': w, 'b': b}
    _L0_conv_all = _L0_conv_setup()
    _L0_conv_in = {k: v for k, v in _L0_conv_all.items() if k in ('w', 'b')}
    del _L0_conv_all

    def _L1_conv_setup():
        import jax, jax.numpy as jnp
        from jax import lax
        import numpy as np
        DIM = 8
        BN_EPS = 1e-05
        ATT_EPS = 1e-15
        key = jax.random.key(seed)
        ks = jax.random.split(key, 6)
        B, C, H, W = (2, 256, 64, 64)
        total_dim = 256
        c3 = 3 * total_dim
        x = jax.random.normal(ks[0], (B, C, H, W), dtype=jnp.float32)
        w_qkv = jax.random.normal(ks[1], (c3, C), dtype=jnp.float32) * 0.02
        w_dw = jax.random.normal(ks[2], (c3, 1, 5, 5), dtype=jnp.float32) * 0.05
        w_pw = jax.random.normal(ks[3], (c3, 8, 1, 1), dtype=jnp.float32) * 0.1
        w_proj = jax.random.normal(ks[4], (256, 2 * total_dim), dtype=jnp.float32) * 0.02
        bn_gamma = jnp.ones((256,), jnp.float32)
        bn_beta = jnp.zeros((256,), jnp.float32)
        bn_mean = jnp.zeros((256,), jnp.float32)
        bn_var = jnp.ones((256,), jnp.float32)
        return {'x': x, 'w_qkv': w_qkv, 'w_dw': w_dw, 'w_pw': w_pw, 'w_proj': w_proj, 'bn_gamma': bn_gamma, 'bn_beta': bn_beta, 'bn_mean': bn_mean, 'bn_var': bn_var}
    _L1_conv_all = _L1_conv_setup()
    _L1_conv_in = {k: v for k, v in _L1_conv_all.items() if k in ('w_qkv', 'w_dw', 'w_pw', 'w_proj', 'bn_gamma', 'bn_beta', 'bn_mean', 'bn_var')}
    del _L1_conv_all
    return {'x': x, 'L0_conv_w': _L0_conv_in['w'], 'L0_conv_b': _L0_conv_in['b'], 'L1_conv_w_qkv': _L1_conv_in['w_qkv'], 'L1_conv_w_dw': _L1_conv_in['w_dw'], 'L1_conv_w_pw': _L1_conv_in['w_pw'], 'L1_conv_w_proj': _L1_conv_in['w_proj'], 'L1_conv_bn_gamma': _L1_conv_in['bn_gamma'], 'L1_conv_bn_beta': _L1_conv_in['bn_beta'], 'L1_conv_bn_mean': _L1_conv_in['bn_mean'], 'L1_conv_bn_var': _L1_conv_in['bn_var']}

def reference(x, L0_conv_w, L0_conv_b, L1_conv_w_qkv, L1_conv_w_dw, L1_conv_w_pw, L1_conv_w_proj, L1_conv_bn_gamma, L1_conv_bn_beta, L1_conv_bn_mean, L1_conv_bn_var):
    import jax
    import jax.numpy as jnp

    def _L0_conv_ref(x, w, b):
        import jax, jax.numpy as jnp
        import numpy as np
        WS = 8
        SHIFT = 4
        HEADS = 16
        ws, shift, heads = (WS, SHIFT, HEADS)
        B, C, H, W = x.shape
        hd = C // heads
        ws2 = ws * ws
        x = jnp.transpose(x, (0, 2, 3, 1))
        Pl, Pr, Pt, Pb = (ws - shift, shift, ws - shift, shift)
        x = jnp.pad(x, ((0, 0), (Pt, Pb), (Pl, Pr), (0, 0)))
        _H, _W = (H + ws, W + ws)
        nWh, nWw = (_H // ws, _W // ws)
        xw = x.reshape(B, nWh, ws, nWw, ws, C)
        xw = jnp.transpose(xw, (0, 1, 3, 2, 4, 5)).reshape(-1, ws2, heads, hd)
        xw = jnp.transpose(xw, (0, 2, 1, 3))
        y = jnp.einsum('nhjd,hij->nhid', xw, w) + b[None, :, :, None]
        y = jnp.transpose(y, (0, 2, 1, 3)).reshape(-1, ws, ws, C)
        y = y.reshape(B, nWh, nWw, ws, ws, C)
        y = jnp.transpose(y, (0, 1, 3, 2, 4, 5)).reshape(B, _H, _W, C)
        y = y[:, Pt:_H - Pb, Pl:_W - Pr, :]
        return jnp.transpose(y, (0, 3, 1, 2))

    def _L1_conv_ref(x, w_qkv, w_dw, w_pw, w_proj, bn_gamma, bn_beta, bn_mean, bn_var):
        import jax, jax.numpy as jnp
        from jax import lax
        import numpy as np
        DIM = 8
        BN_EPS = 1e-05
        ATT_EPS = 1e-15
        B, C, H, W = x.shape
        dn = ('NCHW', 'OIHW', 'NCHW')
        qkv = jnp.einsum('bchw,oc->bohw', x, w_qkv)
        y = lax.conv_general_dilated(qkv, w_dw, (1, 1), [(2, 2), (2, 2)], feature_group_count=w_dw.shape[0], dimension_numbers=dn)
        y = lax.conv_general_dilated(y, w_pw, (1, 1), [(0, 0), (0, 0)], feature_group_count=w_pw.shape[0] // w_pw.shape[1], dimension_numbers=dn)
        mqkv = jnp.concatenate([qkv, y], axis=1)
        N = H * W
        mqkv = mqkv.reshape(B, -1, 3 * DIM, N)
        q = jax.nn.relu(mqkv[:, :, :DIM])
        k = jax.nn.relu(mqkv[:, :, DIM:2 * DIM])
        v = mqkv[:, :, 2 * DIM:]
        v = jnp.pad(v, ((0, 0), (0, 0), (0, 1), (0, 0)), constant_values=1.0)
        vk = jnp.einsum('bhdn,bhen->bhde', v, k)
        out = jnp.einsum('bhde,bhen->bhdn', vk, q)
        out = out[:, :, :-1] / (out[:, :, -1:] + ATT_EPS)
        out = out.reshape(B, -1, H, W)
        out = jnp.einsum('bchw,oc->bohw', out, w_proj)
        inv = bn_gamma / jnp.sqrt(bn_var + BN_EPS)
        out = out * inv[None, :, None, None] + (bn_beta - bn_mean * inv)[None, :, None, None]
        return out

    def _gn(v, G=32, eps=1e-05):
        B_, C_, H_, W_ = v.shape
        g = v.reshape(B_, G, C_ // G, H_, W_)
        m = jnp.mean(g, axis=(2, 3, 4), keepdims=True)
        s = jnp.var(g, axis=(2, 3, 4), keepdims=True)
        return ((g - m) / jnp.sqrt(s + eps)).reshape(v.shape)

    def _ln_c(v, eps=1e-06):
        m = jnp.mean(v, axis=1, keepdims=True)
        s = jnp.var(v, axis=1, keepdims=True)
        return (v - m) / jnp.sqrt(s + eps)

    def _ln_t(v, eps=1e-05):
        m = jnp.mean(v, axis=-1, keepdims=True)
        s = jnp.var(v, axis=-1, keepdims=True)
        return (v - m) / jnp.sqrt(s + eps)

    def _to_tokens(v):
        B_, C_, H_, W_ = v.shape
        return v.reshape(B_, C_, H_ * W_).transpose(0, 2, 1)

    def _from_tokens(t, like):
        B_, C_, H_, W_ = like.shape
        return t.transpose(0, 2, 1).reshape(B_, C_, H_, W_)
    x = x + _L0_conv_ref(_gn(x), L0_conv_w, L0_conv_b)
    x = x + _L1_conv_ref(_gn(x), L1_conv_w_qkv, L1_conv_w_dw, L1_conv_w_pw, L1_conv_w_proj, L1_conv_bn_gamma, L1_conv_bn_beta, L1_conv_bn_mean, L1_conv_bn_var)
    return x

_drawn_inputs = setup_inputs


def setup_inputs(seed=0):
    import zlib

    import numpy as np

    out = dict(_drawn_inputs(seed))
    spreads = {'L1_conv_bn_gamma': (1.0, 0.6),
     'L1_conv_bn_beta': (0.0, 0.1),
     'L1_conv_bn_mean': (0.0, 0.1),
     'L1_conv_bn_var': (1.0, 0.6)}
    factors = {'L0_conv_b': 2.844,
     'L1_conv_w_qkv': 8.0,
     'L1_conv_w_dw': 8.0,
     'L1_conv_w_pw': 8.0,
     'L1_conv_w_proj': 8.0}
    for name, (base, spread) in spreads.items():
        noise = np.random.default_rng([zlib.crc32(name.encode()), seed]).standard_normal(out[name].shape)
        drawn = base * np.exp(spread * noise) if base else spread * noise
        out[name] = jnp.asarray(drawn.astype(out[name].dtype))
    for name, factor in factors.items():
        out[name] = (out[name] * factor).astype(out[name].dtype)
    return out
```

```python
from contextlib import ExitStack

import concourse.bass as bass
from concourse import mybir

F32 = mybir.dt.float32
F32R = mybir.dt.float32r
ALU = mybir.AluOpType
ACT = mybir.ActivationFunctionType
AX = mybir.AxisListType

P = 128
B, C, H, W = 8, 256, 64, 64
CT = C // P
GN_CH = 8
GN_EPS = 1e-5
WS, SHIFT, MIX_HEADS = 8, 4, 16
MIX_CH = C // MIX_HEADS
WIN_ROWS = (H + WS) // WS
PAIRS = (W + WS + 15) // 16
PAD_W = PAIRS * 16
WR = 3
GROUPS = WIN_ROWS // WR
GP = WR * PAIRS
FILLS = (GP + 1) // 2
D = 8
AH = 32
HT = P // D
QT = 6
NB = 16
PBK = NB + 1
PN = PBK * PBK
NPH = 16
POS = NB * NB
TAP = 8
BN_EPS = 1e-5
ATT_EPS = 1e-15
VW = P + 1


def at_least(eng, sem, value):
    if isinstance(value, int) and value <= 0:
        return
    eng.wait_ge(sem, value)


class Own:

    def __init__(self, eng, start):
        self.eng, self.start = eng, start

    def wait_ge(self, sem, value):
        if not isinstance(value, int):
            self.eng.wait_ge(self.start, 1)
        self.eng.wait_ge(sem, value)


def over_image_pairs(eng, body):
    body(0, False)
    with eng.Fori(1, B // 2 - 1) as i:
        body(i, False)
    body(B // 2 - 1, True)


class Chain:

    def __init__(self, eng, sem):
        self.eng, self.sem, self.base, self.n = eng, sem, 0, 0

    def __call__(self, ins):
        self.n += 1
        ins.then_inc(self.sem, 1)
        self.eng.wait_ge(self.sem, self.base + self.n)


STAT_LINKS = 11


def norm_moments(dve, chain, mv, bst, x, ct):
    flat = x[:, ct, :]
    for k in range(8):
        last = dve.bn_stats(bst[:, ct, k, :], flat[:, 512 * k:512 * k + 512])
    return last


def norm_scale(dve, chain, b, T, mv, bst, stat_ps, sem):
    for ct in range(CT):
        last = dve.bn_aggr(mv[:, ct, :], bst[:, ct, :, :].rearrange("p a s -> p (a s)"))
    last.then_inc(sem["moments"], 1)
    dve.wait_ge(sem["group_sum"], 2 * b + 1)
    chain(dve.tensor_tensor(T["dm"][:, :], mv[:, :, 0], stat_ps[:, 0:2], ALU.subtract))
    chain(dve.tensor_tensor(T["sq"][:, :], T["dm"][:, :], T["dm"][:, :], ALU.mult))
    dve.tensor_tensor(T["vc"][:, :], T["sq"][:, :], mv[:, :, 1], ALU.add).then_inc(sem["moments"], 1)
    dve.wait_ge(sem["group_sum"], 2 * b + 2)
    dve.tensor_scalar(T["ve"][:, :], stat_ps[:, 2:4], GN_EPS, None, ALU.add).then_inc(sem["var"], 1)
    dve.wait_ge(sem["std"], b + 1)
    chain(dve.reciprocal(T["r0"][:, :], T["std"][:, :]))
    chain(dve.tensor_tensor(T["t1"][:, :], T["r0"][:, :], T["r0"][:, :], ALU.mult))
    chain(dve.tensor_tensor(T["t2"][:, :], T["t1"][:, :], T["ve"][:, :], ALU.mult))
    chain(dve.tensor_scalar(T["t3"][:, :], T["t2"][:, :], -0.5, 1.5, ALU.mult, ALU.add))
    at_least(dve, sem["scaled"], b)
    chain(dve.tensor_tensor(T["sc"][:, :], T["r0"][:, :], T["t3"][:, :], ALU.mult))
    dve.scalar_tensor_tensor(T["nb"][:, :], stat_ps[:, 0:2], -1.0, T["sc"][:, :], ALU.mult,
                             ALU.mult).then_inc(sem["scale"], 1)


NORM_CHAIN = 7


def norm_group_sums(pe, b, T, mv, stat_ps, gavg, sem):
    pe.wait_ge(sem["moments"], 2 * b + 1)
    pe.matmul(stat_ps[:, 0:2], gavg[:, :], mv[:, :, 0], start=True, stop=True).then_inc(sem["group_sum"], 1)
    pe.wait_ge(sem["moments"], 2 * b + 2)
    pe.matmul(stat_ps[:, 2:4], gavg[:, :], T["vc"][:, :], start=True, stop=True).then_inc(sem["group_sum"], 1)


def norm_std(act, b, T, sem):
    act.wait_ge(sem["var"], b + 1)
    act.activation(T["std"][:, :], T["ve"][:, :], ACT.Sqrt).then_inc(sem["std"], 1)


def norm_tiles(sb, sem_of, tag):
    T = {n: sb(f"{tag}_{n}", [P, CT], F32) for n in
         ("dm", "sq", "vc", "ve", "std", "r0", "t1", "t2", "t3", "sc", "nb", "used")}
    sem = {n: sem_of(f"{tag}_{n}") for n in ("moments", "group_sum", "var", "std", "scale", "scaled", "chain")}
    return T, sem


def make_constants(nc, ctx, K):
    def sb(name, shape):
        return ctx.enter_context(nc.sbuf_tensor(name, shape, F32))
    K["ident"] = sb("ident", [P, P])
    K["gmask"] = sb("gmask", [P, P])
    K["gavg"] = sb("gavg", [P, P])
    K["same_ch"] = sb("same_ch", [P, P])
    K["vk"] = sb("vk_direct", [P, B, 2, VW])
    with ExitStack() as c2:
        done = c2.enter_context(nc.semaphore("const_done"))
        block = c2.enter_context(nc.Block())

        @block.gpsimd
        def _(pool):
            n = 0

            def step(ins):
                nonlocal n
                n += 1
                ins.then_inc(done, 1)
                pool.wait_ge(done, n)
            step(pool.memset(K["ident"][:, :], 0.0))
            step(pool.affine_select(out=K["ident"][:, :], in_=K["ident"][:, :], compare_op=ALU.not_equal,
                                    fill=1.0, base=0, pattern=[[-1, P]], channel_multiplier=1))
            step(pool.memset(K["gmask"][:, :], 1.0))
            g = K["gmask"][:, :].rearrange("p (a c) -> p a c", c=GN_CH)
            step(pool.affine_select(out=g, in_=g, compare_op=ALU.is_ge, fill=0.0, base=0,
                                    pattern=[[-GN_CH, P // GN_CH], [0, GN_CH]], channel_multiplier=1))
            step(pool.affine_select(out=g, in_=g, compare_op=ALU.is_ge, fill=0.0, base=GN_CH - 1,
                                    pattern=[[GN_CH, P // GN_CH], [0, GN_CH]], channel_multiplier=-1))
            step(pool.tensor_scalar(K["gavg"][:, :], K["gmask"][:, :], 1.0 / GN_CH, None, ALU.mult))
            step(pool.memset(K["same_ch"][:, :], 0.0))
            s = K["same_ch"][:, :].rearrange("p (a c) -> p a c", c=D)
            for m in range(NPH):
                step(pool.affine_select(out=s, in_=s, compare_op=ALU.not_equal, fill=1.0, base=-D * m,
                                        pattern=[[0, NPH], [-1, D]], channel_multiplier=1))


def window_mixing(nc, K, x_in, w_mix, b_mix, x1_dram):
    with ExitStack() as ctx:
        def sb(name, shape, dt=F32):
            return ctx.enter_context(nc.sbuf_tensor(name, shape, dt))

        def psum(name, shape):
            return ctx.enter_context(nc.psum_tensor(name, shape, F32))

        def sem(name):
            return ctx.enter_context(nc.semaphore(name))

        x = [sb(f"mx{i}", [P, CT, H * W]) for i in range(2)]
        xpad = sb("xpad", [P, CT, PAIRS, H + WS, 16])
        xT = sb("xT", [P, 2, GP, C])
        yT = sb("yT", [P, 2, GP, C])
        w_raw = sb("w_raw", [P, MIX_HEADS, P])
        wT = sb("wT", [P, MIX_HEADS, P])
        w_in = sb("w_in", [P, MIX_HEADS, WS * WS])
        side = sb("side", [P, 2])
        bias = sb("mix_bias", [P, MIX_HEADS])
        bst = sb("mbst", [P, CT, 8, 6])
        mv = sb("mmv", [P, CT, 2])
        T, ns = norm_tiles(sb, sem, "m")

        t_ps = psum("t_ps", [P, 2, 512])
        m_ps = psum("m_ps", [P, 2, 512])
        k_ps = psum("k_ps", [P, 3, 512])
        stat_ps = psum("mstat_ps", [P, 4])

        w_loaded, w_zero = sem("w_loaded"), sem("w_zero")
        w_turned, w_ready = sem("w_turned"), sem("w_ready")
        pad_zero = sem("pad_zero")
        x_loaded = [sem(f"x_loaded{i}") for i in range(2)]
        x_stored = [sem(f"x_stored{i}") for i in range(2)]
        x1_done = sem("x1_done")
        t_full, t_taken = sem("t_full"), sem("t_taken")
        m_full, m_taken = sem("m_full"), sem("m_taken")
        k_full, k_taken = sem("k_full"), sem("k_taken")
        xn_ready = sem("xn_ready")
        counted = sem("m_counted")
        N_T, N_M, N_K = GROUPS * FILLS, GROUPS * MIX_HEADS // 2, WIN_ROWS

        block = ctx.enter_context(nc.Block())

        @block.sync
        def _(sp):
            for r in range(WS):
                for w in range(2):
                    p0 = 16 * r + 8 * w
                    sp.dma_start(w_in[p0:p0 + 8, :, :], w_mix[:, 8 * r:8 * r + 8, :].rearrange("h i j -> i h j"))\
                        .then_inc(w_loaded, 16)
                    with nc.allow_non_contiguous_dma(reason="2048 values"):
                        sp.dma_start(bias[p0:p0 + 8, :], b_mix[:, 8 * r:8 * r + 8].rearrange("h i -> i h"))\
                            .then_inc(w_loaded, 16)

            def body(i, last):
                for par in range(2):
                    b = 2 * i + par
                    sp.wait_ge(x1_done, b + 1)
                    sp.dma_start(x1_dram[b, :, :].rearrange("(t p) n -> p t n", p=P), x[par][:, :, :])\
                        .then_inc(x_stored[par], 16)
            over_image_pairs(sp, body)
            for par in range(2):
                sp.wait_ge(x_stored[par], 16 * (B // 2))

        @block.gpsimd
        def _(pool):
            pool.memset(xpad[:, :, :, :, :], 0.0).then_inc(pad_zero, 1)

            def body(i, last):
                for par in range(2):
                    b = 2 * i + par
                    at_least(pool, x_stored[par], 16 * i)
                    pool.dma_start(x[par][:, :, :], x_in[b, :, :, :].rearrange("(t p) h w -> p t (h w)", p=P))\
                        .then_inc(x_loaded[par], 16)
            over_image_pairs(pool, body)

        @block.scalar
        def _(act):
            for f in range(MIX_HEADS // 4):
                act.wait_ge(w_turned, f + 1)
                act.activation(wT[:, 4 * f:4 * f + 4, :].rearrange("p h m -> p (h m)"), t_ps[:, f % 2, :],
                               ACT.Copy).then_inc(w_ready, 1)
            act.wait_ge(pad_zero, 1)
            norm_std(act, 0, T, ns)

            def normalise(b, par):
                act.wait_ge(ns["scale"], b + 1)
                at_least(act, t_full, N_T * b)
                for ct in range(CT):
                    for q0, q1, c0, c1 in ((0, 1, SHIFT, 16), (1, PAIRS - 1, 0, 16), (PAIRS - 1, PAIRS, 0, SHIFT)):
                        x0 = 16 * q0 + c0 - SHIFT
                        cols = (q1 - q0) * (c1 - c0)
                        src = x[par][:, ct, :].rearrange("p (h w) -> p h w", w=W)[:, :, x0:x0 + cols]\
                            .rearrange("p h (q c) -> p h q c", q=q1 - q0)
                        dst = xpad[:, ct, q0:q1, SHIFT:SHIFT + H, c0:c1].rearrange("p q h c -> p h q c")
                        last = act.activation(dst, src, ACT.Identity, bias=T["nb"][:, ct:ct + 1],
                                              scale=T["sc"][:, ct:ct + 1])
                last.then_inc(xn_ready, 1)
                act.wait_ge(xn_ready, b + 1)
                act.activation(T["used"][:, 0:1], T["sc"][:, 0:1], ACT.Copy).then_inc(ns["scaled"], 1)

            def body(i, last_body):
                for par in range(2):
                    b = 2 * i + par
                    normalise(b, par)
                    for g in range(GROUPS):
                        at_least(act, m_full, N_M * b + (MIX_HEADS // 2) * (g - 1))
                        for f in range(FILLS):
                            n = FILLS * g + f
                            np_ = min(2, GP - 2 * f)
                            act.wait_ge(t_full, N_T * b + n + 1)
                            act.activation(xT[:, (g + par) % 2, 2 * f:2 * f + np_, :].rearrange("p a c -> p (a c)"),
                                           t_ps[:, n % 2, 0:np_ * C], ACT.Copy).then_inc(t_taken, 1)
                        if g == 2 and not (last_body and par == 1):
                            norm_std(act, b + 1, T, ns)
            over_image_pairs(act, body)

        @block.tensor
        def _(pe):
            pe.wait_ge(w_zero, 3)
            for f in range(MIX_HEADS // 4):
                at_least(pe, w_ready, f - 1)
                for j in range(4):
                    last = pe.transpose(t_ps[:, f % 2, P * j:P * j + P], w_raw[:, 4 * f + j, :], K["ident"][:, :])
                last.then_inc(w_turned, 1)
            pe.wait_ge(w_ready, MIX_HEADS // 4)
            norm_group_sums(pe, 0, T, mv, stat_ps, K["gavg"], ns)

            def turn(b, g):
                for f in range(FILLS):
                    n = FILLS * g + f
                    at_least(pe, t_taken, N_T * b + n - 1)
                    for a in range(2 * f, min(2 * f + 2, GP)):
                        wy, q = WR * g + a // PAIRS, a % PAIRS
                        for ct in range(CT):
                            o = (a - 2 * f) * C + ct * P
                            last = pe.transpose(t_ps[:, n % 2, o:o + P],
                                                xpad[:, ct, q, WS * wy:WS * wy + WS, :].rearrange("p r c -> p (r c)"), K["ident"][:, :])
                    last.then_inc(t_full, 1)

            def mix(b, g, par):
                for hp in range(MIX_HEADS // 2):
                    n = (MIX_HEADS // 2) * g + hp
                    if hp == 0:
                        pe.wait_ge(t_taken, N_T * b + FILLS * (g + 1))
                    at_least(pe, m_taken, N_M * b + n - 1)
                    for j in range(2):
                        h = 2 * hp + j
                        last = pe.matmul(m_ps[:, n % 2, j * GP * MIX_CH:(j + 1) * GP * MIX_CH], wT[:, h, :],
                                         xT[:, (g + par) % 2, :, MIX_CH * h:MIX_CH * h + MIX_CH],
                                         start=True, stop=True)
                    last.then_inc(m_full, 1)

            def turn_back(b, g, par):
                pe.wait_ge(m_taken, N_M * b + (MIX_HEADS // 2) * (g + 1))
                for r in range(WR):
                    wy = WR * g + r
                    at_least(pe, k_taken, N_K * b + wy)
                    for q in range(PAIRS):
                        for ct in range(CT):
                            dst = k_ps[:, ct, P * q:P * q + P] if q < 4 else k_ps[:, 2, P * ct:P * ct + P]
                            last = pe.transpose(dst, yT[:, (g + par) % 2, PAIRS * r + q, P * ct:P * ct + P], K["ident"][:, :])
                    last.then_inc(k_full, 1)

            def body(i, last_body):
                for par in range(2):
                    b = 2 * i + par
                    pe.wait_ge(xn_ready, b + 1)
                    turn(b, 0)
                    turn(b, 1)
                    mix(b, 0, par)
                    turn(b, 2)
                    mix(b, 1, par)
                    turn_back(b, 0, par)
                    if not (last_body and par == 1):
                        norm_group_sums(pe, b + 1, T, mv, stat_ps, K["gavg"], ns)
                    mix(b, 2, par)
                    turn_back(b, 1, par)
                    turn_back(b, 2, par)
            over_image_pairs(pe, body)

        @block.vector
        def _(dve):
            chain = Chain(dve, ns["chain"])

            def stats(b, par, i_next):
                chain.base, chain.n = NORM_CHAIN * b, 0
                norm_scale(dve, chain, b, T, mv, bst, stat_ps, ns)

            def moments(b, par, i, ct):
                if ct == 0:
                    dve.wait_ge(x_loaded[par], 16 * (i + 1))
                norm_moments(dve, chain, mv, bst, x[par], ct).then_inc(counted, 1)
                if ct == CT - 1:
                    dve.wait_ge(counted, CT * (b + 1))
                    dve.tensor_copy(T["t1"][:, 0:1], K["ident"][:, 0:1])

            dve.tensor_reduce(side[:, :], K["gmask"][:, :].rearrange("p (a w c) -> p w a c", w=2, c=8)[:, :, :, 0],
                              AX.X, ALU.add).then_inc(w_zero, 1)
            dve.wait_ge(w_zero, 1)
            dve.wait_ge(w_loaded, 16 * 4 * WS)
            for w in range(2):
                dve.tensor_scalar(w_raw[:, :, :].rearrange("p h (r w c) -> p h r w c", w=2, c=8)[:, :, :, w, :],
                                  w_in[:, :, :].rearrange("p h (r c) -> p h r c", c=8), side[:, w:w + 1], None,
                                  ALU.mult).then_inc(w_zero, 1)
            moments(0, 0, 0, 0)
            moments(0, 0, 0, 1)
            stats(0, 0, 0)

            def add_bias(b, g, par):
                for hp in range(MIX_HEADS // 2):
                    n = (MIX_HEADS // 2) * g + hp
                    if hp == 0:
                        at_least(dve, k_full, N_K * b + WR * (g - 1))
                    dve.wait_ge(m_full, N_M * b + n + 1)
                    c0 = 2 * hp * MIX_CH
                    out = yT[:, (g + par) % 2, :, c0:c0 + 2 * MIX_CH].rearrange("p a (h c) -> p h a c", h=2)
                    src = m_ps[:, n % 2, 0:2 * GP * MIX_CH].rearrange("p (h a c) -> p h a c", h=2, c=MIX_CH)
                    bb = bias[:, 2 * hp:2 * hp + 2].unsqueeze(2).unsqueeze(3).broadcast_to([P, 2, GP, MIX_CH])
                    dve.tensor_tensor(out, src, bb, ALU.add).then_inc(m_taken, 1)

            def add_rows(b, g, par):
                img = x[par][:, :, :].rearrange("p t (h w) -> p t h w", w=W)
                for r in range(WR):
                    wy = WR * g + r
                    r0, r1 = max(0, SHIFT - WS * wy), min(WS, H + SHIFT - WS * wy)
                    y0 = WS * wy + r0 - SHIFT
                    y1 = y0 + r1 - r0
                    dve.wait_ge(k_full, N_K * b + wy + 1)
                    for ct in range(CT):
                        quad = k_ps[:, ct, :].rearrange("p (q r c) -> p r q c", q=4, c=16)
                        left = img[:, ct, y0:y1, 0:12]
                        dve.tensor_tensor(left, left, quad[:, r0:r1, 0, SHIFT:16], ALU.add)
                        mid = img[:, ct, y0:y1, 12:60].rearrange("p r (q c) -> p r q c", c=16)
                        dve.tensor_tensor(mid, mid, quad[:, r0:r1, 1:4, :], ALU.add)
                        right = img[:, ct, y0:y1, 60:64]
                        edge = k_ps[:, 2, P * ct:P * ct + P].rearrange("p (r c) -> p r c", c=16)
                        last = dve.tensor_tensor(right, right, edge[:, r0:r1, 0:SHIFT], ALU.add)
                    last.then_inc(k_taken, 1)
                return last

            def body(i, last_body):
                for par in range(2):
                    b = 2 * i + par
                    nxt = not (last_body and par == 1)
                    npar, ni = (1, i) if par == 0 else (0, i + 1)
                    add_bias(b, 0, par)
                    if nxt:
                        moments(b + 1, npar, ni, 0)
                    add_bias(b, 1, par)
                    dve.wait_ge(xn_ready, b + 1)
                    add_rows(b, 0, par)
                    if nxt:
                        moments(b + 1, npar, ni, 1)
                        stats(b + 1, npar, ni)
                    add_bias(b, 2, par)
                    add_rows(b, 1, par)
                    add_rows(b, 2, par)
                    dve.wait_ge(k_taken, N_K * (b + 1))
                    dve.tensor_copy(T["dm"][:, 0:1], T["sc"][:, 0:1]).then_inc(x1_done, 1)
            over_image_pairs(dve, body)


def projections(nc, K, w_qkv, x1_dram, qkv_dram):
    with ExitStack() as ctx:
        def sb(name, shape, dt=F32):
            return ctx.enter_context(nc.sbuf_tensor(name, shape, dt))

        def psum(name, shape):
            return ctx.enter_context(nc.psum_tensor(name, shape, F32))

        def sem(name):
            return ctx.enter_context(nc.semaphore(name))

        NCH = 8
        TILES = (2, 4, 3, 5, 0, 1)
        x1 = [sb(f"px{i}", [P, CT, H * W]) for i in range(2)]
        xn = sb("xn", [P, 2, CT, 512])
        xh = sb("xh", [P, 2, CT, 512], F32R)
        xl = sb("xl", [P, 2, CT, 512], F32R)
        w_raw = sb("wq_raw", [P, QT, C])
        wh = sb("wqh", [P, CT, QT * P], F32R)
        wl = sb("wql", [P, CT, QT * P], F32R)
        stage = sb("stage", [P, 4, QT, 2, PN])
        kv = sb("kv", [P, 2, 4, 512])
        kT = sb("kT", [P, 2, 4, P])
        vT = sb("vT", [P, 2, 4, VW])
        tick = sb("ptick", [P, 4])
        bst = sb("pbst", [P, CT, 8, 6])
        mv = sb("pmv", [P, CT, 2])
        T, ns = norm_tiles(sb, sem, "p")

        o_ps = psum("o_ps", [P, 3, 512])
        t_ps = psum("pt_ps", [P, 2, 512])
        vk_ps = psum("vk_ps", [P, 2, 512])
        stat_ps = psum("pstat_ps", [P, 4])

        w_loaded, w_turned, w_split = sem("wq_loaded"), sem("wq_turned"), sem("wq_split")
        zeroed = sem("zeroed")
        x_loaded = [sem(f"x1_loaded{i}") for i in range(2)]
        xn_ready, x_free = sem("pxn_ready"), sem("px_free")
        xh_ready, xl_ready = sem("xh_ready"), sem("xl_ready")
        o_full = sem("o_full")
        kv_ready, q_ready = sem("kv_ready"), sem("q_ready")
        kv_ready_v, q_ready_v = sem("kv_ready_v"), sem("q_ready_v")
        staged = sem("staged")
        t_full, k_turned, v_turned = sem("pt_full"), sem("k_turned"), sem("v_turned")
        vk_full, vk_taken = sem("vk_full"), sem("vk_taken")
        stored = [sem(f"qkv_stored{i}") for i in range(4)]
        counted = sem("p_counted")

        def place(n):
            return 2 * (n // 4) + n % 2

        def uses(n):
            return sum(place(m) == place(n) for m in range(n))

        def inside(t, n):
            c = place(n)
            return stage[:, c, t, :, :].rearrange("p a (y x) -> p a y x", x=PBK)[:, :, c // 2:c // 2 + NB, c % 2:c % 2 + NB]

        def dense(ap):
            return ap.rearrange("p (a y x) -> p a y x", a=2, x=NB)

        block = ctx.enter_context(nc.Block())

        @block.sync
        def _(sp):
            for t in range(QT):
                src = w_qkv.rearrange("(h k c) i -> k h c i", k=3, c=D)[t // 2, HT * (t % 2):HT * (t % 2) + HT, :, :]
                for h in range(HT):
                    sp.dma_start(w_raw[D * h:D * h + D, t, :], src[h, :, :]).then_inc(w_loaded, 16)

            own = Own(sp, w_loaded)

            def body(i, last):
                for par in range(2):
                    b = 2 * i + par
                    for n in range(NCH):
                        c = place(n)
                        p0 = 4 * ((n // 2 + 2) % 4) + 2 * ((n + 1) % 2)
                        own.wait_ge(staged, NCH * b + n + 1)
                        for t in (2, 4, 3, 5):
                            sp.dma_start(qkv_dram[P * t:P * t + P, p0:p0 + 2, b, :], stage[:, c, t, :, :])\
                                .then_inc(stored[c], 16)
                        own.wait_ge(q_ready, NCH * b + n + 1)
                        own.wait_ge(q_ready_v, NCH * b + n + 1)
                        for t in (0, 1):
                            sp.dma_start(qkv_dram[P * t:P * t + P, p0:p0 + 2, b, :], stage[:, c, t, :, :])\
                                .then_inc(stored[c], 16)
            over_image_pairs(sp, body)
            for c in range(4):
                sp.wait_ge(stored[c], 16 * QT * 2 * B)

        def stage_free(eng, b, n):
            at_least(eng, stored[place(n)], 16 * QT * (2 * b + uses(n)))

        @block.gpsimd
        def _(pool):
            pool.memset(stage[:, :, :, :, :], 0.0).then_inc(zeroed, 1)
            pool.memset(vT[:, :, :, P:VW], 1.0).then_inc(zeroed, 1)
            pool.wait_ge(zeroed, 2)

            def body(i, last_body):
                for par in range(2):
                    b = 2 * i + par
                    for n in range(NCH):
                        pool.wait_ge(kv_ready, 2 * (NCH * b + n + 1))
                        pool.wait_ge(kv_ready_v, 2 * (NCH * b + n + 1))
                        stage_free(pool, b, n)
                        pool.tensor_tensor(tick[:, n % 4:n % 4 + 1], K["ident"][:, 0:1], K["ident"][:, 1:2], ALU.add)
                        for j, t in enumerate((2, 4, 3, 5)):
                            last = pool.tensor_copy(inside(t, n), dense(kv[:, n % 2, j, :]))
                        last.then_inc(staged, 1)
            over_image_pairs(pool, body)

        @block.scalar
        def _(act):
            def load(b, par):
                act.dma_start(x1[par][:, :, :], x1_dram[b, :, :].rearrange("(t p) n -> p t n", p=P))\
                    .then_inc(x_loaded[par], 16)

            load(0, 0)
            load(1, 1)
            for f in range(3):
                act.wait_ge(w_turned, f + 1)
                act.activation(wh[:, :, P * 2 * f:P * 2 * f + 2 * P], t_ps[:, f % 2, :].rearrange("p (c m) -> p c m", c=CT),
                               ACT.Copy).then_inc(w_split, 1)
                act.wait_ge(w_split, 2 * f + 2)
            norm_std(act, 0, T, ns)
            act.wait_ge(zeroed, 2)

            def split(b, n, par):
                if n == 0:
                    act.wait_ge(ns["scale"], b + 1)
                at_least(act, xl_ready, NCH * b + n - 1)
                py, px = n // 2, 2 * (n % 2)
                for ct in range(CT):
                    src = x1[par][:, ct, :].rearrange("p (y py x px) -> p py px y x", py=4, x=NB, px=4)[:, py, px:px + 2, :, :]
                    last = act.activation(dense(xn[:, n % 2, ct, :]), src, ACT.Identity, bias=T["nb"][:, ct:ct + 1],
                                          scale=T["sc"][:, ct:ct + 1])
                last.then_inc(xn_ready, 1)
                act.wait_ge(xn_ready, NCH * b + n + 1)
                if n == NCH - 1:
                    act.activation(T["used"][:, 0:1], T["nb"][:, 0:1], ACT.Copy).then_inc(ns["scaled"], 1)
                at_least(act, o_full, QT * (NCH * b + n - 1))
                act.activation(xh[:, n % 2, :, :], xn[:, n % 2, :, :], ACT.Copy).then_inc(xh_ready, 1)

            def body(i, last_body):
                for par in range(2):
                    b = 2 * i + par
                    split(b, 0, par)
                    for n in range(NCH):
                        if n + 1 < NCH:
                            split(b, n + 1, par)
                        o0 = QT * (NCH * b + n)
                        for u in range(2):
                            act.wait_ge(o_full, o0 + 2 * u + 1)
                            if u == 0:
                                at_least(act, staged, NCH * b + n - 1)
                                at_least(act, t_full, 4 * (NCH * b + n - 1))
                            act.activation(kv[:, n % 2, 2 * u, :], o_ps[:, (2 * u) % 3, :], ACT.Copy).then_inc(kv_ready, 1)
                        act.wait_ge(o_full, o0 + 5)
                        stage_free(act, b, n)
                        act.activation(inside(0, n), dense(o_ps[:, 1, :]), ACT.Copy).then_inc(q_ready, 1)
                        for u in range(2):
                            act.wait_ge(t_full, 4 * (NCH * b + n) + 2 * u + 1)
                            at_least(act, vk_full, NCH * b + n)
                            act.activation(kT[:, u, :, :].rearrange("p a c -> p (a c)"), t_ps[:, 0, :], ACT.Relu)\
                                .then_inc(k_turned, 1)
                        if n == 6 and not (last_body and par == 1):
                            norm_std(act, b + 1, T, ns)
                    if not last_body:
                        act.wait_ge(x_free, b + 1)
                        act.dma_start(x1[par][:, :, :], x1_dram[b + 2, :, :].rearrange("(t p) n -> p t n", p=P))\
                            .then_inc(x_loaded[par], 16)
            over_image_pairs(act, body)

        @block.tensor
        def _(pe):
            pe.wait_ge(w_loaded, 16 * QT * HT)
            for f in range(3):
                at_least(pe, w_split, 2 * (f - 1))
                for ct in range(CT):
                    for j in range(2):
                        last = pe.transpose(t_ps[:, f % 2, P * (2 * ct + j):P * (2 * ct + j) + P],
                                            w_raw[:, 2 * f + j, P * ct:P * ct + P], K["ident"][:, :])
                last.then_inc(w_turned, 1)
            norm_group_sums(pe, 0, T, mv, stat_ps, K["gavg"], ns)
            pe.wait_ge(w_split, 6)
            pe.wait_ge(zeroed, 2)

            def product(b, n, j):
                t = TILES[j]
                if j == 0:
                    at_least(pe, kv_ready_v, 2 * (NCH * b + n))
                    at_least(pe, q_ready, NCH * b + n)
                if j == 1:
                    at_least(pe, q_ready, NCH * b + n)
                if j == 2:
                    at_least(pe, q_ready_v, NCH * b + n)
                if j == 3:
                    pe.wait_ge(kv_ready, 2 * (NCH * b + n) + 1)
                if j == 4:
                    pe.wait_ge(kv_ready_v, 2 * (NCH * b + n) + 1)
                if j == 5:
                    pe.wait_ge(kv_ready, 2 * (NCH * b + n) + 2)
                k = 0
                for ct in range(CT):
                    for w, xx in ((wh, xh), (wl, xh), (wh, xl)):
                        last = pe.matmul(o_ps[:, j % 3, :], w[:, ct, P * t:P * t + P], xx[:, n % 2, ct, :],
                                         start=(k == 0), stop=(k == 5))
                        k += 1
                last.then_inc(o_full, 1)

            def turn(b, n, u):
                at_least(pe, k_turned, 2 * (NCH * b + n) + u)
                at_least(pe, v_turned, 2 * (NCH * b + n) + u)
                if u == 0:
                    pe.wait_ge(kv_ready, 2 * (NCH * b + n + 1))
                    pe.wait_ge(kv_ready_v, 2 * (NCH * b + n + 1))
                for s in range(2):
                    for a in range(4):
                        last = pe.transpose(t_ps[:, s, P * a:P * a + P], kv[:, n % 2, 2 * u + s, P * a:P * a + P],
                                            K["ident"][:, :])
                    last.then_inc(t_full, 1)

            def sum_vk(b, n, u):
                pe.wait_ge(k_turned, 2 * (NCH * b + n) + u + 1)
                pe.wait_ge(v_turned, 2 * (NCH * b + n) + u + 1)
                if n == 0:
                    at_least(pe, vk_taken, 2 * b)
                for a in range(4):
                    last = pe.matmul(vk_ps[:, u, 0:VW], kT[:, u, a, :], vT[:, u, a, :],
                                     start=(n == 0 and a == 0), stop=(n == NCH - 1 and a == 3))
                if u == 1:
                    last.then_inc(vk_full, 1)

            def body(i, last_body):
                for par in range(2):
                    b = 2 * i + par
                    for n in range(NCH):
                        pe.wait_ge(xh_ready, NCH * b + n + 1)
                        pe.wait_ge(xl_ready, NCH * b + n + 1)
                        for j in range(4):
                            product(b, n, j)
                        product(b, n, 4)
                        turn(b, n, 0)
                        product(b, n, 5)
                        turn(b, n, 1)
                        sum_vk(b, n, 0)
                        sum_vk(b, n, 1)
                        if n == 6 and not (last_body and par == 1):
                            norm_group_sums(pe, b + 1, T, mv, stat_ps, K["gavg"], ns)
            over_image_pairs(pe, body)

        @block.vector
        def _(dve):
            chain = Chain(dve, ns["chain"])
            for f in range(3):
                dve.wait_ge(w_split, 2 * f + 1)
                hi = wh[:, :, P * 2 * f:P * 2 * f + 2 * P]
                dve.tensor_tensor(wl[:, :, P * 2 * f:P * 2 * f + 2 * P], t_ps[:, f % 2, :].rearrange("p (c m) -> p c m", c=CT),
                                  hi.bitcast(F32), ALU.subtract).then_inc(w_split, 1)

            def moments(b, par, i, ct):
                if ct == 0:
                    dve.wait_ge(x_loaded[par], 16 * (i + 1))
                norm_moments(dve, chain, mv, bst, x1[par], ct).then_inc(counted, 1)
                if ct == CT - 1:
                    dve.wait_ge(counted, CT * (b + 1))
                    dve.tensor_copy(T["t1"][:, 0:1], K["ident"][:, 0:1])

            def scale(b):
                chain.base, chain.n = NORM_CHAIN * b, 0
                norm_scale(dve, chain, b, T, mv, bst, stat_ps, ns)

            moments(0, 0, 0, 0)
            moments(0, 0, 0, 1)
            scale(0)
            dve.wait_ge(zeroed, 2)

            def split(b, n):
                dve.wait_ge(xh_ready, NCH * b + n + 1)
                dve.tensor_tensor(xl[:, n % 2, :, :], xn[:, n % 2, :, :], xh[:, n % 2, :, :].bitcast(F32),
                                  ALU.subtract).then_inc(xl_ready, 1)

            def body(i, last_body):
                for par in range(2):
                    b = 2 * i + par
                    nxt = not (last_body and par == 1)
                    npar, ni = (1, i) if par == 0 else (0, i + 1)
                    split(b, 0)
                    for n in range(NCH):
                        if n + 1 < NCH:
                            split(b, n + 1)
                        if n == NCH - 1:
                            dve.wait_ge(xn_ready, NCH * (b + 1))
                            dve.tensor_copy(T["t1"][:, 0:1], K["ident"][:, 0:1]).then_inc(x_free, 1)
                        o0 = QT * (NCH * b + n)
                        for u in range(2):
                            dve.wait_ge(o_full, o0 + 2 * u + 2)
                            if u == 0:
                                at_least(dve, staged, NCH * b + n - 1)
                            dve.tensor_copy(kv[:, n % 2, 2 * u + 1, :], o_ps[:, (2 * u + 1) % 3, :]).then_inc(kv_ready_v, 1)
                        dve.wait_ge(o_full, o0 + 6)
                        stage_free(dve, b, n)
                        dve.tensor_copy(inside(1, n), dense(o_ps[:, 2, :])).then_inc(q_ready_v, 1)
                        for u in range(2):
                            dve.wait_ge(t_full, 4 * (NCH * b + n) + 2 * u + 2)
                            at_least(dve, vk_full, NCH * b + n)
                            dve.tensor_copy(vT[:, u, :, 0:P], t_ps[:, 1, :].rearrange("p (a c) -> p a c", a=4))\
                                .then_inc(v_turned, 1)
                        if nxt and n in (2, 4):
                            moments(b + 1, npar, ni, 0 if n == 2 else 1)
                        if nxt and n == 6:
                            scale(b + 1)
                    dve.wait_ge(vk_full, NCH * (b + 1))
                    for u in range(2):
                        dve.tensor_copy(K["vk"][:, bass.ds(b, 1), u, :].rearrange("p a c -> p (a c)"), vk_ps[:, u, 0:VW])\
                            .then_inc(vk_taken, 1)
            over_image_pairs(dve, body)


def over_head_pairs(eng, body):
    body(0, False)
    with eng.Fori(1, AH // 2 - 1) as i:
        body(i, False)
    body(AH // 2 - 1, True)


def convolved_heads(nc, K, w_dw, w_pw, taps_dram, qkv_dram, att_dram):
    with ExitStack() as ctx:
        def sb(name, shape, dt=F32):
            return ctx.enter_context(nc.sbuf_tensor(name, shape, dt))

        def psum(name, shape):
            return ctx.enter_context(nc.psum_tensor(name, shape, F32))

        def sem(name):
            return ctx.enter_context(nc.semaphore(name))

        STEPS = B // 2
        TT = TAP * TAP
        dw = sb("dw", [P, QT, 25])
        flip = sb("flip", [P, QT, 25])
        shifted = sb("shifted", [P, QT, NPH, TT])
        taps = sb("taps", [P, QT * HT, TT])
        pw_raw = sb("pw_raw", [P, QT, D])
        pw_rep = sb("pw_rep", [P, QT, NPH, D])
        pw = sb("pw", [P, QT * HT, D])
        wprod = sb("wprod", [P, 3, TT, D])
        wh = [sb(f"wh{i}", [P, 3, TT * D], F32R) for i in range(2)]
        wl = [sb(f"wl{i}", [P, 3, TT * D], F32R) for i in range(2)]
        raw = [sb(f"raw{i}", [P, 3, 2 * PN]) for i in range(2)]
        dh = [sb(f"dh{i}", [P, 3, 2 * PN], F32R) for i in range(2)]
        dl = [sb(f"dl{i}", [P, 3, 2 * PN], F32R) for i in range(2)]
        qy = sb("qy", [P, 2, 512])
        ky = sb("ky", [P, 512])
        vy = sb("vy", [P, 512])
        kT = sb("ykT", [P, 4, P])
        vT = sb("yvT", [P, 4, VW])
        diag = sb("diag", [P, 2, VW])
        mask1 = sb("mask1", [P, VW])
        vkr = sb("vkr", [P, 2, D])
        vkb = sb("vkb", [P, 2, P])
        ksb = sb("ksb", [P, 2, P])
        den = sb("den", [P, 512])
        rec = sb("rec", [P, 512])
        att = sb("att", [P, 2, 512])

        c_ps = psum("c_ps", [P, 2, 512])
        kt_ps, vt_ps = psum("kt_ps", [P, 512]), psum("vt_ps", [P, 512])
        vk_ps, t1_ps = psum("yvk_ps", [P, 512]), psum("t1_ps", [P, 512])
        out_ps, den_ps = psum("out_ps", [P, 512]), psum("den_ps", [P, 512])

        dw_loaded, pw_loaded, taps_out, taps_loaded = sem("dw_loaded"), sem("pw_loaded"), sem("taps_out"), sem("taps_loaded")
        init, turned, pw_ready = sem("init"), sem("pw_turned"), sem("pw_ready")
        raw_loaded = [sem(f"raw_loaded{i}") for i in range(2)]
        hi_ready, lo_ready = sem("hi_ready"), sem("lo_ready")
        w_prod, w_hi, w_lo = sem("w_prod"), sem("w_hi"), sem("w_lo")
        c_full, q_out, k_out, v_out = sem("c_full"), sem("q_out"), sem("k_out"), sem("v_out")
        kt_full, vt_full = sem("kt_full"), sem("vt_full")
        k_taken, v_taken = sem("yk_taken"), sem("yv_taken")
        vk_full, diag_ready, t1_full, bd_ready = sem("yvk_full"), sem("diag_ready"), sem("t1_full"), sem("bd_ready")
        out_full, out_taken = sem("out_full"), sem("out_taken")
        stored = [sem(f"att_stored{i}") for i in range(2)]
        link = sem("y_chain")
        lo_div = sem("div_chain")

        qkv_v = qkv_dram.rearrange("(k h c) p b n -> k h p c (b n)", k=3, c=D)
        att_v = att_dram.rearrange("(h d) p b n -> h p d (b n)", d=D)

        block = ctx.enter_context(nc.Block())

        def steps_of(i):
            for hp in range(2):
                for j in range(STEPS):
                    yield hp, 2 * i + hp, j, 2 * STEPS * i + STEPS * hp + j

        @block.sync
        def _(sp):
            own = Own(sp, init)
            for t in range(QT):
                rows = w_dw.rearrange("(h k c) i y x -> k h c (i y x)", k=3, c=D)[t // 2, HT * (t % 2):HT * (t % 2) + HT, :, :]
                sp.dma_start(dw[:, t, :], rows).then_inc(dw_loaded, 16)
                rows = w_pw.rearrange("(h k o) c y x -> k h o (c y x)", k=3, o=D)[t // 2, HT * (t % 2):HT * (t % 2) + HT, :, :]
                sp.dma_start(pw_raw[:, t, :], rows).then_inc(pw_loaded, 16)
            sp.wait_ge(init, 3)
            sp.dma_start(taps_dram.rearrange("t q p n -> q t (p n)"), shifted[:, :, :, :].rearrange("q t p n -> q t (p n)"))\
                .then_inc(taps_out, 16)
            sp.wait_ge(taps_out, 16)
            for p in range(NPH):
                src = taps_dram.rearrange("t (h c) p n -> p c (t h) n", c=D)[p, :, :, :]
                sp.dma_start(taps[D * p:D * p + D, :, :], src).then_inc(taps_loaded, 16)

            def store(h, j, s):
                own.wait_ge(out_taken, s + 1)
                sp.dma_start(att_v[h, :, :, 2 * POS * j:2 * POS * j + 2 * POS], att[:, j % 2, :]).then_inc(stored[j % 2], 16)

            def body(i, last):
                for hp, h, j, s in steps_of(i):
                    if not isinstance(s, int) or s >= 2:
                        own.wait_ge(hi_ready, s - 1)
                        own.wait_ge(lo_ready, s - 1)
                    for k in range(3):
                        sp.dma_start(raw[j % 2][:, k, :], qkv_v[k, h, :, :, 2 * PN * j:2 * PN * j + 2 * PN])\
                            .then_inc(raw_loaded[j % 2], 16)
                    if not isinstance(s, int) or s >= STEPS:
                        store(h - 1, j, s - STEPS)
            over_head_pairs(sp, body)
            for j in range(STEPS):
                store(AH - 1, j, STEPS * (AH - 1) + j)
            for c in range(2):
                sp.wait_ge(stored[c], 16 * STEPS * AH // 2)

        @block.gpsimd
        def _(pool):
            pool.memset(shifted[:, :, :, :], 0.0).then_inc(init, 1)

            def weights_low(h, par):
                pool.wait_ge(w_hi, h + 1)
                at_least(pool, c_full, 3 * STEPS * (h - 1))
                pool.tensor_tensor(wl[par][:, :, :], wprod[:, :, :, :].rearrange("p k a o -> p k (a o)"),
                                   wh[par][:, :, :].bitcast(F32), ALU.subtract).then_inc(w_lo, 1)

            def split(s, j):
                pool.wait_ge(hi_ready, s + 1)
                pool.tensor_tensor(dl[j % 2][:, :, :], raw[j % 2][:, :, :], dh[j % 2][:, :, :].bitcast(F32), ALU.subtract)\
                    .then_inc(lo_ready, 1)

            weights_low(0, 0)
            split(0, 0)

            def body(i, last):
                for hp, h, j, s in steps_of(i):
                    end = last and hp == 1
                    if not (end and j == STEPS - 1):
                        split(s + 1, j + 1)
                    if j == 2 and not end:
                        weights_low(h + 1, 1 - hp)
            over_head_pairs(pool, body)

        @block.scalar
        def _(act):
            act.wait_ge(pw_loaded, 16 * QT)
            act.activation(pw_rep[:, :, :, :], pw_raw[:, :, :].unsqueeze(2).broadcast_to([P, QT, NPH, D]), ACT.Copy)\
                .then_inc(pw_ready, 1)
            act.wait_ge(turned, 1)
            act.activation(pw[:, 0:4 * HT, :].rearrange("p g o -> p (g o)"), c_ps[:, 0, :], ACT.Copy).then_inc(pw_ready, 1)
            act.activation(pw[:, 4 * HT:6 * HT, :].rearrange("p g o -> p (g o)"), c_ps[:, 1, 0:2 * P], ACT.Copy)\
                .then_inc(pw_ready, 1)

            def weights_high(h, par):
                act.wait_ge(w_prod, h + 1)
                at_least(act, c_full, 3 * STEPS * (h - 1))
                act.activation(wh[par][:, :, :], wprod[:, :, :, :].rearrange("p k a o -> p k (a o)"), ACT.Copy)\
                    .then_inc(w_hi, 1)

            def split(s, j, use):
                act.wait_ge(raw_loaded[j % 2], 48 * use)
                at_least(act, c_full, 3 * (s - 1))
                act.activation(dh[j % 2][:, :, :], raw[j % 2][:, :, :], ACT.Copy).then_inc(hi_ready, 1)

            weights_high(0, 0)
            split(0, 0, 1)

            def body(i, last):
                for hp, h, j, s in steps_of(i):
                    end = last and hp == 1
                    if not (end and j == STEPS - 1):
                        split(s + 1, j + 1, 4 * i + 2 * hp + (j + 1) // 2 + 1)
                    act.wait_ge(c_full, 3 * s + 1)
                    act.activation(qy[:, j % 2, :], c_ps[:, j % 2, :], ACT.Relu).then_inc(q_out, 1)
                    if j == 2 and not end:
                        weights_high(h + 1, 1 - hp)
                    act.wait_ge(c_full, 3 * s + 2)
                    at_least(act, kt_full, s)
                    act.activation(ky[:, :], c_ps[:, (j + 1) % 2, :], ACT.Relu).then_inc(k_out, 1)
                    act.wait_ge(kt_full, s + 1)
                    at_least(act, vk_full, s)
                    act.activation(kT[:, :, :].rearrange("p a c -> p (a c)"), kt_ps[:, :], ACT.Copy).then_inc(k_taken, 1)
            over_head_pairs(act, body)

        @block.tensor
        def _(pe):
            pe.wait_ge(pw_ready, 1)
            for t in range(QT):
                dst = c_ps[:, t // 4, P * (t % 4):P * (t % 4) + P]
                last = pe.transpose(dst, pw_rep[:, t, :, :].rearrange("p a c -> p (a c)"), K["ident"][:, :])
            last.then_inc(turned, 1)
            pe.wait_ge(pw_ready, 3)
            pe.wait_ge(init, 5)

            def convolve(s, j, par, kind):
                if kind == 0:
                    pe.wait_ge(lo_ready, s + 1)
                if kind == 0:
                    at_least(pe, k_out, s)
                elif kind == 1:
                    at_least(pe, v_out, s)
                else:
                    pe.wait_ge(q_out, s + 1)
                k = 0
                for dy in range(2):
                    for dx in range(2):
                        o = (1 - dx) * 4 * TAP * D + (1 - dy) * P
                        for w, d in ((wh, dh), (wl, dh), (wh, dl)):
                            src = d[j % 2][:, kind, :].rearrange("p (b y x) -> p b y x", b=2, x=PBK)[:, :, dy:dy + NB, dx:dx + NB]
                            last = pe.matmul(c_ps[:, (j + kind) % 2, :], w[par][:, kind, o:o + P], src,
                                             start=(k == 0), stop=(k == 11))
                            k += 1
                last.then_inc(c_full, 1)

            def turn(s, src, ps, ready, taken, full):
                pe.wait_ge(ready, s + 1)
                at_least(pe, taken, s)
                for a in range(4):
                    last = pe.transpose(ps[:, P * a:P * a + P], src[:, P * a:P * a + P], K["ident"][:, :])
                last.then_inc(full, 1)

            def sum_vk(s):
                pe.wait_ge(k_taken, s + 1)
                pe.wait_ge(v_taken, s + 1)
                at_least(pe, diag_ready, s)
                for b in range(2):
                    for half in range(2):
                        a = 2 * b + half
                        last = pe.matmul(vk_ps[:, VW * b:VW * b + VW], kT[:, a, :], vT[:, a, :],
                                         start=(half == 0), stop=(half == 1))
                last.then_inc(vk_full, 1)

            def sum_phases(s):
                pe.wait_ge(diag_ready, s + 1)
                at_least(pe, bd_ready, s)
                pe.matmul(t1_ps[:, 0:2 * VW], K["same_ch"][:, :], diag[:, :, :].rearrange("p b n -> p (b n)"),
                          start=True, stop=True).then_inc(t1_full, 1)

            def attend(s, j):
                pe.wait_ge(bd_ready, s + 1)
                at_least(pe, out_taken, s)
                for ps, w in ((out_ps, vkb), (den_ps, ksb)):
                    for b in range(2):
                        last = pe.matmul(ps[:, POS * b:POS * b + POS], w[:, b, :], qy[:, j % 2, POS * b:POS * b + POS],
                                         start=True, stop=True)
                last.then_inc(out_full, 1)

            def body(i, last):
                for hp, h, j, s in steps_of(i):
                    pj = (j + 1) % 2
                    prev = not isinstance(s, int) or s >= 1
                    if j == 0:
                        pe.wait_ge(w_lo, h + 1)
                    convolve(s, j, hp, 0)
                    if prev:
                        sum_vk(s - 1)
                    convolve(s, j, hp, 1)
                    if prev:
                        sum_phases(s - 1)
                    convolve(s, j, hp, 2)
                    turn(s, ky, kt_ps, k_out, k_taken, kt_full)
                    if prev:
                        attend(s - 1, pj)
                    turn(s, vy, vt_ps, v_out, v_taken, vt_full)
            over_head_pairs(pe, body)
            s = AH * STEPS - 1
            sum_vk(s)
            sum_phases(s)
            attend(s, 1)

        @block.vector
        def _(dve):
            dve.wait_ge(dw_loaded, 16 * QT)
            dve.wait_ge(init, 1)
            for k in range(25):
                last = dve.tensor_copy(flip[:, :, k:k + 1], dw[:, :, 24 - k:25 - k])
            last.then_inc(init, 1)
            dve.wait_ge(init, 2)
            fl = flip[:, :, :].rearrange("p t (y x) -> p t y x", x=5)
            for p in range(NPH):
                py, px = p // 4, p % 4
                grid = shifted[:, :, p, :].rearrange("p t (d u q) -> p d t u q", d=2, q=4)
                dve.tensor_copy(grid[:, 0, :, py:py + 5, px:4], fl[:, :, :, 0:4 - px])
                last = dve.tensor_copy(grid[:, 1, :, py:py + 5, 0:px + 1], fl[:, :, :, 4 - px:5])
            last.then_inc(init, 1)
            dve.tensor_copy(mask1[:, 0:P], K["gmask"][:, :]).then_inc(init, 1)
            dve.memset(mask1[:, P:VW], 1.0)
            dve.memset(vT[:, :, P:VW], 1.0).then_inc(init, 1)
            dve.wait_ge(pw_ready, 3)
            dve.wait_ge(taps_loaded, 16 * NPH)
            dve.wait_ge(init, 5)

            chain = Chain(dve, link)

            def weights(h):
                at_least(dve, w_lo, h)
                at_least(dve, w_hi, h)
                tv = taps[:, :, :].rearrange("p (k h) n -> p k h n", k=3)[:, :, bass.ds(h, 1), :]
                pv = pw[:, :, :].rearrange("p (k h) o -> p k h o", k=3)[:, :, bass.ds(h, 1), :]
                tv = tv.rearrange("p k a n -> p k (a n)").unsqueeze(3).broadcast_to([P, 3, TT, D])
                pv = pv.broadcast_to([P, 3, TT, D])
                dve.tensor_tensor(wprod[:, :, :, :], tv, pv, ALU.mult).then_inc(w_prod, 1)

            def keep_diagonal(s):
                dve.wait_ge(vk_full, s + 1)
                dve.tensor_tensor(diag[:, :, :], vk_ps[:, 0:2 * VW].rearrange("p (b n) -> p b n", b=2),
                                  mask1[:, :].unsqueeze(1).broadcast_to([P, 2, VW]), ALU.mult).then_inc(diag_ready, 1)

            def spread(s):
                dve.wait_ge(t1_full, s + 1)
                t1 = t1_ps[:, 0:2 * VW].rearrange("p (b n) -> p b n", b=2)
                chain.base, chain.n = s, 0
                chain(dve.tensor_reduce(vkr[:, :, :], t1[:, :, 0:P].rearrange("p b (a d) -> p b d a", d=D), AX.X, ALU.add))
                for b in range(2):
                    dve.tensor_tensor(vkb[:, b, :].rearrange("p (a d) -> p a d", d=D),
                                      K["gmask"][:, :].rearrange("p (a d) -> p a d", d=D),
                                      vkr[:, b, :].unsqueeze(1).broadcast_to([P, NPH, D]), ALU.mult)
                    last = dve.tensor_scalar(ksb[:, b, :], K["gmask"][:, :], t1[:, b, P:VW], None, ALU.mult)
                last.then_inc(bd_ready, 1)

            link2 = Chain(dve, lo_div)

            def divide(s, j, stored_use):
                dve.wait_ge(out_full, s + 1)
                link2.base, link2.n = 2 * s, 0
                link2(dve.tensor_scalar(den[:, :], den_ps[:, :], ATT_EPS, None, ALU.add))
                link2(dve.reciprocal(rec[:, :], den[:, :]))
                at_least(dve, stored[j % 2], 16 * stored_use)
                dve.tensor_tensor(att[:, j % 2, :], out_ps[:, :], rec[:, :], ALU.mult).then_inc(out_taken, 1)

            weights(0)

            def body(i, last):
                for hp, h, j, s in steps_of(i):
                    end = last and hp == 1
                    prev = not isinstance(s, int) or s >= 1
                    if prev:
                        keep_diagonal(s - 1)
                        spread(s - 1)
                    dve.wait_ge(c_full, 3 * s + 3)
                    at_least(dve, vt_full, s)
                    dve.tensor_copy(vy[:, :], c_ps[:, j % 2, :]).then_inc(v_out, 1)
                    dve.wait_ge(vt_full, s + 1)
                    at_least(dve, vk_full, s)
                    dve.tensor_copy(vT[:, :, 0:P], vt_ps[:, :].rearrange("p (a c) -> p a c", a=4)).then_inc(v_taken, 1)
                    if j == 1 and not end:
                        weights(h + 1)
                    if prev:
                        divide(s - 1, (j - 1) % 2, 4 * i + 2 * hp + (j - 1) // 2)
            over_head_pairs(dve, body)
            s = AH * STEPS - 1
            keep_diagonal(s)
            spread(s)
            divide(s, 1, AH * STEPS // 2 - 1)


def output(nc, K, w_proj, gamma, beta, mean, var, x1_dram, qkv_dram, att_dram, out_dram):
    with ExitStack() as ctx:
        def sb(name, shape, dt=F32):
            return ctx.enter_context(nc.sbuf_tensor(name, shape, dt))

        def psum(name, shape):
            return ctx.enter_context(nc.psum_tensor(name, shape, F32))

        def sem(name):
            return ctx.enter_context(nc.semaphore(name))

        KT = 4
        CH = 4
        projT = sb("projT", [P, KT, C])
        bn = {n: sb(f"bn_{n}", [P, CT]) for n in ("gamma", "beta", "mean", "var", "ve", "std", "r0", "t1", "t2", "t3",
                                                  "r", "inv", "mi", "shift")}
        pick = sb("pick", [P, 2, 4, 32])
        spread = sb("spread", [P, 2, P])
        fold_all = sb("fold_all", [P, B, 2, C])
        ks_all = sb("ks_all", [P, B, 2, 32])
        fold = [sb(f"fold{i}", [P, 2, C]) for i in range(2)]
        vkm, vkT = fold[0][:, :, 0:P], fold[1][:, :, 0:P]
        ks = [sb(f"ks{i}", [P, 2, 32]) for i in range(2)]
        x1 = [sb(f"ox{i}", [P, CT, H * W]) for i in range(2)]
        q = [sb(f"oq{i}", [P, 2, 8, PN]) for i in range(2)]
        att = [sb(f"oatt{i}", [P, 2, 8, POS]) for i in range(2)]
        pr_raw = att[1][:, 0, 0:4, :].rearrange("p (t a) n -> p t (a n)", t=CT)
        prs = att[1][:, 1, 0:4, :].rearrange("p (t a) n -> p t (a n)", t=CT)
        qr = [sb(f"qr{i}", [P, 2, CH, 512]) for i in range(2)]
        rec = [sb(f"orec{i}", [P, 512]) for i in range(2)]

        den_ps = psum("oden_ps", [P, 512])
        bc_ps = psum("bc_ps", [P, 2, 512])
        z_ps = psum("z_ps", [P, 2, 2, 512])

        w_loaded, link, turned, ready = sem("ow_loaded"), sem("o_chain"), sem("o_turned"), sem("o_ready")
        std_in, std_out = sem("bn_var"), sem("bn_std")
        x_loaded = [sem(f"ox_loaded{i}") for i in range(2)]
        in_loaded = [sem(f"oin_loaded{i}") for i in range(2)]
        x_stored = [sem(f"ox_stored{i}") for i in range(2)]
        q_relu, a_ready = sem("q_relu"), sem("a_ready")
        den_full, den_taken, rec_ready = sem("den_full"), sem("den_taken"), sem("rec_ready")
        bc_full, q_scaled = sem("bc_full"), sem("q_scaled")
        z_full, z_taken = sem("z_full"), sem("z_taken")
        link_vk, x_shifted = sem("vk_masked"), sem("x_shifted")

        block = ctx.enter_context(nc.Block())

        @block.sync
        def _(sp):
            sp.dma_start(pr_raw, w_proj.rearrange("(t p) k -> p t k", p=P)).then_inc(w_loaded, 16)
            with nc.allow_non_contiguous_dma(reason="256 values each"):
                for n, v in (("gamma", gamma), ("beta", beta), ("mean", mean), ("var", var)):
                    sp.dma_start(bn[n][:, :], v.rearrange("(t p) -> p t", p=P)).then_inc(w_loaded, 16)

            def body(i, last):
                for par in range(2):
                    b = 2 * i + par
                    sp.wait_ge(z_taken, 4 * CH * (b + 1))
                    sp.dma_start(out_dram[b, :, :].rearrange("(t p) n -> p t n", p=P), x1[par][:, :, :])\
                        .then_inc(x_stored[par], 16)
            over_image_pairs(sp, body)
            for par in range(2):
                sp.wait_ge(x_stored[par], 16 * (B // 2))

        @block.gpsimd
        def _(pool):
            def body(i, last):
                for par in range(2):
                    b = 2 * i + par
                    at_least(pool, x_stored[par], 16 * i)
                    pool.dma_start(x1[par][:, :, :], x1_dram[b, :, :].rearrange("(t p) n -> p t n", p=P))\
                        .then_inc(x_loaded[par], 16)
                    for hb in range(2):
                        g = 2 * b + hb
                        if isinstance(g, int) and g == 1:
                            pool.wait_ge(ready, 2 + KT)
                        if not isinstance(g, int) or g >= 2:
                            pool.wait_ge(z_full, CH * (g - 1))
                        for t in range(2):
                            pool.dma_start(q[hb][:, t, :, :], qkv_dram[P * t:P * t + P, 8 - 8 * hb:16 - 8 * hb, b, :])\
                                .then_inc(in_loaded[hb], 16)
                            pool.dma_start(att[hb][:, t, :, :], att_dram[P * t:P * t + P, 8 * hb:8 * hb + 8, b, :])\
                                .then_inc(in_loaded[hb], 16)
            over_image_pairs(pool, body)

        @block.scalar
        def _(act):
            act.wait_ge(std_in, 1)
            act.activation(bn["std"][:, :], bn["ve"][:, :], ACT.Sqrt).then_inc(std_out, 1)
            for kt in range(KT):
                act.wait_ge(turned, kt + 1)
                act.activation(projT[:, kt, :], z_ps[:, 0, kt % 2, 0:C], ACT.Copy).then_inc(ready, 1)
            act.wait_ge(turned, KT + 1)
            act.activation(spread[:, :, :].rearrange("p t c -> p (t c)"), z_ps[:, 1, 0, 0:2 * P], ACT.Copy).then_inc(ready, 1)
            for n in range(2 * B):
                b, t = n // 2, n % 2
                act.wait_ge(turned, KT + 2 + 2 * n)
                act.activation(vkT[:, t, :], bc_ps[:, 0, 0:P], ACT.Copy).then_inc(ready, 1)
                act.wait_ge(turned, KT + 3 + 2 * n)
                act.activation(fold_all[:, b, t, :], bc_ps[:, 1, 0:C], ACT.Copy).then_inc(ready, 1)

            def body(i, last):
                for par in range(2):
                    b = 2 * i + par
                    for hb in range(2):
                        g = 2 * b + hb
                        act.wait_ge(in_loaded[hb], 64 * (2 * i + par + 1))
                        at_least(act, z_full, CH * (g - 1))
                        for t in range(2):
                            for c in range(CH):
                                p0 = 4 * (c // 2) + 2 * ((c + 1) % 2)
                                ox = c % 2
                                src = q[hb][:, t, p0:p0 + 2, :].rearrange("p a (y x) -> p a y x", x=PBK)[:, :, hb:hb + NB, ox:ox + NB]
                                last_i = act.activation(qr[hb][:, t, c, :].rearrange("p (a y x) -> p a y x", a=2, x=NB), src, ACT.Relu)
                        last_i.then_inc(q_relu, 1)
                        if hb == 0:
                            act.activation(fold[par][:, :, :], fold_all[:, bass.ds(b, 1), :, :].rearrange("p a t c -> p (a t) c"), ACT.Copy)
                            act.activation(ks[par][:, :, :], ks_all[:, bass.ds(b, 1), :, :].rearrange("p a t c -> p (a t) c"), ACT.Copy)\
                                .then_inc(a_ready, 1)
                            act.wait_ge(x_loaded[par], 16 * (i + 1))
                            for o in range(CT):
                                last_i = act.activation(x1[par][:, o, :], x1[par][:, o, :], ACT.Identity,
                                                        bias=bn["shift"][:, o:o + 1])
                            last_i.then_inc(x_shifted, 1)
            over_image_pairs(act, body)

        @block.tensor
        def _(pe):
            for kt in range(KT):
                if kt == 0:
                    pe.wait_ge(ready, 2)
                at_least(pe, ready, 2 + kt - 1)
                for o in range(CT):
                    last = pe.transpose(z_ps[:, 0, kt % 2, P * o:P * o + P], prs[:, o, P * kt:P * kt + P], K["ident"][:, :])
                last.then_inc(turned, 1)
            for t in range(2):
                last = pe.transpose(z_ps[:, 1, 0, P * t:P * t + P], pick[:, t, :, :].rearrange("p a c -> p (a c)"), K["ident"][:, :])
            last.then_inc(turned, 1)
            for n in range(2 * B):
                b, t = n // 2, n % 2
                pe.wait_ge(link_vk, n + 1)
                pe.wait_ge(ready, 2 + KT + 1 + 2 * n)
                pe.transpose(bc_ps[:, 0, 0:P], vkm[:, n % 2, :], K["ident"][:, :]).then_inc(turned, 1)
                pe.wait_ge(ready, 2 + KT + 2 + 2 * n)
                pe.matmul(bc_ps[:, 1, 0:C], vkT[:, t, :], projT[:, t, :], start=True, stop=True).then_inc(turned, 1)
            pe.wait_ge(ready, 2 + KT + 1 + 4 * B)

            def denominators(g, hb, par, b):
                pe.wait_ge(q_relu, g + 1)
                if hb == 0:
                    pe.wait_ge(a_ready, b + 1)
                at_least(pe, den_taken, g)
                for c in range(CH):
                    for t in range(2):
                        last = pe.matmul(den_ps[32 * c:32 * c + 32, :], ks[par][:, t, :], qr[hb][:, t, c, :],
                                         start=(t == 0), stop=(t == 1))
                last.then_inc(den_full, 1)

            def to_channels(g, hb, c):
                if c == 0:
                    pe.wait_ge(rec_ready, g + 1)
                at_least(pe, q_scaled, CH * g + c)
                for t in range(2):
                    last = pe.matmul(bc_ps[:, t, :], spread[32 * c:32 * c + 32, t, :], rec[hb][32 * c:32 * c + 32, :],
                                     start=True, stop=True)
                last.then_inc(bc_full, 1)

            def project(g, hb, par, c, direct):
                if not direct:
                    at_least(pe, z_taken, 2 * (CH * g + c - 1))
                else:
                    pe.wait_ge(q_scaled, CH * g + c + 1)
                for o in range(CT):
                    for t in range(2):
                        if direct:
                            last = pe.matmul(z_ps[:, c % 2, o, :], fold[par][:, t, P * o:P * o + P], qr[hb][:, t, c, :],
                                             start=False, stop=(t == 1))
                        else:
                            last = pe.matmul(z_ps[:, c % 2, o, :], projT[:, 2 + t, P * o:P * o + P],
                                             att[hb][:, t, 2 * c:2 * c + 2, :].rearrange("p a n -> p (a n)"),
                                             start=(t == 0), stop=False)
                if direct:
                    last.then_inc(z_full, 1)

            pe.wait_ge(in_loaded[0], 64)
            denominators(0, 0, 0, 0)

            def body(i, last_body):
                for par in range(2):
                    b = 2 * i + par
                    for hb in range(2):
                        g = 2 * b + hb
                        to_channels(g, hb, 0)
                        for c in range(CH):
                            if c == 0:
                                pe.wait_ge(in_loaded[hb], 64 * (2 * i + par + 1))
                            project(g, hb, par, c, False)
                            if c + 1 < CH:
                                to_channels(g, hb, c + 1)
                            project(g, hb, par, c, True)
                            if c == 1 and not (last_body and par == 1 and hb == 1):
                                npar = par if hb == 0 else 1 - par
                                denominators(g + 1, 1 - hb, npar, b + hb)
            over_image_pairs(pe, body)

        @block.vector
        def _(dve):
            chain = Chain(dve, link)
            dve.wait_ge(w_loaded, 16 * 5)
            chain(dve.tensor_scalar(bn["ve"][:, :], bn["var"][:, :], BN_EPS, None, ALU.add))
            dve.tensor_copy(bn["t1"][:, :], bn["ve"][:, :]).then_inc(std_in, 1)
            dve.wait_ge(std_out, 1)
            chain(dve.reciprocal(bn["r0"][:, :], bn["std"][:, :]))
            chain(dve.tensor_tensor(bn["t2"][:, :], bn["r0"][:, :], bn["r0"][:, :], ALU.mult))
            chain(dve.tensor_tensor(bn["t3"][:, :], bn["t2"][:, :], bn["ve"][:, :], ALU.mult))
            chain(dve.tensor_scalar(bn["mi"][:, :], bn["t3"][:, :], -0.5, 1.5, ALU.mult, ALU.add))
            chain(dve.tensor_tensor(bn["r"][:, :], bn["r0"][:, :], bn["mi"][:, :], ALU.mult))
            chain(dve.tensor_tensor(bn["inv"][:, :], bn["r"][:, :], bn["gamma"][:, :], ALU.mult))
            chain(dve.tensor_tensor(bn["std"][:, :], bn["inv"][:, :], bn["mean"][:, :], ALU.mult))
            chain(dve.tensor_tensor(bn["shift"][:, :], bn["beta"][:, :], bn["std"][:, :], ALU.subtract))
            for o in range(CT):
                last = dve.tensor_scalar(prs[:, o, :], pr_raw[:, o, :], bn["inv"][:, o:o + 1], None, ALU.mult)
            last.then_inc(ready, 1)
            chain(dve.memset(pick[:, :, :, :], 0.0))
            heads = K["gmask"][:, :].rearrange("p (h c) -> p h c", c=D)[:, :, 0]
            for t in range(2):
                for r in range(4):
                    last = dve.tensor_copy(pick[:, t, r, HT * t:HT * t + HT], heads)
            last.then_inc(ready, 1)
            dve.wait_ge(ready, 2)
            for n in range(2 * B):
                b, t = n // 2, n % 2
                at_least(dve, turned, KT + 1 + 2 * (n - 1))
                dve.tensor_scalar(ks_all[:, b, t, :], pick[:, t, 0, :], K["vk"][:, b, t, P:VW], None, ALU.mult)
                dve.tensor_tensor(vkm[:, n % 2, :], K["vk"][:, b, t, 0:P], K["gmask"][:, :], ALU.mult).then_inc(link_vk, 1)

            def reciprocals(g, hb):
                dve.wait_ge(den_full, g + 1)
                at_least(dve, bc_full, CH * (g - 1))
                dve.tensor_scalar(rec[hb][:, :], den_ps[:, :], ATT_EPS, None, ALU.add).then_inc(den_taken, 1)
                dve.wait_ge(den_taken, g + 1)
                dve.reciprocal(rec[hb][:, :], rec[hb][:, :]).then_inc(rec_ready, 1)
                dve.wait_ge(rec_ready, g + 1)

            def add(g, hb, par, c):
                dve.wait_ge(z_full, CH * g + c + 1)
                py, px = 2 * hb + c // 2, 2 * (c % 2)
                for o in range(CT):
                    img = x1[par][:, o, :].rearrange("p (y py x px) -> p py px y x", py=4, x=NB, px=4)[:, py, px:px + 2, :, :]
                    dve.tensor_tensor(img, z_ps[:, c % 2, o, :].rearrange("p (a y x) -> p a y x", a=2, x=NB), img,
                                      ALU.add).then_inc(z_taken, 1)

            reciprocals(0, 0)

            def body(i, last_body):
                for par in range(2):
                    b = 2 * i + par
                    for hb in range(2):
                        g = 2 * b + hb
                        for c in range(CH):
                            dve.wait_ge(bc_full, CH * g + c + 1)
                            for t in range(2):
                                last = dve.tensor_tensor(qr[hb][:, t, c, :], qr[hb][:, t, c, :], bc_ps[:, t, :], ALU.mult)
                            last.then_inc(q_scaled, 1)
                            if c == 0 and hb == 0:
                                dve.wait_ge(x_shifted, b + 1)
                            if c >= 1:
                                add(g, hb, par, c - 1)
                            if c == 2 and not (last_body and par == 1 and hb == 1):
                                reciprocals(g + 1, 1 - hb)
                        add(g, hb, par, CH - 1)
            over_image_pairs(dve, body)


def build(nc, a, out, scratch):
    with ExitStack() as ctx:
        K = {}
        make_constants(nc, ctx, K)
        window_mixing(nc, K, a["x"], a["L0_conv_w"], a["L0_conv_b"], scratch["x1"])
        projections(nc, K, a["L1_conv_w_qkv"], scratch["x1"], scratch["qkv"])
        convolved_heads(nc, K, a["L1_conv_w_dw"], a["L1_conv_w_pw"], scratch["taps"], scratch["qkv"], scratch["att"])
        output(nc, K, a["L1_conv_w_proj"], a["L1_conv_bn_gamma"], a["L1_conv_bn_beta"], a["L1_conv_bn_mean"],
               a["L1_conv_bn_var"], scratch["x1"], scratch["qkv"], scratch["att"], out.rearrange("b c h w -> b c (h w)"))



_INS = ["x", "L0_conv_w", "L0_conv_b", "L1_conv_w_qkv", "L1_conv_w_dw", "L1_conv_w_pw", "L1_conv_w_proj",
        "L1_conv_bn_gamma", "L1_conv_bn_beta", "L1_conv_bn_mean", "L1_conv_bn_var"]


def kernel(**inputs):
    import numpy as np
    import concourse.bacc as bacc
    from concourse.bass_utils import run_bass_kernel_spmd

    nc = bacc.Bacc("TRN2", target_bir_lowering=False, num_devices=1)
    arrays, aps = {}, {}
    for name in _INS:
        arr = np.ascontiguousarray(inputs[name])
        arrays[f"in_{name}"] = arr
        aps[name] = nc.dram_tensor(f"in_{name}", arr.shape, mybir.dt.from_np(arr.dtype), kind="ExternalInput").ap()
    out = nc.dram_tensor("out_0", (B, C, H, W), F32, kind="ExternalOutput").ap()
    scratch = {
        "x1": nc.dram_tensor("x1_scratch", (B, C, H * W), F32, kind="Internal").ap(),
        "qkv": nc.dram_tensor("qkv_scratch", (3 * C, NPH, B, PN), F32, kind="Internal").ap(),
        "att": nc.dram_tensor("att_scratch", (C, NPH, B, POS), F32, kind="Internal").ap(),
        "taps": nc.dram_tensor("tap_scratch", (QT, P, NPH, TAP * TAP), F32, kind="Internal").ap(),
    }
    build(nc, aps, out, scratch)
    r = run_bass_kernel_spmd(nc, [arrays], core_ids=[0])
    return r.results[0]["out_0"]
```

```python
from contextlib import ExitStack

import concourse.bass as bass
from concourse import mybir

F32 = mybir.dt.float32
F32R = mybir.dt.float32r
ALU = mybir.AluOpType
ACT = mybir.ActivationFunctionType
AX = mybir.AxisListType

P = 128
B, C, H, W = 8, 256, 64, 64
CT = C // P
GN_CH = 8
GN_EPS = 1e-5
WS, SHIFT, MIX_HEADS = 8, 4, 16
MIX_CH = C // MIX_HEADS
WIN_ROWS = (H + WS) // WS
PAIRS = (W + WS + 15) // 16
PAD_W = PAIRS * 16
WR = 3
GROUPS = WIN_ROWS // WR
GP = WR * PAIRS
FILLS = (GP + 1) // 2
D = 8
AH = 32
HT = P // D
QT = 6
NB = 16
PBK = NB + 1
PN = PBK * PBK
NPH = 16
POS = NB * NB
TAP = 8
BN_EPS = 1e-5
ATT_EPS = 1e-15
VW = P + 1


def at_least(eng, sem, value):
    if isinstance(value, int) and value <= 0:
        return
    eng.wait_ge(sem, value)


class Own:

    def __init__(self, eng, start):
        self.eng, self.start = eng, start

    def wait_ge(self, sem, value):
        if not isinstance(value, int):
            self.eng.wait_ge(self.start, 1)
        self.eng.wait_ge(sem, value)


def over_image_pairs(eng, body):
    body(0, False)
    with eng.Fori(1, B // 2 - 1) as i:
        body(i, False)
    body(B // 2 - 1, True)


class Chain:

    def __init__(self, eng, sem):
        self.eng, self.sem, self.base, self.n = eng, sem, 0, 0

    def __call__(self, ins):
        self.n += 1
        ins.then_inc(self.sem, 1)
        self.eng.wait_ge(self.sem, self.base + self.n)


def norm_moments(dve, bst, x, pieces):
    for ct, k in pieces:
        last = dve.bn_stats(bst[:, ct, k, :], x[:, ct, 512 * k:512 * k + 512])
    return last


def norm_scale(dve, chain, b, T, mv, bst, stat_ps, sem):
    def moments():
        for ct in range(CT):
            last = dve.bn_aggr(mv[:, ct, :], bst[:, ct, :, :].rearrange("p a s -> p (a s)"))
        last.then_inc(sem["moments"], 1)

    def centre():
        chain.base, chain.n = NORM_CHAIN * b, 0
        dve.wait_ge(sem["group_sum"], 2 * b + 1)
        chain(dve.tensor_tensor(T["dm"][:, :], mv[:, :, 0], stat_ps[:, 0:2], ALU.subtract))
        chain(dve.tensor_tensor(T["sq"][:, :], T["dm"][:, :], T["dm"][:, :], ALU.mult))
        dve.tensor_tensor(T["vc"][:, :], T["sq"][:, :], mv[:, :, 1], ALU.add).then_inc(sem["moments"], 1)

    def variance():
        dve.wait_ge(sem["group_sum"], 2 * b + 2)
        dve.tensor_scalar(T["ve"][:, :], stat_ps[:, 2:4], GN_EPS, None, ALU.add).then_inc(sem["var"], 1)

    def scale():
        dve.wait_ge(sem["std"], b + 1)
        chain(dve.reciprocal(T["r0"][:, :], T["std"][:, :]))
        chain(dve.tensor_tensor(T["t1"][:, :], T["r0"][:, :], T["r0"][:, :], ALU.mult))
        chain(dve.tensor_tensor(T["t2"][:, :], T["t1"][:, :], T["ve"][:, :], ALU.mult))
        chain(dve.tensor_scalar(T["t3"][:, :], T["t2"][:, :], -0.5, 1.5, ALU.mult, ALU.add))
        at_least(dve, sem["scaled"], b)
        chain(dve.tensor_tensor(T["sc"][:, :], T["r0"][:, :], T["t3"][:, :], ALU.mult))
        dve.scalar_tensor_tensor(T["nb"][:, :], stat_ps[:, 0:2], -1.0, T["sc"][:, :], ALU.mult,
                                 ALU.mult).then_inc(sem["scale"], 1)
    return moments, centre, variance, scale


NORM_CHAIN = 7
CONST_STEPS = 7 + NPH


def norm_group_sums(pe, b, T, mv, stat_ps, gavg, sem):
    def means():
        pe.wait_ge(sem["moments"], 2 * b + 1)
        pe.matmul(stat_ps[:, 0:2], gavg[:, :], mv[:, :, 0], start=True, stop=True).then_inc(sem["group_sum"], 1)

    def variances():
        pe.wait_ge(sem["moments"], 2 * b + 2)
        pe.matmul(stat_ps[:, 2:4], gavg[:, :], T["vc"][:, :], start=True, stop=True).then_inc(sem["group_sum"], 1)
    return means, variances


def norm_std(act, b, T, sem):
    act.wait_ge(sem["var"], b + 1)
    act.activation(T["std"][:, :], T["ve"][:, :], ACT.Sqrt).then_inc(sem["std"], 1)


def norm_tiles(sb, sem_of, tag):
    T = {n: sb(f"{tag}_{n}", [P, CT], F32) for n in
         ("dm", "sq", "vc", "ve", "std", "r0", "t1", "t2", "t3", "sc", "nb", "used")}
    sem = {n: sem_of(f"{tag}_{n}") for n in ("moments", "group_sum", "var", "std", "scale", "scaled", "chain")}
    return T, sem


def make_constants(nc, ctx, two_phases, K):
    def sb(name, shape):
        return ctx.enter_context(nc.sbuf_tensor(name, shape, F32))
    K["ident"] = sb("ident", [P, P])
    K["gmask"] = sb("gmask", [P, P])
    K["gavg"] = sb("gavg", [P, P])
    K["same_ch"] = sb("same_ch", [P, P])
    K["vk"] = sb("vk_direct", [P, B, 2, VW])
    K["images"] = [two_phases.enter_context(nc.sbuf_tensor(f"image{i}", [P, CT, H * W], F32)) for i in range(2)]
    K["x_stored"] = [[ctx.enter_context(nc.semaphore(f"x_stored{i}_{g}")) for g in range(GROUPS)] for i in range(2)]
    K["w_qkv"] = two_phases.enter_context(nc.sbuf_tensor("wq_raw", [P, QT, C], F32))
    K["wq_loaded"] = ctx.enter_context(nc.semaphore("wq_loaded"))
    done = K["const_done"] = ctx.enter_context(nc.semaphore("const_done"))

    def fill(pool):
        n = 0

        def step(ins):
            nonlocal n
            n += 1
            ins.then_inc(done, 1)
            pool.wait_ge(done, n)
        step(pool.memset(K["ident"][:, :], 0.0))
        step(pool.affine_select(out=K["ident"][:, :], in_=K["ident"][:, :], compare_op=ALU.not_equal,
                                fill=1.0, base=0, pattern=[[-1, P]], channel_multiplier=1))
        step(pool.memset(K["gmask"][:, :], 1.0))
        g = K["gmask"][:, :].rearrange("p (a c) -> p a c", c=GN_CH)
        step(pool.affine_select(out=g, in_=g, compare_op=ALU.is_ge, fill=0.0, base=0,
                                pattern=[[-GN_CH, P // GN_CH], [0, GN_CH]], channel_multiplier=1))
        step(pool.affine_select(out=g, in_=g, compare_op=ALU.is_ge, fill=0.0, base=GN_CH - 1,
                                pattern=[[GN_CH, P // GN_CH], [0, GN_CH]], channel_multiplier=-1))
        step(pool.tensor_scalar(K["gavg"][:, :], K["gmask"][:, :], 1.0 / GN_CH, None, ALU.mult))
        step(pool.memset(K["same_ch"][:, :], 0.0))
        s = K["same_ch"][:, :].rearrange("p (a c) -> p a c", c=D)
        for m in range(NPH):
            step(pool.affine_select(out=s, in_=s, compare_op=ALU.not_equal, fill=1.0, base=-D * m,
                                    pattern=[[0, NPH], [-1, D]], channel_multiplier=1))
    K["fill"] = fill


def window_mixing(nc, K, x_in, w_mix, b_mix, w_qkv, x1_dram):
    with ExitStack() as ctx:
        def sb(name, shape, dt=F32):
            return ctx.enter_context(nc.sbuf_tensor(name, shape, dt))

        def psum(name, shape):
            return ctx.enter_context(nc.psum_tensor(name, shape, F32))

        def sem(name):
            return ctx.enter_context(nc.semaphore(name))

        x = K["images"]
        xpad = sb("xpad", [P, CT, PAIRS, H + WS, 16])
        xT = sb("xT", [P, 2, GP, C])
        yT = sb("yT", [P, 2, GP, C])
        w_raw = sb("w_raw", [P, MIX_HEADS, P])
        wT = sb("wT", [P, MIX_HEADS, P])
        b_raw = sb("b_raw", [MIX_HEADS, WS * WS])
        b_wide = sb("b_wide", [MIX_HEADS, P])
        w_in = sb("w_in", [P, MIX_HEADS, WS * WS])
        side = sb("side", [P, 2])
        bias = sb("mix_bias", [P, MIX_HEADS])
        bst = sb("mbst", [P, CT, 8, 6])
        mv = sb("mmv", [P, CT, 2])
        T, ns = norm_tiles(sb, sem, "m")

        t_ps = psum("t_ps", [P, 2, 512])
        m_ps = psum("m_ps", [P, 2, 512])
        k_ps = psum("k_ps", [P, 3, 512])
        stat_ps = psum("mstat_ps", [P, 4])

        w_loaded, w_zero, b_loaded, b_ready = sem("w_loaded"), sem("w_zero"), sem("b_loaded"), sem("b_ready")
        b_turned = sem("b_turned")
        w_turned, w_ready = sem("w_turned"), sem("w_ready")
        pad_zero = sem("pad_zero")
        LOAD_ROWS = ((0, 16), (16, 40), (40, 64))
        STORE_ROWS = ((0, 20), (20, 44), (44, 64))
        x_loaded = [[sem(f"x_loaded{i}_{g}") for g in range(GROUPS)] for i in range(2)]
        x_stored = K["x_stored"]
        t_full, t_taken = sem("t_full"), sem("t_taken")
        m_full, m_taken = sem("m_full"), sem("m_taken")
        k_full, k_taken = sem("k_full"), sem("k_taken")
        xn_ready = sem("xn_ready")
        counted = sem("m_counted")
        N_T, N_M, N_K = GROUPS * FILLS, GROUPS * MIX_HEADS // 2, 3 * WIN_ROWS

        def load_matrices(eng, w):
            for r in range(WS):
                p0 = 16 * r + 8 * w
                eng.dma_start(w_in[p0:p0 + 8, :, :], w_mix[:, 8 * r:8 * r + 8, :].rearrange("h i j -> i h j"))\
                    .then_inc(w_loaded, 16)

        block = ctx.enter_context(nc.Block())

        @block.sync
        def _(sp):
            load_matrices(sp, 0)
            sp.dma_start(b_raw[:, :], b_mix[:, :]).then_inc(b_loaded, 16)
            for t in range(QT):
                src = w_qkv.rearrange("(h k c) i -> k h c i", k=3, c=D)[t // 2, HT * (t % 2):HT * (t % 2) + HT, :, :]
                sp.dma_start(K["w_qkv"][:, t, :], src).then_inc(K["wq_loaded"], 16)

            def body(i, last):
                for par in range(2):
                    b = 2 * i + par
                    for g in range(GROUPS):
                        y0, y1 = STORE_ROWS[g]
                        sp.wait_ge(k_taken, N_K * b + 3 * WR * (g + 1))
                        sp.dma_start(x1_dram[b, :, W * y0:W * y1].rearrange("(t p) n -> p t n", p=P),
                                     x[par][:, :, W * y0:W * y1]).then_inc(x_stored[par][g], 16)
            over_image_pairs(sp, body)

        @block.gpsimd
        def _(pool):
            def load(b, i, par):
                for g in range(GROUPS):
                    y0, y1 = LOAD_ROWS[g]
                    at_least(pool, x_stored[par][g], 16 * i)
                    pool.dma_start(x[par][:, :, W * y0:W * y1],
                                   x_in[b, :, :, :].rearrange("(t p) h w -> p t (h w)", p=P)[:, :, W * y0:W * y1])\
                        .then_inc(x_loaded[par][g], 16)

            load(0, 0, 0)
            K["fill"](pool)
            pool.memset(xpad[:, :, :, :, :], 0.0).then_inc(pad_zero, 1)
            load(1, 0, 1)

            def body(i, last):
                for par in range(2):
                    load(2 * i + par, i, par)
            with pool.Fori(1, B // 2) as i:
                body(i, False)

        @block.scalar
        def _(act):
            load_matrices(act, 1)
            act.wait_ge(b_loaded, 16)
            act.activation(b_wide[:, :].rearrange("h (r w c) -> h r w c", w=2, c=8),
                           b_raw[:, :].rearrange("h (r c) -> h r c", c=8).unsqueeze(2).broadcast_to([MIX_HEADS, WS, 2, WS]),
                           ACT.Copy).then_inc(b_ready, 1)
            act.wait_ge(b_turned, 1)
            act.activation(bias[:, :], k_ps[:, 0, 0:MIX_HEADS], ACT.Copy).then_inc(b_ready, 1)
            act.wait_ge(pad_zero, 1)

            def normalise(b, par):
                act.wait_ge(ns["scale"], b + 1)
                at_least(act, t_full, N_T * b)
                for ct in range(CT):
                    for q0, q1, c0, c1 in ((0, 1, SHIFT, 16), (1, PAIRS - 1, 0, 16), (PAIRS - 1, PAIRS, 0, SHIFT)):
                        x0 = 16 * q0 + c0 - SHIFT
                        cols = (q1 - q0) * (c1 - c0)
                        src = x[par][:, ct, :].rearrange("p (h w) -> p h w", w=W)[:, :, x0:x0 + cols]\
                            .rearrange("p h (q c) -> p h q c", q=q1 - q0)
                        dst = xpad[:, ct, q0:q1, SHIFT:SHIFT + H, c0:c1].rearrange("p q h c -> p h q c")
                        last = act.activation(dst, src, ACT.Identity, bias=T["nb"][:, ct:ct + 1],
                                              scale=T["sc"][:, ct:ct + 1])
                last.then_inc(xn_ready, 1)
                act.wait_ge(xn_ready, b + 1)
                act.activation(T["used"][:, 0:1], T["sc"][:, 0:1], ACT.Copy).then_inc(ns["scaled"], 1)

            norm_std(act, 0, T, ns)
            normalise(0, 0)
            for f in range(MIX_HEADS // 4):
                act.wait_ge(w_turned, f + 1)
                act.activation(wT[:, 4 * f:4 * f + 4, :].rearrange("p h m -> p (h m)"), t_ps[:, f % 2, :],
                               ACT.Copy).then_inc(w_ready, 1)

            def body(i, last_body):
                for par in range(2):
                    b = 2 * i + par
                    for g in range(GROUPS):
                        at_least(act, m_full, N_M * b + (MIX_HEADS // 2) * (g - 1))
                        for f in range(FILLS):
                            n = FILLS * g + f
                            np_ = min(2, GP - 2 * f)
                            act.wait_ge(t_full, N_T * b + n + 1)
                            act.activation(xT[:, (g + par) % 2, 2 * f:2 * f + np_, :].rearrange("p a c -> p (a c)"),
                                           t_ps[:, n % 2, 0:np_ * C], ACT.Copy).then_inc(t_taken, 1)
                    if not (last_body and par == 1):
                        norm_std(act, b + 1, T, ns)
                        normalise(b + 1, 1 - par)
            over_image_pairs(act, body)

        @block.tensor
        def _(pe):
            pe.wait_ge(b_ready, 1)
            pe.wait_ge(K["const_done"], CONST_STEPS)
            pe.transpose(k_ps[:, 0, 0:MIX_HEADS], b_wide[:, :], K["ident"][0:MIX_HEADS, 0:MIX_HEADS]).then_inc(b_turned, 1)
            for link in norm_group_sums(pe, 0, T, mv, stat_ps, K["gavg"], ns):
                link()
            pe.wait_ge(w_zero, 3)
            for f in range(MIX_HEADS // 4):
                at_least(pe, w_ready, f - 1)
                for j in range(4):
                    last = pe.transpose(t_ps[:, f % 2, P * j:P * j + P], w_raw[:, 4 * f + j, :], K["ident"][:, :])
                last.then_inc(w_turned, 1)
            pe.wait_ge(w_ready, MIX_HEADS // 4)

            def turn(b, g):
                for f in range(FILLS):
                    n = FILLS * g + f
                    at_least(pe, t_taken, N_T * b + n - 1)
                    for a in range(2 * f, min(2 * f + 2, GP)):
                        wy, q = WR * g + a // PAIRS, a % PAIRS
                        for ct in range(CT):
                            o = (a - 2 * f) * C + ct * P
                            last = pe.transpose(t_ps[:, n % 2, o:o + P],
                                                xpad[:, ct, q, WS * wy:WS * wy + WS, :].rearrange("p r c -> p (r c)"), K["ident"][:, :])
                    last.then_inc(t_full, 1)

            def mix(b, g, par, between={}):
                for hp in range(MIX_HEADS // 2):
                    if hp in between:
                        between[hp]()
                    n = (MIX_HEADS // 2) * g + hp
                    if hp == 0:
                        pe.wait_ge(t_taken, N_T * b + FILLS * (g + 1))
                    at_least(pe, m_taken, N_M * b + n - 1)
                    for j in range(2):
                        h = 2 * hp + j
                        last = pe.matmul(m_ps[:, n % 2, j * GP * MIX_CH:(j + 1) * GP * MIX_CH], wT[:, h, :],
                                         xT[:, (g + par) % 2, :, MIX_CH * h:MIX_CH * h + MIX_CH],
                                         start=True, stop=True)
                    last.then_inc(m_full, 1)

            def turn_back(b, g, par):
                pe.wait_ge(m_taken, N_M * b + (MIX_HEADS // 2) * (g + 1))
                for r in range(WR):
                    wy = WR * g + r
                    for u in range(3):
                        at_least(pe, k_taken, N_K * b + 3 * wy + u - 2)
                        for q, ct in ([(q, u) for q in range(4)] if u < CT else [(4, 0), (4, 1)]):
                            o = P * q if u < CT else P * ct
                            last = pe.transpose(k_ps[:, u, o:o + P], yT[:, (g + par) % 2, PAIRS * r + q, P * ct:P * ct + P],
                                                K["ident"][:, :])
                        last.then_inc(k_full, 1)

            def body(i, last_body):
                for par in range(2):
                    b = 2 * i + par
                    pe.wait_ge(xn_ready, b + 1)
                    turn(b, 0)
                    turn(b, 1)
                    mix(b, 0, par)
                    turn(b, 2)
                    if last_body and par == 1:
                        mix(b, 1, par)
                    else:
                        means, variances = norm_group_sums(pe, b + 1, T, mv, stat_ps, K["gavg"], ns)
                        mix(b, 1, par, {2: means, 4: variances})
                    turn_back(b, 0, par)
                    mix(b, 2, par)
                    turn_back(b, 1, par)
                    turn_back(b, 2, par)
            over_image_pairs(pe, body)

        @block.vector
        def _(dve):
            chain = Chain(dve, ns["chain"])

            PIECES = [[(ct, k) for ct in range(CT) for k in range(W * y0 // 512, W * y1 // 512)] for y0, y1 in LOAD_ROWS]

            def moments(b, par, i, g):
                dve.wait_ge(x_loaded[par][g], 16 * (i + 1))
                norm_moments(dve, bst, x[par], PIECES[g]).then_inc(counted, 1)
                if g == GROUPS - 1:
                    dve.wait_ge(counted, GROUPS * (b + 1))
                    dve.tensor_copy(T["t1"][:, 0:1], K["ident"][:, 0:1])

            dve.wait_ge(K["const_done"], CONST_STEPS)
            for g in range(GROUPS):
                moments(0, 0, 0, g)
            for link in norm_scale(dve, chain, 0, T, mv, bst, stat_ps, ns):
                link()
            dve.tensor_reduce(side[:, :], K["gmask"][:, :].rearrange("p (a w c) -> p w a c", w=2, c=8)[:, :, :, 0],
                              AX.X, ALU.add).then_inc(w_zero, 1)
            dve.wait_ge(w_zero, 1)
            dve.wait_ge(w_loaded, 16 * 2 * WS)
            for w in range(2):
                dve.tensor_scalar(w_raw[:, :, :].rearrange("p h (r w c) -> p h r w c", w=2, c=8)[:, :, :, w, :],
                                  w_in[:, :, :].rearrange("p h (r c) -> p h r c", c=8), side[:, w:w + 1], None,
                                  ALU.mult).then_inc(w_zero, 1)
            dve.wait_ge(b_ready, 2)

            def add_bias(b, g, par, between={}):
                for hp in range(MIX_HEADS // 2):
                    if hp in between:
                        between[hp]()
                    n = (MIX_HEADS // 2) * g + hp
                    if hp == 0:
                        at_least(dve, k_full, N_K * b + 3 * WR * (g - 1))
                    dve.wait_ge(m_full, N_M * b + n + 1)
                    c0 = 2 * hp * MIX_CH
                    out = yT[:, (g + par) % 2, :, c0:c0 + 2 * MIX_CH].rearrange("p a (h c) -> p h a c", h=2)
                    src = m_ps[:, n % 2, 0:2 * GP * MIX_CH].rearrange("p (h a c) -> p h a c", h=2, c=MIX_CH)
                    bb = bias[:, 2 * hp:2 * hp + 2].unsqueeze(2).unsqueeze(3).broadcast_to([P, 2, GP, MIX_CH])
                    dve.tensor_tensor(out, src, bb, ALU.add).then_inc(m_taken, 1)

            def add_rows(b, g, par):
                img = x[par][:, :, :].rearrange("p t (h w) -> p t h w", w=W)
                for r in range(WR):
                    wy = WR * g + r
                    r0, r1 = max(0, SHIFT - WS * wy), min(WS, H + SHIFT - WS * wy)
                    y0 = WS * wy + r0 - SHIFT
                    y1 = y0 + r1 - r0
                    for u in range(3):
                        dve.wait_ge(k_full, N_K * b + 3 * wy + u + 1)
                        if u < CT:
                            quad = k_ps[:, u, :].rearrange("p (q r c) -> p r q c", q=4, c=16)
                            left = img[:, u, y0:y1, 0:12]
                            dve.tensor_tensor(left, left, quad[:, r0:r1, 0, SHIFT:16], ALU.add)
                            mid = img[:, u, y0:y1, 12:60].rearrange("p r (q c) -> p r q c", c=16)
                            last = dve.tensor_tensor(mid, mid, quad[:, r0:r1, 1:4, :], ALU.add)
                        else:
                            right = img[:, :, y0:y1, 60:64]
                            edge = k_ps[:, u, 0:CT * P].rearrange("p (t r c) -> p t r c", t=CT, c=16)
                            last = dve.tensor_tensor(right, right, edge[:, :, r0:r1, 0:SHIFT], ALU.add)
                        last.then_inc(k_taken, 1)

            def body(i, last_body):
                for par in range(2):
                    b = 2 * i + par
                    nxt = not (last_body and par == 1)
                    npar, ni = (1, i) if par == 0 else (0, i + 1)
                    if nxt:
                        moments(b + 1, npar, ni, 0)
                        moments(b + 1, npar, ni, 1)
                    add_bias(b, 0, par)
                    if nxt:
                        moments(b + 1, npar, ni, 2)
                        start, centre, variance, scale = norm_scale(dve, chain, b + 1, T, mv, bst, stat_ps, ns)
                        start()
                        add_bias(b, 1, par, {2: centre, 4: variance, 5: scale})
                    else:
                        add_bias(b, 1, par)
                    dve.wait_ge(xn_ready, b + 1)
                    add_rows(b, 0, par)
                    add_bias(b, 2, par)
                    add_rows(b, 1, par)
                    add_rows(b, 2, par)
            over_image_pairs(dve, body)


def projections(nc, K, x1_dram, qkv_dram):
    with ExitStack() as ctx:
        def sb(name, shape, dt=F32):
            return ctx.enter_context(nc.sbuf_tensor(name, shape, dt))

        def psum(name, shape):
            return ctx.enter_context(nc.psum_tensor(name, shape, F32))

        def sem(name):
            return ctx.enter_context(nc.semaphore(name))

        NCH = 8
        TILES = (2, 4, 3, 5, 0, 1)
        x1 = K["images"]
        xn = sb("xn", [P, 2, CT, 512])
        xh = sb("xh", [P, 2, CT, 512], F32R)
        xl = sb("xl", [P, 2, CT, 512], F32R)
        w_raw = K["w_qkv"]
        wh = sb("wqh", [P, CT, QT * P], F32R)
        wl = sb("wql", [P, CT, QT * P], F32R)
        stage = sb("stage", [P, 4, QT, 2, PN])
        kv = sb("kv", [P, 2, 4, 512])
        kT = sb("kT", [P, 2, 4, P])
        vT = sb("vT", [P, 2, 4, VW])
        tick = sb("ptick", [P, 4])
        bst = sb("pbst", [P, CT, 8, 6])
        mv = sb("pmv", [P, CT, 2])
        T, ns = norm_tiles(sb, sem, "p")

        o_ps = psum("o_ps", [P, 3, 512])
        t_ps = psum("pt_ps", [P, 2, 512])
        vk_ps = psum("vk_ps", [P, 2, 512])
        stat_ps = psum("pstat_ps", [P, 4])

        w_loaded, w_turned, w_split = K["wq_loaded"], sem("wq_turned"), sem("wq_split")
        zeroed = sem("zeroed")
        x_loaded = [sem(f"x1_loaded{i}") for i in range(2)]
        xn_ready, x_free = sem("pxn_ready"), sem("px_free")
        xh_ready, xl_ready = sem("xh_ready"), sem("xl_ready")
        o_full = sem("o_full")
        kv_ready, q_ready = sem("kv_ready"), sem("q_ready")
        kv_ready_v, q_ready_v = sem("kv_ready_v"), sem("q_ready_v")
        staged = sem("staged")
        t_full, k_turned, v_turned = sem("pt_full"), sem("k_turned"), sem("v_turned")
        vk_full, vk_taken = sem("vk_full"), sem("vk_taken")
        stored = [sem(f"qkv_stored{i}") for i in range(4)]
        counted = sem("p_counted")

        def place(n):
            return 2 * (n // 4) + n % 2

        def image(i, par):
            if isinstance(i, int) and i == 0:
                return B - 2 + par
            return 2 * i + par - 2

        def uses(n):
            return sum(place(m) == place(n) for m in range(n))

        def inside(t, n):
            c = place(n)
            return stage[:, c, t, :, :].rearrange("p a (y x) -> p a y x", x=PBK)[:, :, c // 2:c // 2 + NB, c % 2:c % 2 + NB]

        def dense(ap):
            return ap.rearrange("p (a y x) -> p a y x", a=2, x=NB)

        block = ctx.enter_context(nc.Block())

        @block.sync
        def _(sp):
            for par in range(2):
                for g in range(GROUPS):
                    sp.wait_ge(K["x_stored"][par][g], 16 * (B // 2))
            own = Own(sp, w_loaded)

            def body(i, last):
                for par in range(2):
                    b = 2 * i + par
                    for n in range(NCH):
                        c = place(n)
                        p0 = 4 * ((n // 2 + 2) % 4) + 2 * ((n + 1) % 2)
                        own.wait_ge(staged, NCH * b + n + 1)
                        for t in (2, 4, 3, 5):
                            sp.dma_start(qkv_dram[P * t:P * t + P, p0:p0 + 2, image(i, par), :], stage[:, c, t, :, :])\
                                .then_inc(stored[c], 16)
                        own.wait_ge(q_ready, NCH * b + n + 1)
                        own.wait_ge(q_ready_v, NCH * b + n + 1)
                        for t in (0, 1):
                            sp.dma_start(qkv_dram[P * t:P * t + P, p0:p0 + 2, image(i, par), :], stage[:, c, t, :, :])\
                                .then_inc(stored[c], 16)
            over_image_pairs(sp, body)
            for c in range(4):
                sp.wait_ge(stored[c], 16 * QT * 2 * B)

        def stage_free(eng, b, n):
            at_least(eng, stored[place(n)], 16 * QT * (2 * b + uses(n)))

        @block.gpsimd
        def _(pool):
            pool.memset(stage[:, :, :, :, :], 0.0).then_inc(zeroed, 1)
            pool.memset(vT[:, :, :, P:VW], 1.0).then_inc(zeroed, 1)
            pool.wait_ge(zeroed, 2)

            def body(i, last_body):
                for par in range(2):
                    b = 2 * i + par
                    for n in range(NCH):
                        pool.wait_ge(kv_ready, 2 * (NCH * b + n + 1))
                        pool.wait_ge(kv_ready_v, 2 * (NCH * b + n + 1))
                        stage_free(pool, b, n)
                        pool.tensor_tensor(tick[:, n % 4:n % 4 + 1], K["ident"][:, 0:1], K["ident"][:, 1:2], ALU.add)
                        for j, t in enumerate((2, 4, 3, 5)):
                            last = pool.tensor_copy(inside(t, n), dense(kv[:, n % 2, j, :]))
                        last.then_inc(staged, 1)
            over_image_pairs(pool, body)

        @block.scalar
        def _(act):
            for f in range(3):
                act.wait_ge(w_turned, f + 1)
                act.activation(wh[:, :, P * 2 * f:P * 2 * f + 2 * P], t_ps[:, f % 2, :].rearrange("p (c m) -> p c m", c=CT),
                               ACT.Copy).then_inc(w_split, 1)
                act.wait_ge(w_split, 2 * f + 2)
            norm_std(act, 0, T, ns)
            act.wait_ge(zeroed, 2)

            def split(b, n, par):
                if n == 0:
                    act.wait_ge(ns["scale"], b + 1)
                at_least(act, xl_ready, NCH * b + n - 1)
                py, px = n // 2, 2 * (n % 2)
                for ct in range(CT):
                    src = x1[par][:, ct, :].rearrange("p (y py x px) -> p py px y x", py=4, x=NB, px=4)[:, py, px:px + 2, :, :]
                    last = act.activation(dense(xn[:, n % 2, ct, :]), src, ACT.Identity, bias=T["nb"][:, ct:ct + 1],
                                          scale=T["sc"][:, ct:ct + 1])
                last.then_inc(xn_ready, 1)
                act.wait_ge(xn_ready, NCH * b + n + 1)
                if n == NCH - 1:
                    act.activation(T["used"][:, 0:1], T["nb"][:, 0:1], ACT.Copy).then_inc(ns["scaled"], 1)
                at_least(act, o_full, QT * (NCH * b + n - 1))
                act.activation(xh[:, n % 2, :, :], xn[:, n % 2, :, :], ACT.Copy).then_inc(xh_ready, 1)

            def body(i, last_body):
                for par in range(2):
                    b = 2 * i + par
                    split(b, 0, par)
                    for n in range(NCH):
                        if n + 1 < NCH:
                            split(b, n + 1, par)
                        o0 = QT * (NCH * b + n)

                        def key(u):
                            act.wait_ge(o_full, o0 + 2 * u + 1)
                            if u == 0:
                                at_least(act, staged, NCH * b + n - 1)
                                at_least(act, t_full, 4 * (NCH * b + n - 1))
                            act.activation(kv[:, n % 2, 2 * u, :], o_ps[:, (2 * u) % 3, :], ACT.Copy).then_inc(kv_ready, 1)

                        def turned(u):
                            act.wait_ge(t_full, 4 * (NCH * b + n) + 2 * u + 1)
                            at_least(act, vk_full, NCH * b + n)
                            act.activation(kT[:, u, :, :].rearrange("p a c -> p (a c)"), t_ps[:, 0, :], ACT.Relu)\
                                .then_inc(k_turned, 1)
                        key(0)
                        key(1)
                        turned(0)
                        act.wait_ge(o_full, o0 + 5)
                        stage_free(act, b, n)
                        act.activation(inside(0, n), dense(o_ps[:, 1, :]), ACT.Copy).then_inc(q_ready, 1)
                        turned(1)
                        if n == 6 and not (last_body and par == 1):
                            norm_std(act, b + 1, T, ns)
                    if not last_body:
                        act.wait_ge(x_free, b + 1)
                        for g in range(GROUPS):
                            act.wait_ge(K["x_stored"][par][g], 16 * (B // 2))
                        act.dma_start(x1[par][:, :, :], x1_dram[b, :, :].rearrange("(t p) n -> p t n", p=P))\
                            .then_inc(x_loaded[par], 16)
            over_image_pairs(act, body)

        @block.tensor
        def _(pe):
            pe.wait_ge(w_loaded, 16 * QT)
            for f in range(3):
                at_least(pe, w_split, 2 * (f - 1))
                for ct in range(CT):
                    for j in range(2):
                        last = pe.transpose(t_ps[:, f % 2, P * (2 * ct + j):P * (2 * ct + j) + P],
                                            w_raw[:, 2 * f + j, P * ct:P * ct + P], K["ident"][:, :])
                last.then_inc(w_turned, 1)
            for link in norm_group_sums(pe, 0, T, mv, stat_ps, K["gavg"], ns):
                link()
            pe.wait_ge(w_split, 6)
            pe.wait_ge(zeroed, 2)

            def product(b, n, j):
                t = TILES[j]
                if j == 0:
                    at_least(pe, kv_ready_v, 2 * (NCH * b + n))
                    at_least(pe, q_ready, NCH * b + n)
                if j == 1:
                    at_least(pe, q_ready, NCH * b + n)
                if j == 2:
                    at_least(pe, q_ready_v, NCH * b + n)
                if j == 3:
                    pe.wait_ge(kv_ready, 2 * (NCH * b + n) + 1)
                if j == 4:
                    pe.wait_ge(kv_ready_v, 2 * (NCH * b + n) + 1)
                if j == 5:
                    pe.wait_ge(kv_ready, 2 * (NCH * b + n) + 2)
                k = 0
                for ct in range(CT):
                    for w, xx in ((wh, xh), (wl, xh), (wh, xl)):
                        last = pe.matmul(o_ps[:, j % 3, :], w[:, ct, P * t:P * t + P], xx[:, n % 2, ct, :],
                                         start=(k == 0), stop=(k == 5))
                        k += 1
                last.then_inc(o_full, 1)

            def turn(b, n, u):
                at_least(pe, k_turned, 2 * (NCH * b + n) + u)
                at_least(pe, v_turned, 2 * (NCH * b + n) + u)
                pe.wait_ge(kv_ready, 2 * (NCH * b + n) + u + 1)
                pe.wait_ge(kv_ready_v, 2 * (NCH * b + n) + u + 1)
                for s in range(2):
                    for a in range(4):
                        last = pe.transpose(t_ps[:, s, P * a:P * a + P], kv[:, n % 2, 2 * u + s, P * a:P * a + P],
                                            K["ident"][:, :])
                    last.then_inc(t_full, 1)

            def sum_vk(b, n, u):
                pe.wait_ge(k_turned, 2 * (NCH * b + n) + u + 1)
                pe.wait_ge(v_turned, 2 * (NCH * b + n) + u + 1)
                if n == 0:
                    at_least(pe, vk_taken, 2 * b)
                for a in range(4):
                    last = pe.matmul(vk_ps[:, u, 0:VW], kT[:, u, a, :], vT[:, u, a, :],
                                     start=(n == 0 and a == 0), stop=(n == NCH - 1 and a == 3))
                if u == 1:
                    last.then_inc(vk_full, 1)

            def body(i, last_body):
                for par in range(2):
                    b = 2 * i + par
                    for n in range(NCH):
                        pe.wait_ge(xh_ready, NCH * b + n + 1)
                        pe.wait_ge(xl_ready, NCH * b + n + 1)
                        for j in range(3):
                            product(b, n, j)
                        turn(b, n, 0)
                        product(b, n, 3)
                        sum_vk(b, n, 0)
                        product(b, n, 4)
                        turn(b, n, 1)
                        product(b, n, 5)
                        sum_vk(b, n, 1)
                        if n == 6 and not (last_body and par == 1):
                            for link in norm_group_sums(pe, b + 1, T, mv, stat_ps, K["gavg"], ns):
                                link()
            over_image_pairs(pe, body)

        @block.vector
        def _(dve):
            chain = Chain(dve, ns["chain"])
            for f in range(3):
                dve.wait_ge(w_split, 2 * f + 1)
                hi = wh[:, :, P * 2 * f:P * 2 * f + 2 * P]
                dve.tensor_tensor(wl[:, :, P * 2 * f:P * 2 * f + 2 * P], t_ps[:, f % 2, :].rearrange("p (c m) -> p c m", c=CT),
                                  hi.bitcast(F32), ALU.subtract).then_inc(w_split, 1)

            def moments(b, par, i, quarter):
                if quarter == 0:
                    at_least(dve, x_loaded[par], 16 * i)
                pieces = [(quarter // 2, k) for k in range(4 * (quarter % 2), 4 * (quarter % 2) + 4)]
                norm_moments(dve, bst, x1[par], pieces).then_inc(counted, 1)
                if quarter == 3:
                    dve.wait_ge(counted, 4 * (b + 1))
                    dve.tensor_copy(T["t1"][:, 0:1], K["ident"][:, 0:1])

            def scale(b):
                for link in norm_scale(dve, chain, b, T, mv, bst, stat_ps, ns):
                    link()

            for quarter in range(4):
                moments(0, 0, 0, quarter)
            scale(0)
            dve.wait_ge(zeroed, 2)

            def split(b, n):
                dve.wait_ge(xh_ready, NCH * b + n + 1)
                dve.tensor_tensor(xl[:, n % 2, :, :], xn[:, n % 2, :, :], xh[:, n % 2, :, :].bitcast(F32),
                                  ALU.subtract).then_inc(xl_ready, 1)

            def body(i, last_body):
                for par in range(2):
                    b = 2 * i + par
                    nxt = not (last_body and par == 1)
                    npar, ni = (1, i) if par == 0 else (0, i + 1)
                    split(b, 0)
                    for n in range(NCH):
                        if n + 1 < NCH:
                            split(b, n + 1)
                        if n == NCH - 1:
                            dve.wait_ge(xn_ready, NCH * (b + 1))
                            dve.tensor_copy(T["t1"][:, 0:1], K["ident"][:, 0:1]).then_inc(x_free, 1)
                        o0 = QT * (NCH * b + n)
                        for u in range(2):
                            dve.wait_ge(o_full, o0 + 2 * u + 2)
                            if u == 0:
                                at_least(dve, staged, NCH * b + n - 1)
                            dve.tensor_copy(kv[:, n % 2, 2 * u + 1, :], o_ps[:, (2 * u + 1) % 3, :]).then_inc(kv_ready_v, 1)
                            dve.wait_ge(t_full, 4 * (NCH * b + n) + 2 * u + 2)
                            at_least(dve, vk_full, NCH * b + n)
                            dve.tensor_copy(vT[:, u, :, 0:P], t_ps[:, 1, :].rearrange("p (a c) -> p a c", a=4))\
                                .then_inc(v_turned, 1)
                        dve.wait_ge(o_full, o0 + 6)
                        stage_free(dve, b, n)
                        dve.tensor_copy(inside(1, n), dense(o_ps[:, 2, :])).then_inc(q_ready_v, 1)
                        if nxt and 2 <= n < 6:
                            moments(b + 1, npar, ni, n - 2)
                        if nxt and n == 6:
                            scale(b + 1)
                    dve.wait_ge(vk_full, NCH * (b + 1))
                    for u in range(2):
                        dve.tensor_copy(K["vk"][:, bass.ds(image(i, par), 1), u, :].rearrange("p a c -> p (a c)"), vk_ps[:, u, 0:VW])\
                            .then_inc(vk_taken, 1)
            over_image_pairs(dve, body)


def over_head_pairs(eng, body):
    body(0, False)
    with eng.Fori(1, AH // 2 - 1) as i:
        body(i, False)
    body(AH // 2 - 1, True)


def convolved_heads(nc, K, w_dw, w_pw, taps_dram, qkv_dram, att_dram):
    with ExitStack() as ctx:
        def sb(name, shape, dt=F32):
            return ctx.enter_context(nc.sbuf_tensor(name, shape, dt))

        def psum(name, shape):
            return ctx.enter_context(nc.psum_tensor(name, shape, F32))

        def sem(name):
            return ctx.enter_context(nc.semaphore(name))

        STEPS = B // 2
        TT = TAP * TAP
        dw = sb("dw", [P, QT, 25])
        flip = sb("flip", [P, QT, 25])
        shifted = sb("shifted", [P, QT, NPH, TT])
        taps = sb("taps", [P, QT * HT, TT])
        pw_raw = sb("pw_raw", [P, QT, D])
        pw_rep = sb("pw_rep", [P, QT, NPH, D])
        pw = sb("pw", [P, QT * HT, D])
        wprod = sb("wprod", [P, 3, TT, D])
        wh = [sb(f"wh{i}", [P, 3, TT * D], F32R) for i in range(2)]
        wl = [sb(f"wl{i}", [P, 3, TT * D], F32R) for i in range(2)]
        raw = [sb(f"raw{i}", [P, 3, 2 * PN]) for i in range(2)]
        dh = [sb(f"dh{i}", [P, 3, 2 * PN], F32R) for i in range(2)]
        dl = [sb(f"dl{i}", [P, 3, 2 * PN], F32R) for i in range(2)]
        qy = sb("qy", [P, 2, 512])
        ky = sb("ky", [P, 512])
        vy = sb("vy", [P, 512])
        kT = sb("ykT", [P, 4, P])
        vT = sb("yvT", [P, 4, VW])
        diag = sb("diag", [P, 2, VW])
        mask1 = sb("mask1", [P, VW])
        vkr = sb("vkr", [P, 2, D])
        vkb = sb("vkb", [P, 2, P])
        ksb = sb("ksb", [P, 2, P])
        den = sb("den", [P, 512])
        rec = sb("rec", [P, 512])
        att = sb("att", [P, 2, 512])

        c_ps = psum("c_ps", [P, 2, 512])
        kt_ps, vt_ps = psum("kt_ps", [P, 512]), psum("vt_ps", [P, 512])
        vk_ps, t1_ps = psum("yvk_ps", [P, 512]), psum("t1_ps", [P, 512])
        out_ps, den_ps = psum("out_ps", [P, 512]), psum("den_ps", [P, 512])

        dw_loaded, pw_loaded, taps_out, taps_loaded = sem("dw_loaded"), sem("pw_loaded"), sem("taps_out"), sem("taps_loaded")
        init, turned, pw_ready = sem("init"), sem("pw_turned"), sem("pw_ready")
        raw_loaded = [sem(f"raw_loaded{i}") for i in range(2)]
        hi_ready, lo_ready = sem("hi_ready"), sem("lo_ready")
        w_prod, w_hi, w_lo = sem("w_prod"), sem("w_hi"), sem("w_lo")
        c_full, q_out, k_out, v_out = sem("c_full"), sem("q_out"), sem("k_out"), sem("v_out")
        kt_full, vt_full = sem("kt_full"), sem("vt_full")
        k_taken, v_taken = sem("yk_taken"), sem("yv_taken")
        vk_full, diag_ready, t1_full, bd_ready = sem("yvk_full"), sem("diag_ready"), sem("t1_full"), sem("bd_ready")
        out_full, out_taken = sem("out_full"), sem("out_taken")
        stored = [sem(f"att_stored{i}") for i in range(2)]
        link = sem("y_chain")
        lo_div = sem("div_chain")

        qkv_v = qkv_dram.rearrange("(k h c) p b n -> k h p c (b n)", k=3, c=D)
        att_v = att_dram.rearrange("(h d) p b n -> h p d (b n)", d=D)

        block = ctx.enter_context(nc.Block())

        def steps_of(i):
            for hp in range(2):
                for j in range(STEPS):
                    yield hp, 2 * i + hp, j, 2 * STEPS * i + STEPS * hp + j

        @block.sync
        def _(sp):
            own = Own(sp, init)
            for t in range(QT):
                rows = w_dw.rearrange("(h k c) i y x -> k h c (i y x)", k=3, c=D)[t // 2, HT * (t % 2):HT * (t % 2) + HT, :, :]
                sp.dma_start(dw[:, t, :], rows).then_inc(dw_loaded, 16)
                rows = w_pw.rearrange("(h k o) c y x -> k h o (c y x)", k=3, o=D)[t // 2, HT * (t % 2):HT * (t % 2) + HT, :, :]
                sp.dma_start(pw_raw[:, t, :], rows).then_inc(pw_loaded, 16)
            sp.wait_ge(init, 3)
            sp.dma_start(taps_dram.rearrange("t q p n -> q t (p n)"), shifted[:, :, :, :].rearrange("q t p n -> q t (p n)"))\
                .then_inc(taps_out, 16)
            sp.wait_ge(taps_out, 16)
            for p in range(NPH):
                src = taps_dram.rearrange("t (h c) p n -> p c (t h) n", c=D)[p, :, :, :]
                sp.dma_start(taps[D * p:D * p + D, :, :], src).then_inc(taps_loaded, 16)

            def store(h, j, s):
                own.wait_ge(out_taken, s + 1)
                sp.dma_start(att_v[h, :, :, 2 * POS * j:2 * POS * j + 2 * POS], att[:, j % 2, :]).then_inc(stored[j % 2], 16)

            def body(i, last):
                for hp, h, j, s in steps_of(i):
                    if not isinstance(s, int) or s >= 2:
                        own.wait_ge(hi_ready, s - 1)
                        own.wait_ge(lo_ready, s - 1)
                    for k in range(3):
                        sp.dma_start(raw[j % 2][:, k, :], qkv_v[k, h, :, :, 2 * PN * j:2 * PN * j + 2 * PN])\
                            .then_inc(raw_loaded[j % 2], 16)
                    if not isinstance(s, int) or s >= STEPS:
                        store(h - 1, j, s - STEPS)
            over_head_pairs(sp, body)
            for j in range(STEPS):
                store(AH - 1, j, STEPS * (AH - 1) + j)
            for c in range(2):
                sp.wait_ge(stored[c], 16 * STEPS * AH // 2)

        @block.gpsimd
        def _(pool):
            pool.memset(shifted[:, :, :, :], 0.0).then_inc(init, 1)

            def weights_low(h, par):
                pool.wait_ge(w_hi, h + 1)
                at_least(pool, c_full, 3 * STEPS * (h - 1))
                pool.tensor_tensor(wl[par][:, :, :], wprod[:, :, :, :].rearrange("p k a o -> p k (a o)"),
                                   wh[par][:, :, :].bitcast(F32), ALU.subtract).then_inc(w_lo, 1)

            def split(s, j):
                pool.wait_ge(hi_ready, s + 1)
                pool.tensor_tensor(dl[j % 2][:, :, :], raw[j % 2][:, :, :], dh[j % 2][:, :, :].bitcast(F32), ALU.subtract)\
                    .then_inc(lo_ready, 1)

            weights_low(0, 0)
            split(0, 0)

            def body(i, last):
                for hp, h, j, s in steps_of(i):
                    end = last and hp == 1
                    if not (end and j == STEPS - 1):
                        split(s + 1, j + 1)
                    if j == 2 and not end:
                        weights_low(h + 1, 1 - hp)
            over_head_pairs(pool, body)

        @block.scalar
        def _(act):
            act.wait_ge(pw_loaded, 16 * QT)
            act.activation(pw_rep[:, :, :, :], pw_raw[:, :, :].unsqueeze(2).broadcast_to([P, QT, NPH, D]), ACT.Copy)\
                .then_inc(pw_ready, 1)
            act.wait_ge(turned, 1)
            act.activation(pw[:, 0:4 * HT, :].rearrange("p g o -> p (g o)"), c_ps[:, 0, :], ACT.Copy).then_inc(pw_ready, 1)
            act.activation(pw[:, 4 * HT:6 * HT, :].rearrange("p g o -> p (g o)"), c_ps[:, 1, 0:2 * P], ACT.Copy)\
                .then_inc(pw_ready, 1)

            def weights_high(h, par):
                act.wait_ge(w_prod, h + 1)
                at_least(act, c_full, 3 * STEPS * (h - 1))
                act.activation(wh[par][:, :, :], wprod[:, :, :, :].rearrange("p k a o -> p k (a o)"), ACT.Copy)\
                    .then_inc(w_hi, 1)

            def split(s, j, use):
                act.wait_ge(raw_loaded[j % 2], 48 * use)
                at_least(act, c_full, 3 * (s - 1))
                act.activation(dh[j % 2][:, :, :], raw[j % 2][:, :, :], ACT.Copy).then_inc(hi_ready, 1)

            weights_high(0, 0)
            split(0, 0, 1)

            def body(i, last):
                for hp, h, j, s in steps_of(i):
                    end = last and hp == 1
                    if not (end and j == STEPS - 1):
                        split(s + 1, j + 1, 4 * i + 2 * hp + (j + 1) // 2 + 1)
                    act.wait_ge(c_full, 3 * s + 1)
                    act.activation(qy[:, j % 2, :], c_ps[:, j % 2, :], ACT.Relu).then_inc(q_out, 1)
                    if j == 2 and not end:
                        weights_high(h + 1, 1 - hp)
                    act.wait_ge(c_full, 3 * s + 2)
                    at_least(act, kt_full, s)
                    act.activation(ky[:, :], c_ps[:, (j + 1) % 2, :], ACT.Relu).then_inc(k_out, 1)
                    act.wait_ge(kt_full, s + 1)
                    at_least(act, vk_full, s)
                    act.activation(kT[:, :, :].rearrange("p a c -> p (a c)"), kt_ps[:, :], ACT.Copy).then_inc(k_taken, 1)
            over_head_pairs(act, body)

        @block.tensor
        def _(pe):
            pe.wait_ge(pw_ready, 1)
            for t in range(QT):
                dst = c_ps[:, t // 4, P * (t % 4):P * (t % 4) + P]
                last = pe.transpose(dst, pw_rep[:, t, :, :].rearrange("p a c -> p (a c)"), K["ident"][:, :])
            last.then_inc(turned, 1)
            pe.wait_ge(pw_ready, 3)
            pe.wait_ge(init, 5)

            def convolve(s, j, par, kind):
                if kind == 0:
                    pe.wait_ge(lo_ready, s + 1)
                if kind == 0:
                    at_least(pe, k_out, s)
                elif kind == 1:
                    at_least(pe, v_out, s)
                else:
                    pe.wait_ge(q_out, s + 1)
                k = 0
                for dy in range(2):
                    for dx in range(2):
                        o = (1 - dx) * 4 * TAP * D + (1 - dy) * P
                        for w, d in ((wh, dh), (wl, dh), (wh, dl)):
                            src = d[j % 2][:, kind, :].rearrange("p (b y x) -> p b y x", b=2, x=PBK)[:, :, dy:dy + NB, dx:dx + NB]
                            last = pe.matmul(c_ps[:, (j + kind) % 2, :], w[par][:, kind, o:o + P], src,
                                             start=(k == 0), stop=(k == 11))
                            k += 1
                last.then_inc(c_full, 1)

            def turn(s, src, ps, ready, taken, full):
                pe.wait_ge(ready, s + 1)
                at_least(pe, taken, s)
                for a in range(4):
                    last = pe.transpose(ps[:, P * a:P * a + P], src[:, P * a:P * a + P], K["ident"][:, :])
                last.then_inc(full, 1)

            def sum_vk(s):
                pe.wait_ge(k_taken, s + 1)
                pe.wait_ge(v_taken, s + 1)
                at_least(pe, diag_ready, s)
                for b in range(2):
                    for half in range(2):
                        a = 2 * b + half
                        last = pe.matmul(vk_ps[:, VW * b:VW * b + VW], kT[:, a, :], vT[:, a, :],
                                         start=(half == 0), stop=(half == 1))
                last.then_inc(vk_full, 1)

            def sum_phases(s):
                pe.wait_ge(diag_ready, s + 1)
                at_least(pe, bd_ready, s)
                pe.matmul(t1_ps[:, 0:2 * VW], K["same_ch"][:, :], diag[:, :, :].rearrange("p b n -> p (b n)"),
                          start=True, stop=True).then_inc(t1_full, 1)

            def attend(s, j):
                pe.wait_ge(bd_ready, s + 1)
                at_least(pe, out_taken, s)
                for ps, w in ((out_ps, vkb), (den_ps, ksb)):
                    for b in range(2):
                        last = pe.matmul(ps[:, POS * b:POS * b + POS], w[:, b, :], qy[:, j % 2, POS * b:POS * b + POS],
                                         start=True, stop=True)
                last.then_inc(out_full, 1)

            def body(i, last):
                for hp, h, j, s in steps_of(i):
                    pj = (j + 1) % 2
                    prev = not isinstance(s, int) or s >= 1
                    if j == 0:
                        pe.wait_ge(w_lo, h + 1)
                    convolve(s, j, hp, 0)
                    if prev:
                        sum_vk(s - 1)
                    convolve(s, j, hp, 1)
                    if prev:
                        sum_phases(s - 1)
                    convolve(s, j, hp, 2)
                    turn(s, ky, kt_ps, k_out, k_taken, kt_full)
                    if prev:
                        attend(s - 1, pj)
                    turn(s, vy, vt_ps, v_out, v_taken, vt_full)
            over_head_pairs(pe, body)
            s = AH * STEPS - 1
            sum_vk(s)
            sum_phases(s)
            attend(s, 1)

        @block.vector
        def _(dve):
            dve.wait_ge(dw_loaded, 16 * QT)
            dve.wait_ge(init, 1)
            for k in range(25):
                last = dve.tensor_copy(flip[:, :, k:k + 1], dw[:, :, 24 - k:25 - k])
            last.then_inc(init, 1)
            dve.wait_ge(init, 2)
            fl = flip[:, :, :].rearrange("p t (y x) -> p t y x", x=5)
            for p in range(NPH):
                py, px = p // 4, p % 4
                grid = shifted[:, :, p, :].rearrange("p t (d u q) -> p d t u q", d=2, q=4)
                dve.tensor_copy(grid[:, 0, :, py:py + 5, px:4], fl[:, :, :, 0:4 - px])
                last = dve.tensor_copy(grid[:, 1, :, py:py + 5, 0:px + 1], fl[:, :, :, 4 - px:5])
            last.then_inc(init, 1)
            dve.tensor_copy(mask1[:, 0:P], K["gmask"][:, :]).then_inc(init, 1)
            dve.memset(mask1[:, P:VW], 1.0)
            dve.memset(vT[:, :, P:VW], 1.0).then_inc(init, 1)
            dve.wait_ge(pw_ready, 3)
            dve.wait_ge(taps_loaded, 16 * NPH)
            dve.wait_ge(init, 5)

            chain = Chain(dve, link)

            def weights(h):
                at_least(dve, w_lo, h)
                at_least(dve, w_hi, h)
                tv = taps[:, :, :].rearrange("p (k h) n -> p k h n", k=3)[:, :, bass.ds(h, 1), :]
                pv = pw[:, :, :].rearrange("p (k h) o -> p k h o", k=3)[:, :, bass.ds(h, 1), :]
                tv = tv.rearrange("p k a n -> p k (a n)").unsqueeze(3).broadcast_to([P, 3, TT, D])
                pv = pv.broadcast_to([P, 3, TT, D])
                dve.tensor_tensor(wprod[:, :, :, :], tv, pv, ALU.mult).then_inc(w_prod, 1)

            def keep_diagonal(s):
                dve.wait_ge(vk_full, s + 1)
                dve.tensor_tensor(diag[:, :, :], vk_ps[:, 0:2 * VW].rearrange("p (b n) -> p b n", b=2),
                                  mask1[:, :].unsqueeze(1).broadcast_to([P, 2, VW]), ALU.mult).then_inc(diag_ready, 1)

            def spread(s):
                dve.wait_ge(t1_full, s + 1)
                t1 = t1_ps[:, 0:2 * VW].rearrange("p (b n) -> p b n", b=2)
                chain.base, chain.n = s, 0
                chain(dve.tensor_reduce(vkr[:, :, :], t1[:, :, 0:P].rearrange("p b (a d) -> p b d a", d=D), AX.X, ALU.add))
                for b in range(2):
                    dve.tensor_tensor(vkb[:, b, :].rearrange("p (a d) -> p a d", d=D),
                                      K["gmask"][:, :].rearrange("p (a d) -> p a d", d=D),
                                      vkr[:, b, :].unsqueeze(1).broadcast_to([P, NPH, D]), ALU.mult)
                    last = dve.tensor_scalar(ksb[:, b, :], K["gmask"][:, :], t1[:, b, P:VW], None, ALU.mult)
                last.then_inc(bd_ready, 1)

            link2 = Chain(dve, lo_div)

            def divide(s, j, stored_use):
                dve.wait_ge(out_full, s + 1)
                link2.base, link2.n = 2 * s, 0
                link2(dve.tensor_scalar(den[:, :], den_ps[:, :], ATT_EPS, None, ALU.add))
                link2(dve.reciprocal(rec[:, :], den[:, :]))
                at_least(dve, stored[j % 2], 16 * stored_use)
                dve.tensor_tensor(att[:, j % 2, :], out_ps[:, :], rec[:, :], ALU.mult).then_inc(out_taken, 1)

            weights(0)

            def body(i, last):
                for hp, h, j, s in steps_of(i):
                    end = last and hp == 1
                    prev = not isinstance(s, int) or s >= 1
                    if prev:
                        keep_diagonal(s - 1)
                        spread(s - 1)
                    dve.wait_ge(c_full, 3 * s + 3)
                    at_least(dve, vt_full, s)
                    dve.tensor_copy(vy[:, :], c_ps[:, j % 2, :]).then_inc(v_out, 1)
                    dve.wait_ge(vt_full, s + 1)
                    at_least(dve, vk_full, s)
                    dve.tensor_copy(vT[:, :, 0:P], vt_ps[:, :].rearrange("p (a c) -> p a c", a=4)).then_inc(v_taken, 1)
                    if j == 1 and not end:
                        weights(h + 1)
                    if prev:
                        divide(s - 1, (j - 1) % 2, 4 * i + 2 * hp + (j - 1) // 2)
            over_head_pairs(dve, body)
            s = AH * STEPS - 1
            keep_diagonal(s)
            spread(s)
            divide(s, 1, AH * STEPS // 2 - 1)


def output(nc, K, w_proj, gamma, beta, mean, var, x1_dram, qkv_dram, att_dram, out_dram):
    with ExitStack() as ctx:
        def sb(name, shape, dt=F32):
            return ctx.enter_context(nc.sbuf_tensor(name, shape, dt))

        def psum(name, shape):
            return ctx.enter_context(nc.psum_tensor(name, shape, F32))

        def sem(name):
            return ctx.enter_context(nc.semaphore(name))

        KT = 4
        CH = 4
        projT = sb("projT", [P, KT, C])
        bn = {n: sb(f"bn_{n}", [P, CT]) for n in ("gamma", "beta", "mean", "var", "ve", "std", "r0", "t1", "t2", "t3",
                                                  "r", "inv", "mi", "shift")}
        pick = sb("pick", [P, 2, 4, 32])
        spread = sb("spread", [P, 2, P])
        fold_all = sb("fold_all", [P, B, 2, C])
        ks_all = sb("ks_all", [P, B, 2, 32])
        fold = [sb(f"fold{i}", [P, 2, C]) for i in range(2)]
        vkm, vkT = fold[0][:, :, 0:P], fold[1][:, :, 0:P]
        ks = [sb(f"ks{i}", [P, 2, 32]) for i in range(2)]
        x1 = [sb(f"ox{i}", [P, CT, H * W]) for i in range(2)]
        q = [sb(f"oq{i}", [P, 2, 8, PN]) for i in range(2)]
        att = [sb(f"oatt{i}", [P, 2, 8, POS]) for i in range(2)]
        pr_raw = att[1][:, 0, 0:4, :].rearrange("p (t a) n -> p t (a n)", t=CT)
        prs = att[1][:, 1, 0:4, :].rearrange("p (t a) n -> p t (a n)", t=CT)
        qr = [sb(f"qr{i}", [P, 2, CH, 512]) for i in range(2)]
        rec = [sb(f"orec{i}", [P, 512]) for i in range(2)]

        den_ps = psum("oden_ps", [P, 512])
        bc_ps = psum("bc_ps", [P, 2, 512])
        z_ps = psum("z_ps", [P, 2, 2, 512])

        w_loaded, link, turned, ready = sem("ow_loaded"), sem("o_chain"), sem("o_turned"), sem("o_ready")
        std_in, std_out = sem("bn_var"), sem("bn_std")
        x_loaded = [sem(f"ox_loaded{i}") for i in range(2)]
        in_loaded = [sem(f"oin_loaded{i}") for i in range(2)]
        x_stored = [sem(f"ox_stored{i}") for i in range(2)]
        q_relu, a_ready = sem("q_relu"), sem("a_ready")
        den_full, den_taken, rec_ready = sem("den_full"), sem("den_taken"), sem("rec_ready")
        bc_full, q_scaled = sem("bc_full"), sem("q_scaled")
        z_full, z_taken = sem("z_full"), sem("z_taken")
        link_vk, x_shifted = sem("vk_masked"), sem("x_shifted")

        block = ctx.enter_context(nc.Block())

        @block.sync
        def _(sp):
            sp.dma_start(pr_raw, w_proj.rearrange("(t p) k -> p t k", p=P)).then_inc(w_loaded, 16)
            with nc.allow_non_contiguous_dma(reason="256 values each"):
                for n, v in (("gamma", gamma), ("beta", beta), ("mean", mean), ("var", var)):
                    sp.dma_start(bn[n][:, :], v.rearrange("(t p) -> p t", p=P)).then_inc(w_loaded, 16)

            def body(i, last):
                for par in range(2):
                    b = 2 * i + par
                    sp.wait_ge(z_taken, 4 * CH * (b + 1))
                    sp.dma_start(out_dram[b, :, :].rearrange("(t p) n -> p t n", p=P), x1[par][:, :, :])\
                        .then_inc(x_stored[par], 16)
            over_image_pairs(sp, body)
            for par in range(2):
                sp.wait_ge(x_stored[par], 16 * (B // 2))

        @block.gpsimd
        def _(pool):
            def body(i, last):
                for par in range(2):
                    b = 2 * i + par
                    at_least(pool, x_stored[par], 16 * i)
                    pool.dma_start(x1[par][:, :, :], x1_dram[b, :, :].rearrange("(t p) n -> p t n", p=P))\
                        .then_inc(x_loaded[par], 16)
                    for hb in range(2):
                        g = 2 * b + hb
                        if isinstance(g, int) and g == 1:
                            pool.wait_ge(ready, 2 + KT)
                        if not isinstance(g, int) or g >= 2:
                            pool.wait_ge(z_full, CH * (g - 1))
                        for t in range(2):
                            pool.dma_start(q[hb][:, t, :, :], qkv_dram[P * t:P * t + P, 8 - 8 * hb:16 - 8 * hb, b, :])\
                                .then_inc(in_loaded[hb], 16)
                            pool.dma_start(att[hb][:, t, :, :], att_dram[P * t:P * t + P, 8 * hb:8 * hb + 8, b, :])\
                                .then_inc(in_loaded[hb], 16)
            over_image_pairs(pool, body)

        @block.scalar
        def _(act):
            act.wait_ge(std_in, 1)
            act.activation(bn["std"][:, :], bn["ve"][:, :], ACT.Sqrt).then_inc(std_out, 1)
            for kt in range(KT):
                act.wait_ge(turned, kt + 1)
                act.activation(projT[:, kt, :], z_ps[:, 0, kt % 2, 0:C], ACT.Copy).then_inc(ready, 1)
            act.wait_ge(turned, KT + 1)
            act.activation(spread[:, :, :].rearrange("p t c -> p (t c)"), z_ps[:, 1, 0, 0:2 * P], ACT.Copy).then_inc(ready, 1)
            for n in range(2 * B):
                b, t = n // 2, n % 2
                act.wait_ge(turned, KT + 2 + 2 * n)
                act.activation(vkT[:, t, :], bc_ps[:, 0, 0:P], ACT.Copy).then_inc(ready, 1)
                act.wait_ge(turned, KT + 3 + 2 * n)
                act.activation(fold_all[:, b, t, :], bc_ps[:, 1, 0:C], ACT.Copy).then_inc(ready, 1)

            def body(i, last):
                for par in range(2):
                    b = 2 * i + par
                    for hb in range(2):
                        g = 2 * b + hb
                        act.wait_ge(in_loaded[hb], 64 * (2 * i + par + 1))
                        at_least(act, z_full, CH * (g - 1))
                        for t in range(2):
                            for c in range(CH):
                                p0 = 4 * (c // 2) + 2 * ((c + 1) % 2)
                                ox = c % 2
                                src = q[hb][:, t, p0:p0 + 2, :].rearrange("p a (y x) -> p a y x", x=PBK)[:, :, hb:hb + NB, ox:ox + NB]
                                last_i = act.activation(qr[hb][:, t, c, :].rearrange("p (a y x) -> p a y x", a=2, x=NB), src, ACT.Relu)
                        last_i.then_inc(q_relu, 1)
                        if hb == 0:
                            act.activation(fold[par][:, :, :], fold_all[:, bass.ds(b, 1), :, :].rearrange("p a t c -> p (a t) c"), ACT.Copy)
                            act.activation(ks[par][:, :, :], ks_all[:, bass.ds(b, 1), :, :].rearrange("p a t c -> p (a t) c"), ACT.Copy)\
                                .then_inc(a_ready, 1)
                            act.wait_ge(x_loaded[par], 16 * (i + 1))
                            for o in range(CT):
                                last_i = act.activation(x1[par][:, o, :], x1[par][:, o, :], ACT.Identity,
                                                        bias=bn["shift"][:, o:o + 1])
                            last_i.then_inc(x_shifted, 1)
            over_image_pairs(act, body)

        @block.tensor
        def _(pe):
            for kt in range(KT):
                if kt == 0:
                    pe.wait_ge(ready, 2)
                at_least(pe, ready, 2 + kt - 1)
                for o in range(CT):
                    last = pe.transpose(z_ps[:, 0, kt % 2, P * o:P * o + P], prs[:, o, P * kt:P * kt + P], K["ident"][:, :])
                last.then_inc(turned, 1)
            for t in range(2):
                last = pe.transpose(z_ps[:, 1, 0, P * t:P * t + P], pick[:, t, :, :].rearrange("p a c -> p (a c)"), K["ident"][:, :])
            last.then_inc(turned, 1)
            for n in range(2 * B):
                b, t = n // 2, n % 2
                pe.wait_ge(link_vk, n + 1)
                pe.wait_ge(ready, 2 + KT + 1 + 2 * n)
                pe.transpose(bc_ps[:, 0, 0:P], vkm[:, n % 2, :], K["ident"][:, :]).then_inc(turned, 1)
                pe.wait_ge(ready, 2 + KT + 2 + 2 * n)
                pe.matmul(bc_ps[:, 1, 0:C], vkT[:, t, :], projT[:, t, :], start=True, stop=True).then_inc(turned, 1)
            pe.wait_ge(ready, 2 + KT + 1 + 4 * B)

            def denominators(g, hb, par, b):
                pe.wait_ge(q_relu, g + 1)
                if hb == 0:
                    pe.wait_ge(a_ready, b + 1)
                at_least(pe, den_taken, g)
                for c in range(CH):
                    for t in range(2):
                        last = pe.matmul(den_ps[32 * c:32 * c + 32, :], ks[par][:, t, :], qr[hb][:, t, c, :],
                                         start=(t == 0), stop=(t == 1))
                last.then_inc(den_full, 1)

            def to_channels(g, hb, c):
                if c == 0:
                    pe.wait_ge(rec_ready, g + 1)
                at_least(pe, q_scaled, CH * g + c)
                for t in range(2):
                    last = pe.matmul(bc_ps[:, t, :], spread[32 * c:32 * c + 32, t, :], rec[hb][32 * c:32 * c + 32, :],
                                     start=True, stop=True)
                last.then_inc(bc_full, 1)

            def project(g, hb, par, c, direct):
                if not direct:
                    at_least(pe, z_taken, 2 * (CH * g + c - 1))
                else:
                    pe.wait_ge(q_scaled, CH * g + c + 1)
                for o in range(CT):
                    for t in range(2):
                        if direct:
                            last = pe.matmul(z_ps[:, c % 2, o, :], fold[par][:, t, P * o:P * o + P], qr[hb][:, t, c, :],
                                             start=False, stop=(t == 1))
                        else:
                            last = pe.matmul(z_ps[:, c % 2, o, :], projT[:, 2 + t, P * o:P * o + P],
                                             att[hb][:, t, 2 * c:2 * c + 2, :].rearrange("p a n -> p (a n)"),
                                             start=(t == 0), stop=False)
                if direct:
                    last.then_inc(z_full, 1)

            pe.wait_ge(in_loaded[0], 64)
            denominators(0, 0, 0, 0)

            def body(i, last_body):
                for par in range(2):
                    b = 2 * i + par
                    for hb in range(2):
                        g = 2 * b + hb
                        to_channels(g, hb, 0)
                        for c in range(CH):
                            if c == 0:
                                pe.wait_ge(in_loaded[hb], 64 * (2 * i + par + 1))
                            project(g, hb, par, c, False)
                            if c + 1 < CH:
                                to_channels(g, hb, c + 1)
                            project(g, hb, par, c, True)
                            if c == 1 and not (last_body and par == 1 and hb == 1):
                                npar = par if hb == 0 else 1 - par
                                denominators(g + 1, 1 - hb, npar, b + hb)
            over_image_pairs(pe, body)

        @block.vector
        def _(dve):
            chain = Chain(dve, link)
            dve.wait_ge(w_loaded, 16 * 5)
            chain(dve.tensor_scalar(bn["ve"][:, :], bn["var"][:, :], BN_EPS, None, ALU.add))
            dve.tensor_copy(bn["t1"][:, :], bn["ve"][:, :]).then_inc(std_in, 1)
            dve.wait_ge(std_out, 1)
            chain(dve.reciprocal(bn["r0"][:, :], bn["std"][:, :]))
            chain(dve.tensor_tensor(bn["t2"][:, :], bn["r0"][:, :], bn["r0"][:, :], ALU.mult))
            chain(dve.tensor_tensor(bn["t3"][:, :], bn["t2"][:, :], bn["ve"][:, :], ALU.mult))
            chain(dve.tensor_scalar(bn["mi"][:, :], bn["t3"][:, :], -0.5, 1.5, ALU.mult, ALU.add))
            chain(dve.tensor_tensor(bn["r"][:, :], bn["r0"][:, :], bn["mi"][:, :], ALU.mult))
            chain(dve.tensor_tensor(bn["inv"][:, :], bn["r"][:, :], bn["gamma"][:, :], ALU.mult))
            chain(dve.tensor_tensor(bn["std"][:, :], bn["inv"][:, :], bn["mean"][:, :], ALU.mult))
            chain(dve.tensor_tensor(bn["shift"][:, :], bn["beta"][:, :], bn["std"][:, :], ALU.subtract))
            for o in range(CT):
                last = dve.tensor_scalar(prs[:, o, :], pr_raw[:, o, :], bn["inv"][:, o:o + 1], None, ALU.mult)
            last.then_inc(ready, 1)
            chain(dve.memset(pick[:, :, :, :], 0.0))
            heads = K["gmask"][:, :].rearrange("p (h c) -> p h c", c=D)[:, :, 0]
            for t in range(2):
                for r in range(4):
                    last = dve.tensor_copy(pick[:, t, r, HT * t:HT * t + HT], heads)
            last.then_inc(ready, 1)
            dve.wait_ge(ready, 2)
            for n in range(2 * B):
                b, t = n // 2, n % 2
                at_least(dve, turned, KT + 1 + 2 * (n - 1))
                dve.tensor_scalar(ks_all[:, b, t, :], pick[:, t, 0, :], K["vk"][:, b, t, P:VW], None, ALU.mult)
                dve.tensor_tensor(vkm[:, n % 2, :], K["vk"][:, b, t, 0:P], K["gmask"][:, :], ALU.mult).then_inc(link_vk, 1)

            def reciprocals(g, hb):
                dve.wait_ge(den_full, g + 1)
                at_least(dve, bc_full, CH * (g - 1))
                dve.tensor_scalar(rec[hb][:, :], den_ps[:, :], ATT_EPS, None, ALU.add).then_inc(den_taken, 1)
                dve.wait_ge(den_taken, g + 1)
                dve.reciprocal(rec[hb][:, :], rec[hb][:, :]).then_inc(rec_ready, 1)
                dve.wait_ge(rec_ready, g + 1)

            def add(g, hb, par, c):
                dve.wait_ge(z_full, CH * g + c + 1)
                py, px = 2 * hb + c // 2, 2 * (c % 2)
                for o in range(CT):
                    img = x1[par][:, o, :].rearrange("p (y py x px) -> p py px y x", py=4, x=NB, px=4)[:, py, px:px + 2, :, :]
                    dve.tensor_tensor(img, z_ps[:, c % 2, o, :].rearrange("p (a y x) -> p a y x", a=2, x=NB), img,
                                      ALU.add).then_inc(z_taken, 1)

            reciprocals(0, 0)

            def body(i, last_body):
                for par in range(2):
                    b = 2 * i + par
                    for hb in range(2):
                        g = 2 * b + hb
                        for c in range(CH):
                            dve.wait_ge(bc_full, CH * g + c + 1)
                            for t in range(2):
                                last = dve.tensor_tensor(qr[hb][:, t, c, :], qr[hb][:, t, c, :], bc_ps[:, t, :], ALU.mult)
                            last.then_inc(q_scaled, 1)
                            if c == 0 and hb == 0:
                                dve.wait_ge(x_shifted, b + 1)
                            if c >= 1:
                                add(g, hb, par, c - 1)
                            if c == 2 and not (last_body and par == 1 and hb == 1):
                                reciprocals(g + 1, 1 - hb)
                        add(g, hb, par, CH - 1)
            over_image_pairs(dve, body)


def build(nc, a, out, scratch):
    with ExitStack() as ctx:
        K = {}
        two_phases = ctx.enter_context(ExitStack())
        make_constants(nc, ctx, two_phases, K)
        window_mixing(nc, K, a["x"], a["L0_conv_w"], a["L0_conv_b"], a["L1_conv_w_qkv"], scratch["x1"])
        projections(nc, K, scratch["x1"], scratch["qkv"])
        two_phases.close()
        convolved_heads(nc, K, a["L1_conv_w_dw"], a["L1_conv_w_pw"], scratch["taps"], scratch["qkv"], scratch["att"])
        output(nc, K, a["L1_conv_w_proj"], a["L1_conv_bn_gamma"], a["L1_conv_bn_beta"], a["L1_conv_bn_mean"],
               a["L1_conv_bn_var"], scratch["x1"], scratch["qkv"], scratch["att"], out.rearrange("b c h w -> b c (h w)"))



_INS = ["x", "L0_conv_w", "L0_conv_b", "L1_conv_w_qkv", "L1_conv_w_dw", "L1_conv_w_pw", "L1_conv_w_proj",
        "L1_conv_bn_gamma", "L1_conv_bn_beta", "L1_conv_bn_mean", "L1_conv_bn_var"]


def kernel(**inputs):
    import numpy as np
    import concourse.bacc as bacc
    from concourse.bass_utils import run_bass_kernel_spmd

    nc = bacc.Bacc("TRN2", target_bir_lowering=False, num_devices=1)
    arrays, aps = {}, {}
    for name in _INS:
        arr = np.ascontiguousarray(inputs[name])
        arrays[f"in_{name}"] = arr
        aps[name] = nc.dram_tensor(f"in_{name}", arr.shape, mybir.dt.from_np(arr.dtype), kind="ExternalInput").ap()
    out = nc.dram_tensor("out_0", (B, C, H, W), F32, kind="ExternalOutput").ap()
    scratch = {
        "x1": nc.dram_tensor("x1_scratch", (B, C, H * W), F32, kind="Internal").ap(),
        "qkv": nc.dram_tensor("qkv_scratch", (3 * C, NPH, B, PN), F32, kind="Internal").ap(),
        "att": nc.dram_tensor("att_scratch", (C, NPH, B, POS), F32, kind="Internal").ap(),
        "taps": nc.dram_tensor("tap_scratch", (QT, P, NPH, TAP * TAP), F32, kind="Internal").ap(),
    }
    build(nc, aps, out, scratch)
    r = run_bass_kernel_spmd(nc, [arrays], core_ids=[0])
    return r.results[0]["out_0"]
```

```python
from contextlib import ExitStack

import concourse.bass as bass
from concourse import mybir

F32 = mybir.dt.float32
F32R = mybir.dt.float32r
ALU = mybir.AluOpType
ACT = mybir.ActivationFunctionType
AX = mybir.AxisListType

P = 128
B, C, H, W = 8, 256, 64, 64
CT = C // P
GN_CH = 8
GN_EPS = 1e-5
WS, SHIFT, MIX_HEADS = 8, 4, 16
MIX_CH = C // MIX_HEADS
WIN_ROWS = (H + WS) // WS
PAIRS = (W + WS + 15) // 16
PAD_W = PAIRS * 16
WR = 3
GROUPS = WIN_ROWS // WR
GP = WR * PAIRS
FILLS = (GP + 1) // 2
D = 8
AH = 32
HT = P // D
QT = 6
NB = 16
PBK = NB + 1
PN = PBK * PBK
NPH = 16
POS = NB * NB
TAP = 8
BN_EPS = 1e-5
ATT_EPS = 1e-15
KT = 4
VW = P + 1


def at_least(eng, sem, value):
    if isinstance(value, int) and value <= 0:
        return
    eng.wait_ge(sem, value)


class Own:

    def __init__(self, eng, start):
        self.eng, self.start = eng, start

    def wait_ge(self, sem, value):
        if not isinstance(value, int):
            self.eng.wait_ge(self.start, 1)
        self.eng.wait_ge(sem, value)


def over_image_pairs(eng, body):
    body(0, False)
    with eng.Fori(1, B // 2 - 1) as i:
        body(i, False)
    body(B // 2 - 1, True)


class Chain:

    def __init__(self, eng, sem):
        self.eng, self.sem, self.base, self.n = eng, sem, 0, 0

    def __call__(self, ins):
        self.n += 1
        ins.then_inc(self.sem, 1)
        self.eng.wait_ge(self.sem, self.base + self.n)


def norm_moments(dve, bst, x, pieces):
    for ct, k in pieces:
        last = dve.bn_stats(bst[:, ct, k, :], x[:, ct, 512 * k:512 * k + 512])
    return last


def norm_scale(dve, chain, b, T, mv, bst, stat_ps, sem):
    def moments():
        for ct in range(CT):
            last = dve.bn_aggr(mv[:, ct, :], bst[:, ct, :, :].rearrange("p a s -> p (a s)"))
        last.then_inc(sem["moments"], 1)

    def centre():
        chain.base, chain.n = NORM_CHAIN * b, 0
        dve.wait_ge(sem["group_sum"], 2 * b + 1)
        chain(dve.tensor_tensor(T["dm"][:, :], mv[:, :, 0], stat_ps[:, 0:2], ALU.subtract))
        chain(dve.tensor_tensor(T["sq"][:, :], T["dm"][:, :], T["dm"][:, :], ALU.mult))
        dve.tensor_tensor(T["vc"][:, :], T["sq"][:, :], mv[:, :, 1], ALU.add).then_inc(sem["moments"], 1)

    def variance():
        dve.wait_ge(sem["group_sum"], 2 * b + 2)
        dve.tensor_scalar(T["ve"][:, :], stat_ps[:, 2:4], GN_EPS, None, ALU.add).then_inc(sem["var"], 1)

    def scale():
        dve.wait_ge(sem["std"], b + 1)
        chain(dve.reciprocal(T["r0"][:, :], T["std"][:, :]))
        chain(dve.tensor_tensor(T["t1"][:, :], T["r0"][:, :], T["r0"][:, :], ALU.mult))
        chain(dve.tensor_tensor(T["t2"][:, :], T["t1"][:, :], T["ve"][:, :], ALU.mult))
        chain(dve.tensor_scalar(T["t3"][:, :], T["t2"][:, :], -0.5, 1.5, ALU.mult, ALU.add))
        at_least(dve, sem["scaled"], b)
        chain(dve.tensor_tensor(T["sc"][:, :], T["r0"][:, :], T["t3"][:, :], ALU.mult))
        dve.scalar_tensor_tensor(T["nb"][:, :], stat_ps[:, 0:2], -1.0, T["sc"][:, :], ALU.mult,
                                 ALU.mult).then_inc(sem["scale"], 1)
    return moments, centre, variance, scale


NORM_CHAIN = 7
CONST_STEPS = 7 + NPH


def norm_group_sums(pe, b, T, mv, stat_ps, gavg, sem):
    def means():
        pe.wait_ge(sem["moments"], 2 * b + 1)
        pe.matmul(stat_ps[:, 0:2], gavg[:, :], mv[:, :, 0], start=True, stop=True).then_inc(sem["group_sum"], 1)

    def variances():
        pe.wait_ge(sem["moments"], 2 * b + 2)
        pe.matmul(stat_ps[:, 2:4], gavg[:, :], T["vc"][:, :], start=True, stop=True).then_inc(sem["group_sum"], 1)
    return means, variances


def norm_std(act, b, T, sem):
    act.wait_ge(sem["var"], b + 1)
    act.activation(T["std"][:, :], T["ve"][:, :], ACT.Sqrt).then_inc(sem["std"], 1)


def norm_tiles(sb, sem_of, tag):
    T = {n: sb(f"{tag}_{n}", [P, CT], F32) for n in
         ("dm", "sq", "vc", "ve", "std", "r0", "t1", "t2", "t3", "sc", "nb", "used")}
    sem = {n: sem_of(f"{tag}_{n}") for n in ("moments", "group_sum", "var", "std", "scale", "scaled", "chain")}
    return T, sem


def make_constants(nc, ctx, two_phases, K):
    def sb(name, shape, dt=F32):
        return ctx.enter_context(nc.sbuf_tensor(name, shape, dt))
    K["ident"] = sb("ident", [P, P])
    K["gmask"] = sb("gmask", [P, P])
    K["gavg"] = sb("gavg", [P, P])
    K["same_ch"] = sb("same_ch", [P, P])
    K["vk"] = sb("vk_table", [P, KT, B, D + 1])
    K["x_stored"] = [[ctx.enter_context(nc.semaphore(f"x_stored{i}_{g}")) for g in range(GROUPS)] for i in range(2)]
    K["taps_out"] = ctx.enter_context(nc.semaphore("taps_out"))
    K["taps_sorted"] = ctx.enter_context(nc.semaphore("taps_sorted"))
    K["pw_raw"] = sb("pw_raw", [P, QT, D])
    K["bn"] = {n: sb(f"bn_{n}", [P, CT]) for n in ("gamma", "beta", "mean", "var", "ve", "std", "r0", "t1", "t2", "t3",
                                                   "r", "inv", "mi", "shift")}
    K["pw_loaded"], K["bn_loaded"] = (ctx.enter_context(nc.semaphore(n)) for n in ("pw_loaded", "bn_loaded"))
    K["qkv_stored"] = [ctx.enter_context(nc.semaphore(f"qkv_stored{i}")) for i in range(4)]
    K["wq_loaded"] = ctx.enter_context(nc.semaphore("wq_loaded"))
    K["p_mv"] = sb("pmv", [P, CT, 2])
    K["p_norm"] = norm_tiles(sb, lambda name: ctx.enter_context(nc.semaphore(name)), "p")
    K["images"] = [two_phases.enter_context(nc.sbuf_tensor(f"image{i}", [P, CT, H * W], F32)) for i in range(2)]
    K["w_qkv"] = two_phases.enter_context(nc.sbuf_tensor("wq_raw", [P, QT, C], F32))
    done = K["const_done"] = ctx.enter_context(nc.semaphore("const_done"))

    def fill(pool):
        n = 0

        def step(ins):
            nonlocal n
            n += 1
            ins.then_inc(done, 1)
            pool.wait_ge(done, n)
        step(pool.memset(K["ident"][:, :], 0.0))
        step(pool.affine_select(out=K["ident"][:, :], in_=K["ident"][:, :], compare_op=ALU.not_equal,
                                fill=1.0, base=0, pattern=[[-1, P]], channel_multiplier=1))
        step(pool.memset(K["gmask"][:, :], 1.0))
        g = K["gmask"][:, :].rearrange("p (a c) -> p a c", c=GN_CH)
        step(pool.affine_select(out=g, in_=g, compare_op=ALU.is_ge, fill=0.0, base=0,
                                pattern=[[-GN_CH, P // GN_CH], [0, GN_CH]], channel_multiplier=1))
        step(pool.affine_select(out=g, in_=g, compare_op=ALU.is_ge, fill=0.0, base=GN_CH - 1,
                                pattern=[[GN_CH, P // GN_CH], [0, GN_CH]], channel_multiplier=-1))
        step(pool.tensor_scalar(K["gavg"][:, :], K["gmask"][:, :], 1.0 / GN_CH, None, ALU.mult))
        step(pool.memset(K["same_ch"][:, :], 0.0))
        s = K["same_ch"][:, :].rearrange("p (a c) -> p a c", c=D)
        for m in range(NPH):
            step(pool.affine_select(out=s, in_=s, compare_op=ALU.not_equal, fill=1.0, base=-D * m,
                                    pattern=[[0, NPH], [-1, D]], channel_multiplier=1))
    K["fill"] = fill


def window_mixing(nc, K, x_in, w_mix, b_mix, w_qkv, w_dw, x1_dram, taps_dram):
    with ExitStack() as ctx:
        def sb(name, shape, dt=F32):
            return ctx.enter_context(nc.sbuf_tensor(name, shape, dt))

        def psum(name, shape):
            return ctx.enter_context(nc.psum_tensor(name, shape, F32))

        def sem(name):
            return ctx.enter_context(nc.semaphore(name))

        x = K["images"]
        xpad = sb("xpad", [P, CT, PAIRS, H + WS, 16])
        xT = sb("xT", [P, 2, GP, C])
        yT = sb("yT", [P, 2, GP, C])
        w_raw = sb("w_raw", [P, MIX_HEADS, P])
        wT = sb("wT", [P, MIX_HEADS, P])
        b_raw = sb("b_raw", [MIX_HEADS, WS * WS])
        b_wide = sb("b_wide", [MIX_HEADS, P])
        w_in = sb("w_in", [P, MIX_HEADS, WS * WS])
        dw = sb("dw", [P, QT, 25])
        flip = sb("flip", [P, 25])
        shifted = sb("shifted", [P, NPH, TAP * TAP])
        side = sb("side", [P, 2])
        bias = sb("mix_bias", [P, MIX_HEADS])
        bst = sb("mbst", [P, CT, 8, 6])
        mv = sb("mmv", [P, CT, 2])
        T, ns = norm_tiles(sb, sem, "m")

        def norm_of(b):
            if isinstance(b, int) and b == B:
                return 0, K["p_norm"][0], K["p_mv"], K["p_norm"][1]
            return b, T, mv, ns

        t_ps = psum("t_ps", [P, 3, 512])
        m_ps = psum("m_ps", [P, 2, 512])
        k_ps = psum("k_ps", [P, 3, 512])
        stat_ps = t_ps[:, 2, 0:4]

        w_loaded, w_zero, b_loaded, b_ready = sem("w_loaded"), sem("w_zero"), sem("b_loaded"), sem("b_ready")
        b_turned = sem("b_turned")
        w_turned, w_ready = sem("w_turned"), sem("w_ready")
        pad_zero = sem("pad_zero")
        dw_loaded, dw_laid, taps_out = sem("dw_loaded"), sem("dw_laid"), K["taps_out"]
        LOAD_ROWS = ((0, 16), (16, 40), (40, 64))
        STORE_ROWS = ((0, 20), (20, 44), (44, 64))
        x_loaded = [[sem(f"x_loaded{i}_{g}") for g in range(GROUPS)] for i in range(2)]
        x_stored = K["x_stored"]
        t_full, t_taken = sem("t_full"), sem("t_taken")
        m_full, m_taken = sem("m_full"), sem("m_taken")
        k_full, k_taken = sem("k_full"), sem("k_taken")
        xn_ready = sem("xn_ready")
        counted = sem("m_counted")
        N_T, N_M, N_K = GROUPS * FILLS, GROUPS * MIX_HEADS // 2, 3 * WIN_ROWS

        def load_matrices(eng, w):
            for r in range(WS):
                p0 = 16 * r + 8 * w
                eng.dma_start(w_in[p0:p0 + 8, :, :], w_mix[:, 8 * r:8 * r + 8, :].rearrange("h i j -> i h j"))\
                    .then_inc(w_loaded, 16)

        block = ctx.enter_context(nc.Block())

        @block.sync
        def _(sp):
            load_matrices(sp, 0)
            sp.dma_start(b_raw[:, :], b_mix[:, :]).then_inc(b_loaded, 16)
            for t in range(QT):
                src = w_qkv.rearrange("(h k c) i -> k h c i", k=3, c=D)[t // 2, HT * (t % 2):HT * (t % 2) + HT, :, :]
                sp.dma_start(K["w_qkv"][:, t, :], src).then_inc(K["wq_loaded"], 16)
                rows = w_dw.rearrange("(h k c) i y x -> k h c (i y x)", k=3, c=D)[t // 2, HT * (t % 2):HT * (t % 2) + HT, :, :]
                sp.dma_start(dw[:, t, :], rows).then_inc(dw_loaded, 16)

            def body(i, last):
                for par in range(2):
                    b = 2 * i + par
                    for g in range(GROUPS):
                        y0, y1 = STORE_ROWS[g]
                        sp.wait_ge(k_taken, N_K * b + 3 * WR * (g + 1))
                        sp.dma_start(x1_dram[b, :, W * y0:W * y1].rearrange("(t p) n -> p t n", p=P),
                                     x[par][:, :, W * y0:W * y1]).then_inc(x_stored[par][g], 16)
            over_image_pairs(sp, body)

        @block.gpsimd
        def _(pool):
            def load(b, i, par):
                for g in range(GROUPS):
                    y0, y1 = LOAD_ROWS[g]
                    at_least(pool, x_stored[par][g], 16 * i)
                    pool.dma_start(x[par][:, :, W * y0:W * y1],
                                   x_in[b, :, :, :].rearrange("(t p) h w -> p t (h w)", p=P)[:, :, W * y0:W * y1])\
                        .then_inc(x_loaded[par][g], 16)

            load(0, 0, 0)
            K["fill"](pool)
            load(1, 0, 1)
            pool.memset(xpad[:, :, :, :, :], 0.0).then_inc(pad_zero, 1)

            def lay_out(t):
                at_least(pool, taps_out, 16 * t)
                for k in range(25):
                    last = pool.tensor_copy(flip[:, k:k + 1], dw[:, t, 24 - k:25 - k])
                last.then_inc(dw_laid, 1)
                pool.wait_ge(dw_laid, 2 * t + 2)
                fl = flip[:, :].rearrange("p (y x) -> p y x", x=5)
                for p in range(NPH):
                    py, px = p // 4, p % 4
                    grid = shifted[:, p, :].rearrange("p (d u q) -> p d u q", d=2, q=4)
                    pool.tensor_copy(grid[:, 0, py:py + 5, px:4], fl[:, :, 0:4 - px])
                    last = pool.tensor_copy(grid[:, 1, py:py + 5, 0:px + 1], fl[:, :, 4 - px:5])
                last.then_inc(dw_laid, 1)
                pool.wait_ge(dw_laid, 2 * t + 3)
                pool.dma_start(taps_dram[t, :, :, :], shifted[:, :, :]).then_inc(taps_out, 16)

            pool.memset(shifted[:, :, :], 0.0).then_inc(dw_laid, 1)
            pool.wait_ge(dw_loaded, 16 * QT)
            for par in range(2):
                for t in range(QT // 2 * par, QT // 2 * (par + 1)):
                    lay_out(t)
                load(2 + par, 1, par)

            def body(i, last):
                for par in range(2):
                    load(2 * i + par, i, par)
            with pool.Fori(2, B // 2) as i:
                body(i, False)

        @block.scalar
        def _(act):
            load_matrices(act, 1)
            act.wait_ge(b_loaded, 16)
            act.activation(b_wide[:, :].rearrange("h (r w c) -> h r w c", w=2, c=8),
                           b_raw[:, :].rearrange("h (r c) -> h r c", c=8).unsqueeze(2).broadcast_to([MIX_HEADS, WS, 2, WS]),
                           ACT.Copy).then_inc(b_ready, 1)
            act.wait_ge(b_turned, 1)
            act.activation(bias[:, :], k_ps[:, 0, 0:MIX_HEADS], ACT.Copy).then_inc(b_ready, 1)
            for f in range(MIX_HEADS // 4):
                act.wait_ge(w_turned, f + 1)
                act.activation(wT[:, 4 * f:4 * f + 4, :].rearrange("p h m -> p (h m)"), (t_ps, m_ps)[f // 2][:, f % 2, :],
                               ACT.Copy).then_inc(w_ready, 1)

            def normalise(b, par):
                act.wait_ge(ns["scale"], b + 1)
                at_least(act, t_full, N_T * b)
                for ct in range(CT):
                    for q0, q1, c0, c1 in ((0, 1, SHIFT, 16), (1, PAIRS - 1, 0, 16), (PAIRS - 1, PAIRS, 0, SHIFT)):
                        x0 = 16 * q0 + c0 - SHIFT
                        cols = (q1 - q0) * (c1 - c0)
                        src = x[par][:, ct, :].rearrange("p (h w) -> p h w", w=W)[:, :, x0:x0 + cols]\
                            .rearrange("p h (q c) -> p h q c", q=q1 - q0)
                        dst = xpad[:, ct, q0:q1, SHIFT:SHIFT + H, c0:c1].rearrange("p q h c -> p h q c")
                        last = act.activation(dst, src, ACT.Identity, bias=T["nb"][:, ct:ct + 1],
                                              scale=T["sc"][:, ct:ct + 1])
                last.then_inc(xn_ready, 1)
                act.wait_ge(xn_ready, b + 1)
                act.activation(T["used"][:, 0:1], T["sc"][:, 0:1], ACT.Copy).then_inc(ns["scaled"], 1)

            norm_std(act, 0, T, ns)
            act.wait_ge(pad_zero, 1)
            normalise(0, 0)

            def body(i, last_body):
                for par in range(2):
                    b = 2 * i + par
                    for g in range(GROUPS):
                        at_least(act, m_full, N_M * b + (MIX_HEADS // 2) * (g - 1))
                        for f in range(FILLS):
                            n = FILLS * g + f
                            np_ = min(2, GP - 2 * f)
                            act.wait_ge(t_full, N_T * b + n + 1)
                            act.activation(xT[:, (g + par) % 2, 2 * f:2 * f + np_, :].rearrange("p a c -> p (a c)"),
                                           t_ps[:, n % 3, 0:np_ * C], ACT.Copy).then_inc(t_taken, 1)
                    image, Tn, _, nsn = norm_of(b + 1)
                    norm_std(act, image, Tn, nsn)
                    if not (last_body and par == 1):
                        normalise(b + 1, 1 - par)
            over_image_pairs(act, body)

        @block.tensor
        def _(pe):
            pe.wait_ge(b_ready, 1)
            pe.wait_ge(K["const_done"], CONST_STEPS)
            pe.transpose(k_ps[:, 0, 0:MIX_HEADS], b_wide[:, :], K["ident"][0:MIX_HEADS, 0:MIX_HEADS]).then_inc(b_turned, 1)
            pe.wait_ge(w_zero, 3)
            for f in range(MIX_HEADS // 4):
                for j in range(4):
                    last = pe.transpose((t_ps, m_ps)[f // 2][:, f % 2, P * j:P * j + P], w_raw[:, 4 * f + j, :],
                                        K["ident"][:, :])
                last.then_inc(w_turned, 1)
            for link in norm_group_sums(pe, 0, T, mv, stat_ps, K["gavg"], ns):
                link()
            pe.wait_ge(w_ready, MIX_HEADS // 4)

            def turn(b, g):
                for f in range(FILLS):
                    n = FILLS * g + f
                    at_least(pe, t_taken, N_T * b + n - 2)
                    for a in range(2 * f, min(2 * f + 2, GP)):
                        wy, q = WR * g + a // PAIRS, a % PAIRS
                        for ct in range(CT):
                            o = (a - 2 * f) * C + ct * P
                            last = pe.transpose(t_ps[:, n % 3, o:o + P],
                                                xpad[:, ct, q, WS * wy:WS * wy + WS, :].rearrange("p r c -> p (r c)"), K["ident"][:, :])
                    last.then_inc(t_full, 1)

            def mix(b, g, par, between={}):
                for hp in range(MIX_HEADS // 2):
                    if hp in between:
                        between[hp]()
                    n = (MIX_HEADS // 2) * g + hp
                    if hp == 0:
                        pe.wait_ge(t_taken, N_T * b + FILLS * (g + 1))
                    at_least(pe, m_taken, N_M * b + n - 1)
                    for j in range(2):
                        h = 2 * hp + j
                        last = pe.matmul(m_ps[:, n % 2, j * GP * MIX_CH:(j + 1) * GP * MIX_CH], wT[:, h, :],
                                         xT[:, (g + par) % 2, :, MIX_CH * h:MIX_CH * h + MIX_CH],
                                         start=True, stop=True)
                    last.then_inc(m_full, 1)

            def turn_back(b, g, par, r):
                wy = WR * g + r
                pe.wait_ge(m_taken, N_M * b + (MIX_HEADS // 2) * (g + 1))
                for u in range(3):
                    at_least(pe, k_taken, N_K * b + 3 * wy + u - 2)
                    for q, ct in ([(q, u) for q in range(4)] if u < CT else [(4, 0), (4, 1)]):
                        o = P * q if u < CT else P * ct
                        last = pe.transpose(k_ps[:, u, o:o + P], yT[:, (g + par) % 2, PAIRS * r + q, P * ct:P * ct + P],
                                            K["ident"][:, :])
                    last.then_inc(k_full, 1)

            def body(i, last_body):
                for par in range(2):
                    b = 2 * i + par
                    pe.wait_ge(xn_ready, b + 1)
                    turn(b, 0)
                    turn(b, 1)
                    mix(b, 0, par)
                    turn(b, 2)
                    rows = {3 + 2 * r: (lambda r=r: turn_back(b, 0, par, r)) for r in range(WR)}
                    image, Tn, mvn, nsn = norm_of(b + 1)
                    means, variances = norm_group_sums(pe, image, Tn, mvn, stat_ps, K["gavg"], nsn)

                    def means_after_pairs():
                        pe.wait_ge(t_taken, N_T * (b + 1))
                        means()
                    rows.update({2: means_after_pairs, 4: variances})
                    mix(b, 1, par, rows)
                    mix(b, 2, par, {2 + 2 * r: (lambda r=r: turn_back(b, 1, par, r)) for r in range(WR)})
                    for r in range(WR):
                        turn_back(b, 2, par, r)
            over_image_pairs(pe, body)

        @block.vector
        def _(dve):
            chain = Chain(dve, ns["chain"])

            PIECES = [[(ct, k) for ct in range(CT) for k in range(W * y0 // 512, W * y1 // 512)] for y0, y1 in LOAD_ROWS]

            def moments(b, par, i, g, parts=None):
                if (parts is None or parts[0] == 0) and not (isinstance(b, int) and b == B):
                    dve.wait_ge(x_loaded[par][g], 16 * (i + 1))
                pieces = PIECES[g] if parts is None else [PIECES[g][k] for k in parts]
                last = norm_moments(dve, bst, x[par], pieces)
                if pieces[-1] == PIECES[g][-1]:
                    last.then_inc(counted, 1)
                if g == GROUPS - 1:
                    dve.wait_ge(counted, GROUPS * (b + 1))
                    dve.tensor_copy(T["t1"][:, 0:1], K["ident"][:, 0:1])

            moments(0, 0, 0, 0)
            moments(0, 0, 0, 1)
            dve.wait_ge(K["const_done"], CONST_STEPS)
            dve.tensor_reduce(side[:, :], K["gmask"][:, :].rearrange("p (a w c) -> p w a c", w=2, c=8)[:, :, :, 0],
                              AX.X, ALU.add).then_inc(w_zero, 1)
            dve.wait_ge(w_zero, 1)
            dve.wait_ge(w_loaded, 16 * 2 * WS)
            for w in range(2):
                dve.tensor_scalar(w_raw[:, :, :].rearrange("p h (r w c) -> p h r w c", w=2, c=8)[:, :, :, w, :],
                                  w_in[:, :, :].rearrange("p h (r c) -> p h r c", c=8), side[:, w:w + 1], None,
                                  ALU.mult).then_inc(w_zero, 1)
            moments(0, 0, 0, 2)
            for link in norm_scale(dve, chain, 0, T, mv, bst, stat_ps, ns):
                link()
            dve.wait_ge(b_ready, 2)

            def add_bias(b, g, par, between={}):
                for hp in range(MIX_HEADS // 2):
                    if hp in between:
                        between[hp]()
                    n = (MIX_HEADS // 2) * g + hp
                    if hp == 0:
                        at_least(dve, k_full, N_K * b + 3 * WR * (g - 1))
                    dve.wait_ge(m_full, N_M * b + n + 1)
                    c0 = 2 * hp * MIX_CH
                    out = yT[:, (g + par) % 2, :, c0:c0 + 2 * MIX_CH].rearrange("p a (h c) -> p h a c", h=2)
                    src = m_ps[:, n % 2, 0:2 * GP * MIX_CH].rearrange("p (h a c) -> p h a c", h=2, c=MIX_CH)
                    bb = bias[:, 2 * hp:2 * hp + 2].unsqueeze(2).unsqueeze(3).broadcast_to([P, 2, GP, MIX_CH])
                    dve.tensor_tensor(out, src, bb, ALU.add).then_inc(m_taken, 1)

            def add_row(b, g, par, r):
                img = x[par][:, :, :].rearrange("p t (h w) -> p t h w", w=W)
                wy = WR * g + r
                r0, r1 = max(0, SHIFT - WS * wy), min(WS, H + SHIFT - WS * wy)
                y0 = WS * wy + r0 - SHIFT
                y1 = y0 + r1 - r0
                if wy == 0:
                    dve.wait_ge(xn_ready, b + 1)
                for u in range(3):
                    dve.wait_ge(k_full, N_K * b + 3 * wy + u + 1)
                    if u < CT:
                        quad = k_ps[:, u, :].rearrange("p (q r c) -> p r q c", q=4, c=16)
                        left = img[:, u, y0:y1, 0:12]
                        dve.tensor_tensor(left, left, quad[:, r0:r1, 0, SHIFT:16], ALU.add)
                        mid = img[:, u, y0:y1, 12:60].rearrange("p r (q c) -> p r q c", c=16)
                        last = dve.tensor_tensor(mid, mid, quad[:, r0:r1, 1:4, :], ALU.add)
                    else:
                        right = img[:, :, y0:y1, 60:64]
                        edge = k_ps[:, u, 0:CT * P].rearrange("p (t r c) -> p t r c", t=CT, c=16)
                        last = dve.tensor_tensor(right, right, edge[:, :, r0:r1, 0:SHIFT], ALU.add)
                    last.then_inc(k_taken, 1)

            def body(i, last_body):
                for par in range(2):
                    b = 2 * i + par
                    npar, ni = (1, i) if par == 0 else (0, i + 1)
                    moments(b + 1, npar, ni, 0)
                    add_bias(b, 0, par, {2 + k: (lambda k=k: moments(b + 1, npar, ni, 1, [k])) for k in range(6)})
                    moments(b + 1, npar, ni, 2)
                    image, Tn, mvn, nsn = norm_of(b + 1)
                    start, centre, variance, scale = norm_scale(dve, Chain(dve, nsn["chain"]), image, Tn, mvn, bst, stat_ps, nsn)
                    start()
                    between = {2: centre, 4: variance, 6: scale}
                    between.update({3 + 2 * r: (lambda r=r: add_row(b, 0, par, r)) for r in range(WR)})
                    add_bias(b, 1, par, between)
                    add_bias(b, 2, par, {2 + 2 * r: (lambda r=r: add_row(b, 1, par, r)) for r in range(WR)})
                    for r in range(WR):
                        add_row(b, 2, par, r)
            over_image_pairs(dve, body)


def projections(nc, K, x1_dram, qkv_dram, w_pw, bn_in, taps_dram, sorted_dram):
    with ExitStack() as ctx:
        def sb(name, shape, dt=F32):
            return ctx.enter_context(nc.sbuf_tensor(name, shape, dt))

        def psum(name, shape):
            return ctx.enter_context(nc.psum_tensor(name, shape, F32))

        def sem(name):
            return ctx.enter_context(nc.semaphore(name))

        NCH = 8
        TILES = (2, 4, 3, 5, 0, 1)
        x1 = K["images"]
        xn = sb("xn", [P, 2, CT, 512])
        xh = sb("xh", [P, 2, CT, 512], F32R)
        xl = sb("xl", [P, 2, CT, 512], F32R)
        w_raw = K["w_qkv"]
        wh = sb("wqh", [P, CT, QT * P], F32R)
        wl = sb("wql", [P, CT, QT * P], F32R)
        stage = sb("stage", [P, 4, QT, 2, PN])
        kv = sb("kv", [P, 2, 4, 512])
        kT = sb("kT", [P, 2, 4, P])
        vT = sb("vT", [P, 2, 4, VW])
        tick = sb("ptick", [P, 4])
        diag = sb("pdiag", [P, 2, P])
        bst = sb("pbst", [P, CT, 8, 6])
        mv = K["p_mv"]
        T, ns = K["p_norm"]

        o_ps = psum("o_ps", [P, 3, 512])
        t_ps = psum("pt_ps", [P, 2, 512])
        vk_ps = psum("vk_ps", [P, 2, 512])
        stat_ps = psum("pstat_ps", [P, 4])

        w_loaded, w_turned, w_split = K["wq_loaded"], sem("wq_turned"), sem("wq_split")
        zeroed = sem("zeroed")
        x_loaded = [sem(f"x1_loaded{i}") for i in range(2)]
        xn_ready, x_free = sem("pxn_ready"), sem("px_free")
        xh_ready, xl_ready = sem("xh_ready"), sem("xl_ready")
        o_full = sem("o_full")
        kv_ready, q_ready = sem("kv_ready"), sem("q_ready")
        kv_ready_v, q_ready_v = sem("kv_ready_v"), sem("q_ready_v")
        staged = sem("staged")
        t_full, k_turned, v_turned = sem("pt_full"), sem("k_turned"), sem("v_turned")
        vk_full, vk_taken = sem("vk_full"), sem("vk_taken")
        stored = K["qkv_stored"]
        counted = sem("p_counted")

        def place(n):
            return 2 * (n // 4) + n % 2

        def image(i, par):
            if isinstance(i, int) and i == 0:
                return B - 2 + par
            return 2 * i + par - 2

        def uses(n):
            return sum(place(m) == place(n) for m in range(n))

        def inside(t, n):
            c = place(n)
            return stage[:, c, t, :, :].rearrange("p a (y x) -> p a y x", x=PBK)[:, :, c // 2:c // 2 + NB, c % 2:c % 2 + NB]

        def dense(ap):
            return ap.rearrange("p (a y x) -> p a y x", a=2, x=NB)

        block = ctx.enter_context(nc.Block())

        @block.sync
        def _(sp):
            for t in range(QT):
                rows = w_pw.rearrange("(h k o) c y x -> k h o (c y x)", k=3, o=D)[t // 2, HT * (t % 2):HT * (t % 2) + HT, :, :]
                sp.dma_start(K["pw_raw"][:, t, :], rows).then_inc(K["pw_loaded"], 16)
            with nc.allow_non_contiguous_dma(reason="256 values each"):
                for n, v in bn_in.items():
                    sp.dma_start(K["bn"][n][:, :], v.rearrange("(t p) -> p t", p=P)).then_inc(K["bn_loaded"], 16)
            sp.wait_ge(K["taps_out"], 16 * QT)
            for p in range(NPH):
                src = taps_dram.rearrange("t (h c) p n -> p c (t h) n", c=D)[p, :, :, :]
                sp.dma_start(sorted_dram[D * p:D * p + D, :, :], src).then_inc(K["taps_sorted"], 16)
            for par in range(2):
                for g in range(GROUPS):
                    sp.wait_ge(K["x_stored"][par][g], 16 * (B // 2))
            own = Own(sp, w_loaded)

            def body(i, last):
                for par in range(2):
                    b = 2 * i + par
                    for n in range(NCH):
                        c = place(n)
                        p0 = 4 * ((n // 2 + 2) % 4) + 2 * ((n + 1) % 2)
                        own.wait_ge(staged, NCH * b + n + 1)
                        for t in (2, 4, 3, 5):
                            sp.dma_start(qkv_dram[P * t:P * t + P, p0:p0 + 2, image(i, par), :], stage[:, c, t, :, :])\
                                .then_inc(stored[c], 16)
                        own.wait_ge(q_ready, NCH * b + n + 1)
                        own.wait_ge(q_ready_v, NCH * b + n + 1)
                        for t in (0, 1):
                            sp.dma_start(qkv_dram[P * t:P * t + P, p0:p0 + 2, image(i, par), :], stage[:, c, t, :, :])\
                                .then_inc(stored[c], 16)
            over_image_pairs(sp, body)

        def stage_free(eng, b, n):
            at_least(eng, stored[place(n)], 16 * QT * (2 * b + uses(n)))

        @block.gpsimd
        def _(pool):
            pool.memset(vT[:, :, :, P:VW], 1.0).then_inc(zeroed, 1)
            pool.memset(stage[:, 0:2, :, :, :], 0.0).then_inc(zeroed, 1)
            pool.wait_ge(zeroed, 3)

            def body(i, last_body):
                for par in range(2):
                    b = 2 * i + par
                    for n in range(NCH):
                        pool.wait_ge(kv_ready, 2 * (NCH * b + n + 1))
                        pool.wait_ge(kv_ready_v, 2 * (NCH * b + n + 1))
                        stage_free(pool, b, n)
                        pool.tensor_tensor(tick[:, n % 4:n % 4 + 1], K["ident"][:, 0:1], K["ident"][:, 1:2], ALU.add)
                        for j, t in enumerate((2, 4, 3, 5)):
                            last = pool.tensor_copy(inside(t, n), dense(kv[:, n % 2, j, :]))
                        last.then_inc(staged, 1)
            over_image_pairs(pool, body)

        @block.scalar
        def _(act):
            for f in range(3):
                act.wait_ge(w_turned, f + 1)
                act.activation(wh[:, :, P * 2 * f:P * 2 * f + 2 * P], t_ps[:, f % 2, :].rearrange("p (c m) -> p c m", c=CT),
                               ACT.Copy).then_inc(w_split, 1)
                act.wait_ge(w_split, 2 * f + 2)
            def split(b, n, par):
                if n == 0:
                    act.wait_ge(ns["scale"], b + 1)
                at_least(act, xl_ready, NCH * b + n - 1)
                py, px = n // 2, 2 * (n % 2)
                for ct in range(CT):
                    src = x1[par][:, ct, :].rearrange("p (y py x px) -> p py px y x", py=4, x=NB, px=4)[:, py, px:px + 2, :, :]
                    last = act.activation(dense(xn[:, n % 2, ct, :]), src, ACT.Identity, bias=T["nb"][:, ct:ct + 1],
                                          scale=T["sc"][:, ct:ct + 1])
                last.then_inc(xn_ready, 1)
                act.wait_ge(xn_ready, NCH * b + n + 1)
                if n == NCH - 1:
                    act.activation(T["used"][:, 0:1], T["nb"][:, 0:1], ACT.Copy).then_inc(ns["scaled"], 1)
                at_least(act, o_full, QT * (NCH * b + n - 1))
                act.activation(xh[:, n % 2, :, :], xn[:, n % 2, :, :], ACT.Copy).then_inc(xh_ready, 1)

            def body(i, last_body):
                for par in range(2):
                    b = 2 * i + par
                    split(b, 0, par)
                    for n in range(NCH):
                        if n + 1 < NCH:
                            split(b, n + 1, par)
                        o0 = QT * (NCH * b + n)

                        def key(u):
                            act.wait_ge(o_full, o0 + 2 * u + 1)
                            if u == 0:
                                at_least(act, staged, NCH * b + n - 1)
                                at_least(act, t_full, 4 * (NCH * b + n - 1))
                            act.activation(kv[:, n % 2, 2 * u, :], o_ps[:, (2 * u) % 3, :], ACT.Copy).then_inc(kv_ready, 1)

                        def turned(u):
                            act.wait_ge(t_full, 4 * (NCH * b + n) + 2 * u + 1)
                            at_least(act, vk_full, NCH * b + n)
                            act.activation(kT[:, u, :, :].rearrange("p a c -> p (a c)"), t_ps[:, 0, :], ACT.Relu)\
                                .then_inc(k_turned, 1)
                        key(0)
                        key(1)
                        turned(0)
                        act.wait_ge(o_full, o0 + 5)
                        if isinstance(b, int) and b == 0 and n == 0:
                            act.wait_ge(zeroed, 3)
                        stage_free(act, b, n)
                        act.activation(inside(0, n), dense(o_ps[:, 1, :]), ACT.Copy).then_inc(q_ready, 1)
                        turned(1)
                        if n == 6 and not (last_body and par == 1):
                            norm_std(act, b + 1, T, ns)
                    if not last_body:
                        act.wait_ge(x_free, b + 1)
                        for g in range(GROUPS):
                            act.wait_ge(K["x_stored"][par][g], 16 * (B // 2))
                        act.dma_start(x1[par][:, :, :], x1_dram[b, :, :].rearrange("(t p) n -> p t n", p=P))\
                            .then_inc(x_loaded[par], 16)
            over_image_pairs(act, body)

        @block.tensor
        def _(pe):
            pe.wait_ge(w_loaded, 16 * QT)
            for f in range(3):
                at_least(pe, w_split, 2 * (f - 1))
                for ct in range(CT):
                    for j in range(2):
                        last = pe.transpose(t_ps[:, f % 2, P * (2 * ct + j):P * (2 * ct + j) + P],
                                            w_raw[:, 2 * f + j, P * ct:P * ct + P], K["ident"][:, :])
                last.then_inc(w_turned, 1)
            pe.wait_ge(w_split, 6)
            pe.wait_ge(zeroed, 3)

            def product(b, n, j):
                t = TILES[j]
                if j == 0:
                    at_least(pe, kv_ready_v, 2 * (NCH * b + n))
                    at_least(pe, q_ready, NCH * b + n)
                if j == 1:
                    at_least(pe, q_ready, NCH * b + n)
                if j == 2:
                    at_least(pe, q_ready_v, NCH * b + n)
                if j == 3:
                    pe.wait_ge(kv_ready, 2 * (NCH * b + n) + 1)
                if j == 4:
                    pe.wait_ge(kv_ready_v, 2 * (NCH * b + n) + 1)
                if j == 5:
                    pe.wait_ge(kv_ready, 2 * (NCH * b + n) + 2)
                k = 0
                for ct in range(CT):
                    for w, xx in ((wh, xh), (wl, xh), (wh, xl)):
                        last = pe.matmul(o_ps[:, j % 3, :], w[:, ct, P * t:P * t + P], xx[:, n % 2, ct, :],
                                         start=(k == 0), stop=(k == 5))
                        k += 1
                last.then_inc(o_full, 1)

            def turn(b, n, u):
                at_least(pe, k_turned, 2 * (NCH * b + n) + u)
                at_least(pe, v_turned, 2 * (NCH * b + n) + u)
                pe.wait_ge(kv_ready, 2 * (NCH * b + n) + u + 1)
                pe.wait_ge(kv_ready_v, 2 * (NCH * b + n) + u + 1)
                for s in range(2):
                    for a in range(4):
                        last = pe.transpose(t_ps[:, s, P * a:P * a + P], kv[:, n % 2, 2 * u + s, P * a:P * a + P],
                                            K["ident"][:, :])
                    last.then_inc(t_full, 1)

            def sum_vk(b, n, u):
                pe.wait_ge(k_turned, 2 * (NCH * b + n) + u + 1)
                pe.wait_ge(v_turned, 2 * (NCH * b + n) + u + 1)
                if n == 0:
                    at_least(pe, vk_taken, 2 * b)
                for a in range(4):
                    last = pe.matmul(vk_ps[:, u, 0:VW], kT[:, u, a, :], vT[:, u, a, :],
                                     start=(n == 0 and a == 0), stop=(n == NCH - 1 and a == 3))
                if u == 1:
                    last.then_inc(vk_full, 1)

            def body(i, last_body):
                for par in range(2):
                    b = 2 * i + par
                    for n in range(NCH):
                        pe.wait_ge(xh_ready, NCH * b + n + 1)
                        pe.wait_ge(xl_ready, NCH * b + n + 1)
                        for j in range(3):
                            product(b, n, j)
                        turn(b, n, 0)
                        product(b, n, 3)
                        sum_vk(b, n, 0)
                        product(b, n, 4)
                        turn(b, n, 1)
                        product(b, n, 5)
                        sum_vk(b, n, 1)
                        if n == 6 and not (last_body and par == 1):
                            for link in norm_group_sums(pe, b + 1, T, mv, stat_ps, K["gavg"], ns):
                                link()
            over_image_pairs(pe, body)

        @block.vector
        def _(dve):
            chain = Chain(dve, ns["chain"])
            for f in range(3):
                dve.wait_ge(w_split, 2 * f + 1)
                hi = wh[:, :, P * 2 * f:P * 2 * f + 2 * P]
                dve.tensor_tensor(wl[:, :, P * 2 * f:P * 2 * f + 2 * P], t_ps[:, f % 2, :].rearrange("p (c m) -> p c m", c=CT),
                                  hi.bitcast(F32), ALU.subtract).then_inc(w_split, 1)

            def moments(b, par, i, quarter):
                if quarter == 0:
                    at_least(dve, x_loaded[par], 16 * i)
                pieces = [(quarter // 2, k) for k in range(4 * (quarter % 2), 4 * (quarter % 2) + 4)]
                norm_moments(dve, bst, x1[par], pieces).then_inc(counted, 1)
                if quarter == 3:
                    dve.wait_ge(counted, 4 * b)
                    dve.tensor_copy(T["t1"][:, 0:1], K["ident"][:, 0:1])

            def scale(b):
                for link in norm_scale(dve, chain, b, T, mv, bst, stat_ps, ns):
                    link()

            dve.memset(stage[:, 2:4, :, :, :], 0.0).then_inc(zeroed, 1)
            dve.wait_ge(zeroed, 3)

            def split(b, n):
                dve.wait_ge(xh_ready, NCH * b + n + 1)
                dve.tensor_tensor(xl[:, n % 2, :, :], xn[:, n % 2, :, :], xh[:, n % 2, :, :].bitcast(F32),
                                  ALU.subtract).then_inc(xl_ready, 1)

            def body(i, last_body):
                for par in range(2):
                    b = 2 * i + par
                    nxt = not (last_body and par == 1)
                    npar, ni = (1, i) if par == 0 else (0, i + 1)
                    split(b, 0)
                    for n in range(NCH):
                        if n + 1 < NCH:
                            split(b, n + 1)
                        if n == NCH - 1:
                            dve.wait_ge(xn_ready, NCH * (b + 1))
                            dve.tensor_copy(T["t1"][:, 0:1], K["ident"][:, 0:1]).then_inc(x_free, 1)
                        o0 = QT * (NCH * b + n)
                        for u in range(2):
                            dve.wait_ge(o_full, o0 + 2 * u + 2)
                            if u == 0:
                                at_least(dve, staged, NCH * b + n - 1)
                            dve.tensor_copy(kv[:, n % 2, 2 * u + 1, :], o_ps[:, (2 * u + 1) % 3, :]).then_inc(kv_ready_v, 1)
                            dve.wait_ge(t_full, 4 * (NCH * b + n) + 2 * u + 2)
                            at_least(dve, vk_full, NCH * b + n)
                            dve.tensor_copy(vT[:, u, :, 0:P], t_ps[:, 1, :].rearrange("p (a c) -> p a c", a=4))\
                                .then_inc(v_turned, 1)
                        dve.wait_ge(o_full, o0 + 6)
                        stage_free(dve, b, n)
                        dve.tensor_copy(inside(1, n), dense(o_ps[:, 2, :])).then_inc(q_ready_v, 1)
                        if nxt and 2 <= n < 6:
                            moments(b + 1, npar, ni, n - 2)
                        if nxt and n == 6:
                            scale(b + 1)
                    dve.wait_ge(vk_full, NCH * (b + 1))
                    at = bass.ds(image(i, par), 1)
                    dve.tensor_tensor(diag[:, :, :], vk_ps[:, :, 0:P], K["gmask"][:, :].unsqueeze(1).broadcast_to([P, 2, P]),
                                      ALU.mult).then_inc(vk_taken, 1)
                    dve.tensor_copy(K["vk"][:, 0:2, at, D:D + 1], vk_ps[:, :, P:VW].unsqueeze(3)).then_inc(vk_taken, 1)
                    dve.wait_ge(vk_taken, 2 * b + 1)
                    dve.tensor_reduce(K["vk"][:, 0:2, at, 0:D], diag[:, :, :].rearrange("p t (a d) -> p t d a", d=D).unsqueeze(2),
                                      AX.X, ALU.add)
            over_image_pairs(dve, body)


def over_head_pairs(eng, body):
    body(0, False)
    with eng.Fori(1, AH // 2 - 1) as i:
        body(i, False)
    body(AH // 2 - 1, True)


def convolved_heads(nc, K, w_proj, sorted_dram, qkv_dram, yq_dram):
    with ExitStack() as ctx:
        def sb(name, shape, dt=F32):
            return ctx.enter_context(nc.sbuf_tensor(name, shape, dt))

        def psum(name, shape):
            return ctx.enter_context(nc.psum_tensor(name, shape, F32))

        def sem(name):
            return ctx.enter_context(nc.semaphore(name))

        STEPS = B // 2
        TT = TAP * TAP
        taps = sb("taps", [P, QT * HT, TT])
        pw_raw, bn = K["pw_raw"], K["bn"]
        pr_raw = sb("pr_raw", [P, CT, KT * P])
        prs = sb("prs", [P, CT, KT * P])
        pick = sb("pick", [P, KT, 2, KT * HT])
        pw_rep = sb("pw_rep", [P, QT, NPH, D])
        pw = sb("pw", [P, QT * HT, D])
        wprod = sb("wprod", [P, 3, TT, D])
        wh = [sb(f"wh{i}", [P, 3, TT * D], F32R) for i in range(2)]
        wl = [sb(f"wl{i}", [P, 3, TT * D], F32R) for i in range(2)]
        raw = [sb(f"raw{i}", [P, 3, 2 * PN]) for i in range(2)]
        dh = [sb(f"dh{i}", [P, 3, 2 * PN], F32R) for i in range(2)]
        dl = [sb(f"dl{i}", [P, 3, 2 * PN], F32R) for i in range(2)]
        qy = sb("qy", [P, 2, 512])
        ky = sb("ky", [P, 512])
        vy = sb("vy", [P, 512])
        kT = sb("ykT", [P, 4, P])
        vT = sb("yvT", [P, 4, VW])
        diag = sb("diag", [P, 2, P])
        sums = sb("sums", [P, AH, B, D + 1])

        c_ps = psum("c_ps", [P, 2, 512])
        kt_ps, vt_ps = psum("kt_ps", [P, 512]), psum("vt_ps", [P, 512])
        vk_ps = psum("yvk_ps", [P, 512])
        s_ps = psum("s_ps", [P, 2, 512])

        pw_loaded, taps_loaded = K["pw_loaded"], [sem(f"taps_loaded{i}") for i in range(2)]
        pr_loaded, std_in, std_out, bn_link = sem("pr_loaded"), sem("bn_var"), sem("bn_std"), sem("bn_chain")
        pr_scaled, pr_turned, pr_ready = sem("pr_scaled"), sem("pr_turned"), sem("pr_ready")
        init, turned, pw_ready = sem("init"), sem("pw_turned"), sem("pw_ready")
        raw_loaded = [sem(f"raw_loaded{i}") for i in range(2)]
        hi_ready, lo_ready = sem("hi_ready"), sem("lo_ready")
        w_prod, w_hi, w_lo = sem("w_prod"), sem("w_hi"), sem("w_lo")
        c_full, q_out, k_out, v_out = sem("c_full"), sem("q_out"), sem("k_out"), sem("v_out")
        kt_full, vt_full = sem("kt_full"), sem("vt_full")
        k_taken, v_taken = sem("yk_taken"), sem("yv_taken")
        vk_full, diag_ready = sem("yvk_full"), sem("diag_ready")
        summed, s_full, s_taken = sem("summed"), sem("s_full"), sem("s_taken")
        stored = [sem(f"yq_stored{i}") for i in range(2)]

        qkv_v = qkv_dram.rearrange("(k h c) p b n -> k h p c (b n)", k=3, c=D)
        yq_v = yq_dram.rearrange("(h d) p b n -> h p d (b n)", d=D)

        block = ctx.enter_context(nc.Block())

        def load_taps(eng, half):
            eng.dma_start(taps[:, :, :].rearrange("p (k a h) n -> p k a (h n)", k=3, a=2)[:, :, half, :],
                          sorted_dram.rearrange("p (k a h) n -> p k a (h n)", k=3, a=2)[:, :, half, :])\
                .then_inc(taps_loaded[half], 16)

        def steps_of(i):
            for hp in range(2):
                for j in range(STEPS):
                    yield hp, 2 * i + hp, j, 2 * STEPS * i + STEPS * hp + j

        @block.sync
        def _(sp):
            own = Own(sp, K["taps_sorted"])
            sp.wait_ge(K["taps_sorted"], 16 * NPH)
            load_taps(sp, 0)
            for c in range(4):
                sp.wait_ge(K["qkv_stored"][c], 16 * QT * 2 * B)

            def store(h, j, s):
                own.wait_ge(q_out, s + 1)
                sp.dma_start(yq_v[h, :, :, 2 * POS * j:2 * POS * j + 2 * POS], qy[:, j % 2, :]).then_inc(stored[j % 2], 16)

            def body(i, last):
                for hp, h, j, s in steps_of(i):
                    if not isinstance(s, int) or s >= 2:
                        own.wait_ge(hi_ready, s - 1)
                        own.wait_ge(lo_ready, s - 1)
                    for k in range(3):
                        sp.dma_start(raw[j % 2][:, k, :], qkv_v[k, h, :, :, 2 * PN * j:2 * PN * j + 2 * PN])\
                            .then_inc(raw_loaded[j % 2], 16)
                    if not isinstance(s, int) or s >= 3:
                        store(h if j == STEPS - 1 else h - 1, (j + 1) % STEPS, s - 3)
            over_head_pairs(sp, body)
            for j in range(1, STEPS):
                store(AH - 1, j, STEPS * (AH - 1) + j)
            for c in range(2):
                sp.wait_ge(stored[c], 16 * STEPS * AH // 2)

        @block.gpsimd
        def _(pool):
            def weights_low(h, par):
                pool.wait_ge(w_hi, h + 1)
                at_least(pool, c_full, 3 * STEPS * (h - 1))
                pool.tensor_tensor(wl[par][:, :, :], wprod[:, :, :, :].rearrange("p k a o -> p k (a o)"),
                                   wh[par][:, :, :].bitcast(F32), ALU.subtract).then_inc(w_lo, 1)

            def split(s, j):
                pool.wait_ge(hi_ready, s + 1)
                pool.tensor_tensor(dl[j % 2][:, :, :], raw[j % 2][:, :, :], dh[j % 2][:, :, :].bitcast(F32), ALU.subtract)\
                    .then_inc(lo_ready, 1)

            pool.wait_ge(raw_loaded[0], 48)
            load_taps(pool, 1)
            pool.dma_start(pr_raw[:, :, :], w_proj.rearrange("(t p) k -> p t k", p=P)).then_inc(pr_loaded, 16)
            weights_low(0, 0)
            pool.wait_ge(lo_ready, 1)

            def body(i, last):
                for hp, h, j, s in steps_of(i):
                    end = last and hp == 1
                    if not (end and j == STEPS - 1):
                        split(s + 1, j + 1)
                    if j == 2 and not end:
                        weights_low(h + 1, 1 - hp)
            over_head_pairs(pool, body)

        @block.scalar
        def _(act):
            act.wait_ge(pw_loaded, 16 * QT)
            act.activation(pw_rep[:, :, :, :], pw_raw[:, :, :].unsqueeze(2).broadcast_to([P, QT, NPH, D]), ACT.Copy)\
                .then_inc(pw_ready, 1)
            act.wait_ge(turned, 1)
            act.activation(pw[:, 0:4 * HT, :].rearrange("p g o -> p (g o)"), c_ps[:, 0, :], ACT.Copy).then_inc(pw_ready, 1)
            act.activation(pw[:, 4 * HT:6 * HT, :].rearrange("p g o -> p (g o)"), c_ps[:, 1, 0:2 * P], ACT.Copy)\
                .then_inc(pw_ready, 1)

            act.wait_ge(std_in, 1)
            act.activation(bn["std"][:, :], bn["ve"][:, :], ACT.Sqrt).then_inc(std_out, 1)

            def weights_high(h, par):
                act.wait_ge(w_prod, h + 1)
                at_least(act, c_full, 3 * STEPS * (h - 1))
                act.activation(wh[par][:, :, :], wprod[:, :, :, :].rearrange("p k a o -> p k (a o)"), ACT.Copy)\
                    .then_inc(w_hi, 1)

            def split(s, j, use):
                act.wait_ge(raw_loaded[j % 2], 48 * use)
                at_least(act, c_full, 3 * (s - 1))
                act.activation(dh[j % 2][:, :, :], raw[j % 2][:, :, :], ACT.Copy).then_inc(hi_ready, 1)

            split(0, 0, 1)
            weights_high(0, 0)

            def body(i, last):
                for hp, h, j, s in steps_of(i):
                    end = last and hp == 1
                    if not (end and j == STEPS - 1):
                        split(s + 1, j + 1, 4 * i + 2 * hp + (j + 1) // 2 + 1)
                    act.wait_ge(c_full, 3 * s + 1)
                    at_least(act, stored[j % 2], 16 * (4 * i + 2 * hp + j // 2))
                    act.activation(qy[:, j % 2, :], c_ps[:, j % 2, :], ACT.Relu).then_inc(q_out, 1)
                    if j == 2 and not end:
                        weights_high(h + 1, 1 - hp)
                    act.wait_ge(c_full, 3 * s + 2)
                    at_least(act, kt_full, s)
                    act.activation(ky[:, :], c_ps[:, (j + 1) % 2, :], ACT.Relu).then_inc(k_out, 1)
                    act.wait_ge(kt_full, s + 1)
                    at_least(act, vk_full, s)
                    act.activation(kT[:, :, :].rearrange("p a c -> p (a c)"), kt_ps[:, :], ACT.Copy).then_inc(k_taken, 1)
            over_head_pairs(act, body)
            act.wait_ge(pr_turned, 1)
            act.activation(K["projT"][:, :, :].rearrange("p k c -> p (k c)"), s_ps[:, :, :].rearrange("p a n -> p (a n)"),
                           ACT.Copy).then_inc(pr_ready, 1)
            act.wait_ge(pr_turned, 2)
            act.activation(K["spread"][:, :, :].rearrange("p t c -> p (t c)"), kt_ps[:, :], ACT.Copy).then_inc(pr_ready, 1)

        @block.tensor
        def _(pe):
            pe.wait_ge(pw_ready, 1)
            for t in range(QT):
                dst = c_ps[:, t // 4, P * (t % 4):P * (t % 4) + P]
                last = pe.transpose(dst, pw_rep[:, t, :, :].rearrange("p a c -> p (a c)"), K["ident"][:, :])
            last.then_inc(turned, 1)
            pe.wait_ge(pw_ready, 3)
            pe.wait_ge(init, 1)

            def convolve(s, j, par, kind):
                if kind == 0:
                    pe.wait_ge(lo_ready, s + 1)
                if kind == 0:
                    at_least(pe, k_out, s)
                elif kind == 1:
                    at_least(pe, v_out, s)
                else:
                    pe.wait_ge(q_out, s + 1)
                k = 0
                for dy in range(2):
                    for dx in range(2):
                        o = (1 - dx) * 4 * TAP * D + (1 - dy) * P
                        for w, d in ((wh, dh), (wl, dh), (wh, dl)):
                            src = d[j % 2][:, kind, :].rearrange("p (b y x) -> p b y x", b=2, x=PBK)[:, :, dy:dy + NB, dx:dx + NB]
                            last = pe.matmul(c_ps[:, (j + kind) % 2, :], w[par][:, kind, o:o + P], src,
                                             start=(k == 0), stop=(k == 11))
                            k += 1
                last.then_inc(c_full, 1)

            def turn(s, src, ps, ready, taken, full):
                pe.wait_ge(ready, s + 1)
                at_least(pe, taken, s)
                for a in range(4):
                    last = pe.transpose(ps[:, P * a:P * a + P], src[:, P * a:P * a + P], K["ident"][:, :])
                last.then_inc(full, 1)

            def sum_vk(s):
                pe.wait_ge(k_taken, s + 1)
                pe.wait_ge(v_taken, s + 1)
                at_least(pe, diag_ready, 2 * s)
                for b in range(2):
                    for half in range(2):
                        a = 2 * b + half
                        last = pe.matmul(vk_ps[:, VW * b:VW * b + VW], kT[:, a, :], vT[:, a, :],
                                         start=(half == 0), stop=(half == 1))
                last.then_inc(vk_full, 1)

            def body(i, last):
                for hp, h, j, s in steps_of(i):
                    prev = not isinstance(s, int) or s >= 1
                    if j == 0:
                        pe.wait_ge(w_lo, h + 1)
                    convolve(s, j, hp, 0)
                    if prev:
                        turn(s - 1, vy, vt_ps, v_out, v_taken, vt_full)
                    convolve(s, j, hp, 1)
                    if prev:
                        sum_vk(s - 1)
                    convolve(s, j, hp, 2)
                    turn(s, ky, kt_ps, k_out, k_taken, kt_full)
            over_head_pairs(pe, body)
            s = AH * STEPS - 1
            turn(s, vy, vt_ps, v_out, v_taken, vt_full)
            sum_vk(s)
            pe.wait_ge(k_taken, s + 1)
            pe.wait_ge(pr_scaled, 1)
            for kt in range(KT):
                for o in range(CT):
                    n0 = C * (kt % 2) + P * o
                    last = pe.transpose(s_ps[:, kt // 2, n0:n0 + P], prs[:, o, P * kt:P * kt + P], K["ident"][:, :])
            last.then_inc(pr_turned, 1)
            pe.wait_ge(pr_scaled, 3)
            for t in range(KT):
                last = pe.transpose(kt_ps[:, P * t:P * t + P], pick[:, t, :, :].rearrange("p a c -> p (a c)"), K["ident"][:, :])
            last.then_inc(pr_turned, 1)
            pe.wait_ge(pr_ready, 1)
            pe.wait_ge(summed, AH * STEPS)
            for n in range(AH // 4):
                at_least(pe, s_taken, n - 1)
                pe.matmul(s_ps[:, n % 2, 0:4 * B * (D + 1)], K["same_ch"][:, :],
                          sums[:, 4 * n:4 * n + 4, :, :].rearrange("p h b n -> p (h b n)"), start=True, stop=True)\
                    .then_inc(s_full, 1)

        @block.vector
        def _(dve):
            dve.memset(vT[:, :, P:VW], 1.0).then_inc(init, 1)
            chain = Chain(dve, bn_link)
            dve.wait_ge(K["bn_loaded"], 16 * 4)
            chain(dve.tensor_scalar(bn["ve"][:, :], bn["var"][:, :], BN_EPS, None, ALU.add))
            dve.tensor_copy(bn["t1"][:, :], bn["ve"][:, :]).then_inc(std_in, 1)
            dve.wait_ge(std_out, 1)
            chain(dve.reciprocal(bn["r0"][:, :], bn["std"][:, :]))
            chain(dve.tensor_tensor(bn["t2"][:, :], bn["r0"][:, :], bn["r0"][:, :], ALU.mult))
            chain(dve.tensor_tensor(bn["t3"][:, :], bn["t2"][:, :], bn["ve"][:, :], ALU.mult))
            chain(dve.tensor_scalar(bn["mi"][:, :], bn["t3"][:, :], -0.5, 1.5, ALU.mult, ALU.add))
            chain(dve.tensor_tensor(bn["r"][:, :], bn["r0"][:, :], bn["mi"][:, :], ALU.mult))
            chain(dve.tensor_tensor(bn["inv"][:, :], bn["r"][:, :], bn["gamma"][:, :], ALU.mult))
            chain(dve.tensor_tensor(bn["std"][:, :], bn["inv"][:, :], bn["mean"][:, :], ALU.mult))
            chain(dve.tensor_tensor(bn["shift"][:, :], bn["beta"][:, :], bn["std"][:, :], ALU.subtract))
            dve.wait_ge(pw_ready, 3)
            dve.wait_ge(taps_loaded[0], 16)


            def weights(h):
                at_least(dve, w_lo, h)
                at_least(dve, w_hi, h)
                tv = taps[:, :, :].rearrange("p (k h) n -> p k h n", k=3)[:, :, bass.ds(h, 1), :]
                pv = pw[:, :, :].rearrange("p (k h) o -> p k h o", k=3)[:, :, bass.ds(h, 1), :]
                tv = tv.rearrange("p k a n -> p k (a n)").unsqueeze(3).broadcast_to([P, 3, TT, D])
                pv = pv.broadcast_to([P, 3, TT, D])
                dve.tensor_tensor(wprod[:, :, :, :], tv, pv, ALU.mult).then_inc(w_prod, 1)

            def turned(s):
                dve.wait_ge(vt_full, s + 1)
                at_least(dve, vk_full, s)
                dve.tensor_copy(vT[:, :, 0:P], vt_ps[:, :].rearrange("p (a c) -> p a c", a=4)).then_inc(v_taken, 1)

            def keep_diagonal(h, j, s):
                at = sums[:, bass.ds(h, 1), 2 * j:2 * j + 2, :]
                prod = vk_ps[:, 0:2 * VW].rearrange("p (b n) -> p b n", b=2)
                dve.wait_ge(vk_full, s + 1)
                dve.tensor_tensor(diag[:, :, :], prod[:, :, 0:P], K["gmask"][:, :].unsqueeze(1).broadcast_to([P, 2, P]),
                                  ALU.mult).then_inc(diag_ready, 1)
                dve.tensor_copy(at[:, :, :, D:D + 1], prod[:, :, P:VW].unsqueeze(1)).then_inc(diag_ready, 1)
                dve.wait_ge(diag_ready, 2 * s + 1)
                dve.tensor_reduce(at[:, :, :, 0:D], diag[:, :, :].rearrange("p b (a d) -> p b d a", d=D).unsqueeze(1),
                                  AX.X, ALU.add).then_inc(summed, 1)

            weights(0)
            dve.wait_ge(hi_ready, 1)
            dve.tensor_tensor(dl[0][:, :, :], raw[0][:, :, :], dh[0][:, :, :].bitcast(F32), ALU.subtract).then_inc(lo_ready, 1)
            dve.wait_ge(pr_loaded, 16)
            for o in range(CT):
                last = dve.tensor_scalar(prs[:, o, :], pr_raw[:, o, :], bn["inv"][:, o:o + 1], None, ALU.mult)
            last.then_inc(pr_scaled, 1)
            dve.memset(pick[:, :, :, :], 0.0).then_inc(pr_scaled, 1)
            dve.wait_ge(pr_scaled, 2)
            heads = K["gmask"][:, :].rearrange("p (h c) -> p h c", c=D)[:, :, 0]
            for t in range(KT):
                for c in range(2):
                    last = dve.tensor_copy(pick[:, t, c, HT * t:HT * t + HT], heads)
            last.then_inc(pr_scaled, 1)
            dve.wait_ge(taps_loaded[1], 16)

            def body(i, last):
                for hp, h, j, s in steps_of(i):
                    end = last and hp == 1
                    if not isinstance(s, int) or s >= 1:
                        turned(s - 1)
                        keep_diagonal(h if j else h - 1, (j - 1) % STEPS, s - 1)
                    if j == 1 and not end:
                        weights(h + 1)
                    dve.wait_ge(c_full, 3 * s + 3)
                    at_least(dve, vt_full, s)
                    dve.tensor_copy(vy[:, :], c_ps[:, j % 2, :]).then_inc(v_out, 1)
            over_head_pairs(dve, body)
            s = AH * STEPS - 1
            turned(s)
            keep_diagonal(AH - 1, STEPS - 1, s)
            for n in range(AH // 4):
                dve.wait_ge(s_full, n + 1)
                dve.tensor_tensor(sums[:, 4 * n:4 * n + 4, :, :].rearrange("p h b n -> p h (b n)"),
                                  s_ps[:, n % 2, 0:4 * B * (D + 1)].rearrange("p (h n) -> p h n", h=4),
                                  heads[:, 4 * n % HT:4 * n % HT + 4].unsqueeze(2).broadcast_to([P, 4, B * (D + 1)]), ALU.mult)\
                    .then_inc(s_taken, 1)
            dve.wait_ge(s_taken, AH // 4)
            for t in range(2):
                dve.tensor_reduce(K["vk"][:, 2 + t, :, :].rearrange("p b n -> p (b n)"),
                                  sums[:, HT * t:HT * t + HT, :, :].rearrange("p h b n -> p (b n) h"), AX.X, ALU.add)


def output(nc, K, x1_dram, qkv_dram, yq_dram, out_dram):
    with ExitStack() as ctx:
        def sb(name, shape, dt=F32):
            return ctx.enter_context(nc.sbuf_tensor(name, shape, dt))

        def psum(name, shape):
            return ctx.enter_context(nc.psum_tensor(name, shape, F32))

        def sem(name):
            return ctx.enter_context(nc.semaphore(name))

        UNITS, NCH = 4, 8
        HEADS = KT * HT
        projT, spread, bn = K["projT"], K["spread"], K["bn"]
        ks = [sb(f"ks{i}", [P, KT, HEADS]) for i in range(2)]
        vkm = sb("vkm", [P, KT, P])
        vkT = sb("vkT", [P, KT, P])
        fh = [sb(f"fh{i}", [P, KT, C], F32R) for i in range(2)]
        fl = [sb(f"fl{i}", [P, KT, C], F32R) for i in range(2)]
        x1 = [sb(f"ox{i}", [P, CT, H * W]) for i in range(2)]
        q_in = sb("q_in", [P, 4, 2, 2 * PN])
        q = sb("q", [P, 4, KT, 512])
        qh = sb("qh", [P, 2, KT, 512], F32R)
        ql = sb("ql", [P, 2, KT, 512], F32R)
        rec = sb("orec", [P, 512])
        rh = sb("rh", [P, 2, 512], F32R)
        rl = sb("rl", [P, 2, 512], F32R)

        den_ps = psum("oden_ps", [P, 512])
        bc_ps = psum("bc_ps", [P, 2, 512])
        z_ps = psum("z_ps", [P, 2, 2, 512])
        f_ps = psum("f_ps", [P, 512])

        zeroed = sem("ks_zeroed")
        x_loaded = [sem(f"ox_loaded{i}") for i in range(2)]
        x_stored = [sem(f"ox_stored{i}") for i in range(2)]
        q_loaded = [sem(f"q_loaded{i}") for i in range(4)]
        y_loaded = [sem(f"y_loaded{i}") for i in range(4)]
        q_relu, x_shifted = sem("q_relu"), sem("x_shifted")
        den_full, den_taken, rec_ready, rh_ready, rl_ready = (sem(n) for n in
                                                              ("den_full", "den_taken", "rec_ready", "rh_ready", "rl_ready"))
        bc_full, q_scaled = sem("bc_full"), sem("q_scaled")
        qh_ready, ql_pool, ql_dve = sem("qh_ready"), sem("ql_pool"), sem("ql_dve")
        z_full, z_taken = sem("z_full"), sem("z_taken")
        vkm_ready, vk_turned, vkT_ready = sem("vkm_ready"), sem("vk_turned"), sem("vkT_ready")
        f_full, fh_ready, fl_ready, ks_ready = sem("f_full"), sem("fh_ready"), sem("fl_ready"), sem("ks_ready")

        block = ctx.enter_context(nc.Block())

        def units_of(i, last_body):
            for par in range(2):
                b = 2 * i + par
                for u in range(UNITS):
                    yield b, par, u, UNITS * b + u, not (last_body and par == 1)

        def load_q(eng, b, n):
            p0 = 4 * ((n // 2 + 2) % 4) + 2 * ((n + 1) % 2)
            for t in range(2):
                eng.dma_start(q_in[:, n % 4, t, :], qkv_dram[P * t:P * t + P, p0:p0 + 2, b, :])\
                    .then_inc(q_loaded[n % 4], 16)

        @block.sync
        def _(sp):
            own = Own(sp, K["taps_out"])

            def load(b, par):
                sp.dma_start(x1[par][:, :, :], x1_dram[b, :, :].rearrange("(t p) n -> p t n", p=P))\
                    .then_inc(x_loaded[par], 16)

            sp.wait_ge(y_loaded[3], 32)
            load(0, 0)

            def body(i, last_body):
                for par in range(2):
                    b = 2 * i + par
                    if isinstance(b, int) and b == 0:
                        load(1, 1)
                    elif not (last_body and par == 1):
                        own.wait_ge(x_stored[1 - par], 16 * (i + par))
                        load(b + 1, 1 - par)
                    own.wait_ge(z_taken, 2 * NCH * (b + 1))
                    sp.dma_start(out_dram[b, :, :].rearrange("(t p) n -> p t n", p=P), x1[par][:, :, :])\
                        .then_inc(x_stored[par], 16)
            over_image_pairs(sp, body)
            for par in range(2):
                sp.wait_ge(x_stored[par], 16 * (B // 2))

        @block.gpsimd
        def _(pool):
            def low(k, r):
                pool.wait_ge(qh_ready, 2 * k + 1)
                pool.tensor_tensor(ql[:, r % 2, 0:2, :], q[:, r, 0:2, :], qh[:, r % 2, 0:2, :].bitcast(F32), ALU.subtract)\
                    .then_inc(ql_pool, 1)

            def load_y(b, n):
                for t in range(2):
                    pool.dma_start(q[:, n % 4, 2 + t, :], yq_dram[P * t:P * t + P, 2 * n:2 * n + 2, b, :])\
                        .then_inc(y_loaded[n % 4], 16)

            def next_q(b, u, c, g, nxt):
                if u < UNITS - 3 or nxt:
                    pool.wait_ge(q_relu, 2 * g + 4)
                    n = 2 * u + 6 + c
                    load_q(pool, b if n < NCH else b + 1, n % NCH)

            def next_y(b, n, k, nxt):
                if n < 4 or nxt:
                    pool.wait_ge(ql_dve, k + 1)
                    load_y(b if n < 4 else b + 1, (n + 4) % NCH)

            for n in (0, 2):
                load_q(pool, 0, n)
                load_q(pool, 0, n + 1)
                load_y(0, n)
                load_y(0, n + 1)
            pool.wait_ge(q_relu, 2)
            load_q(pool, 0, 4)
            load_q(pool, 0, 5)
            low(0, 0)

            def body(i, last_body):
                for b, par, u, g, nxt in units_of(i, last_body):
                    r = 2 * (u % 2)
                    next_y(b, 2 * u, 2 * g, nxt)
                    next_q(b, u, 0, g, nxt)
                    low(2 * g + 1, r + 1)
                    next_q(b, u, 1, g, nxt)
                    next_y(b, 2 * u + 1, 2 * g + 1, nxt)
                    if nxt or u < UNITS - 1:
                        low(2 * g + 2, 2 - r)
            over_image_pairs(pool, body)

        @block.scalar
        def _(act):
            def relu(u, c, r, use, k):
                row = u // 2
                act.wait_ge(q_loaded[r], 32 * use)
                if k is not None:
                    act.wait_ge(ql_pool, k + 1)
                for t in range(2):
                    src = q_in[:, r, t, :].rearrange("p (a y x) -> p a y x", a=2, x=PBK)
                    last = act.activation(q[:, r, t, :].rearrange("p (a y x) -> p a y x", a=2, x=NB),
                                          src[:, :, row:row + NB, c:c + NB], ACT.Relu)
                last.then_inc(q_relu, 1)

            def high(k, r, half):
                act.wait_ge(q_scaled, 2 * k + half + 1)
                at_least(act, z_full, 2 * (k - 1))
                act.activation(qh[:, r % 2, 2 * half:2 * half + 2, :], q[:, r, 2 * half:2 * half + 2, :], ACT.Copy)\
                    .then_inc(qh_ready, 1)

            def rec_high(g, r):
                act.wait_ge(rec_ready, 2 * g + 2)
                at_least(act, bc_full, 4 * (g - 1))
                act.activation(rh[:, r, :], rec[:, :], ACT.Copy).then_inc(rh_ready, 1)

            def vk_out(b):
                act.wait_ge(vk_turned, b + 1)
                act.activation(vkT[:, :, :].rearrange("p t c -> p (t c)"), f_ps[:, :], ACT.Copy).then_inc(vkT_ready, 1)

            def fold_high(b, par, half):
                act.wait_ge(f_full, 2 * b + half + 1)
                at_least(act, z_full, 2 * NCH * (b - 1))
                act.activation(fh[par][:, 2 * half:2 * half + 2, :].rearrange("p t c -> p (t c)"), f_ps[:, :], ACT.Copy)\
                    .then_inc(fh_ready, 1)

            def shift(b, par, use, piece):
                if piece == 0:
                    act.wait_ge(x_loaded[par], 16 * use)
                o, n0 = piece // 4, 1024 * (piece % 4)
                act.activation(x1[par][:, o, n0:n0 + 1024], x1[par][:, o, n0:n0 + 1024], ACT.Identity,
                               bias=bn["shift"][:, o:o + 1]).then_inc(x_shifted, 1)

            vk_out(0)
            fold_high(0, 0, 0)
            fold_high(0, 0, 1)
            relu(0, 0, 0, 1, None)
            relu(0, 1, 1, 1, None)
            rec_high(0, 0)
            high(0, 0, 0)
            high(0, 0, 1)
            relu(1, 0, 2, 1, None)
            relu(1, 1, 3, 1, None)
            for piece in range(8):
                shift(0, 0, 1, piece)

            def body(i, last_body):
                for b, par, u, g, nxt in units_of(i, last_body):
                    r = 2 * (u % 2)
                    more = nxt or u < UNITS - 1

                    def shift_next(p0):
                        if u >= 2 and nxt:
                            for piece in (p0, p0 + 1):
                                shift(b + 1, 1 - par, i + par + 1, 4 * (u - 2) + piece)

                    def relu_next(c):
                        if nxt or u < UNITS - 2:
                            relu((u + 2) % UNITS, c, r + c, 2 * (2 * i + par) + u // 2 + 2, 2 * g + c)
                    high(2 * g + 1, r + 1, 0)
                    high(2 * g + 1, r + 1, 1)
                    if nxt and u == 1:
                        vk_out(b + 1)
                    if nxt and u >= 2:
                        fold_high(b + 1, 1 - par, u - 2)
                    shift_next(0)
                    if more:
                        rec_high(g + 1, (u + 1) % 2)
                        relu_next(0)
                        high(2 * g + 2, 2 - r, 0)
                        relu_next(1)
                        high(2 * g + 2, 2 - r, 1)
                        shift_next(2)
            over_image_pairs(act, body)

        @block.tensor
        def _(pe):
            def turn_vk(b):
                pe.wait_ge(vkm_ready, b + 1)
                at_least(pe, fh_ready, 2 * b)
                at_least(pe, fl_ready, 2 * b)
                for t in range(KT):
                    last = pe.transpose(f_ps[:, P * t:P * t + P], vkm[:, t, :], K["ident"][:, :])
                last.then_inc(vk_turned, 1)

            def fold(b, half):
                pe.wait_ge(vkT_ready, b + 1)
                at_least(pe, fh_ready, 2 * b + half)
                at_least(pe, fl_ready, 2 * b + half)
                for t in range(2):
                    last = pe.matmul(f_ps[:, C * t:C * t + C], vkT[:, 2 * half + t, :], projT[:, 2 * half + t, :],
                                     start=True, stop=True)
                last.then_inc(f_full, 1)

            def denominators(g, c, r, par, b, use):
                if c == 0:
                    pe.wait_ge(ks_ready, b + 1)
                    at_least(pe, den_taken, 2 * g)
                pe.wait_ge(q_relu, 2 * g + c + 1)
                pe.wait_ge(y_loaded[r], 32 * use)
                for t in range(KT):
                    last = pe.matmul(den_ps[HEADS * c:HEADS * c + HEADS, :], ks[par][:, t, :], q[:, r, t, :],
                                     start=(t == 0), stop=(t == KT - 1))
                last.then_inc(den_full, 1)

            def unit_ready(g):
                pe.wait_ge(rh_ready, g + 1)
                pe.wait_ge(rl_ready, g + 1)

            def to_channels(k, c, r, half):
                at_least(pe, q_scaled, 2 * k + half)
                rows = slice(HEADS * c, HEADS * c + HEADS)
                for t in range(2):
                    for m, half_of in enumerate((rh, rl)):
                        last = pe.matmul(bc_ps[:, t, :], spread[rows, 2 * half + t, :], half_of[rows, r, :],
                                         start=(m == 0), stop=(m == 1))
                last.then_inc(bc_full, 1)

            def project(k, r, par, o):
                if o == 0:
                    pe.wait_ge(qh_ready, 2 * k + 2)
                    pe.wait_ge(ql_pool, k + 1)
                    pe.wait_ge(ql_dve, k + 1)
                at_least(pe, z_taken, 2 * k - 3 + o)
                m = 0
                for t in range(KT):
                    for w, d in ((fh, qh), (fl, qh), (fh, ql)):
                        last = pe.matmul(z_ps[:, r % 2, o, :], w[par][:, t, P * o:P * o + P], d[:, r % 2, t, :],
                                         start=(m == 0), stop=(m == 3 * KT - 1))
                        m += 1
                last.then_inc(z_full, 1)

            turn_vk(0)
            fold(0, 0)
            fold(0, 1)
            denominators(0, 0, 0, 0, 0, 1)
            denominators(0, 1, 1, 0, 0, 1)
            unit_ready(0)
            to_channels(0, 0, 0, 0)
            to_channels(0, 0, 0, 1)

            def body(i, last_body):
                for b, par, u, g, nxt in units_of(i, last_body):
                    r = 2 * (u % 2)
                    more = nxt or u < UNITS - 1
                    def next_denominators(c):
                        use = 2 * (2 * i + par) + (u + 1) // 2 + 1
                        if u < UNITS - 1:
                            denominators(g + 1, c, 2 - r + c, par, b, use)
                        else:
                            denominators(g + 1, c, 2 - r + c, 1 - par, b + 1, use)
                    if more:
                        next_denominators(0)
                    to_channels(2 * g + 1, 1, u % 2, 0)
                    if more:
                        next_denominators(1)
                    if nxt and u == 1:
                        turn_vk(b + 1)
                    if nxt and u >= 2:
                        fold(b + 1, u - 2)
                    if u == 0:
                        pe.wait_ge(fh_ready, 2 * (b + 1))
                        pe.wait_ge(fl_ready, 2 * (b + 1))
                    to_channels(2 * g + 1, 1, u % 2, 1)
                    project(2 * g, r, par, 0)
                    project(2 * g, r, par, 1)
                    project(2 * g + 1, r + 1, par, 0)
                    if more:
                        unit_ready(g + 1)
                        to_channels(2 * g + 2, 0, (u + 1) % 2, 0)
                    project(2 * g + 1, r + 1, par, 1)
                    if more:
                        to_channels(2 * g + 2, 0, (u + 1) % 2, 1)
            over_image_pairs(pe, body)

        @block.vector
        def _(dve):
            heads = K["gmask"][:, :].rearrange("p (h c) -> p h c", c=D)[:, :, 0]
            for par in range(2):
                dve.memset(ks[par][:, :, :], 0.0).then_inc(zeroed, 1)
            dve.wait_ge(zeroed, 2)

            def tables(b, par):
                at = K["vk"][:, :, bass.ds(b, 1), :]
                at_least(dve, vk_turned, b)
                dve.tensor_tensor(vkm[:, :, :].rearrange("p t (a d) -> p t a d", d=D),
                                  K["gmask"][:, :].rearrange("p (a d) -> p a d", d=D).unsqueeze(1).broadcast_to([P, KT, HT, D]),
                                  at[:, :, :, 0:D].broadcast_to([P, KT, HT, D]), ALU.mult).then_inc(vkm_ready, 1)
                at_least(dve, den_full, NCH * (b - 1))
                for t in range(KT):
                    last = dve.tensor_tensor(ks[par][:, t, HT * t:HT * t + HT].unsqueeze(1), heads.unsqueeze(1),
                                             at[:, t, :, D:D + 1].broadcast_to([P, 1, HT]), ALU.mult)
                last.then_inc(ks_ready, 1)

            def fold_low(b, par, half):
                dve.wait_ge(fh_ready, 2 * b + half + 1)
                dve.tensor_tensor(fl[par][:, 2 * half:2 * half + 2, :].rearrange("p t c -> p (t c)"), f_ps[:, :],
                                  fh[par][:, 2 * half:2 * half + 2, :].rearrange("p t c -> p (t c)").bitcast(F32),
                                  ALU.subtract).then_inc(fl_ready, 1)

            def reciprocals(g, half):
                if half == 0:
                    dve.wait_ge(den_full, 2 * g + 2)
                    at_least(dve, rh_ready, g)
                n = slice(256 * half, 256 * half + 256)
                dve.tensor_scalar(rec[:, n], den_ps[:, n], ATT_EPS, None, ALU.add).then_inc(den_taken, 1)
                dve.wait_ge(den_taken, 2 * g + half + 1)
                dve.reciprocal(rec[:, n], rec[:, n]).then_inc(rec_ready, 1)

            def rec_low(g, r):
                dve.wait_ge(rh_ready, g + 1)
                dve.tensor_tensor(rl[:, r, :], rec[:, :], rh[:, r, :].bitcast(F32), ALU.subtract).then_inc(rl_ready, 1)

            def scale(k, r, half):
                dve.wait_ge(bc_full, 2 * k + half + 1)
                dve.tensor_tensor(q[:, r, 2 * half:2 * half + 2, :], q[:, r, 2 * half:2 * half + 2, :], bc_ps[:, :, :], ALU.mult)\
                    .then_inc(q_scaled, 1)

            def low(k, r):
                dve.wait_ge(qh_ready, 2 * k + 2)
                dve.tensor_tensor(ql[:, r % 2, 2:4, :], q[:, r, 2:4, :], qh[:, r % 2, 2:4, :].bitcast(F32), ALU.subtract)\
                    .then_inc(ql_dve, 1)

            def add(k, n, par, o):
                dve.wait_ge(z_full, 2 * k + o + 1)
                py, px = n // 2, 2 * (n % 2)
                img = x1[par][:, o, :].rearrange("p (y py x px) -> p py px y x", py=4, x=NB, px=4)[:, py, px:px + 2, :, :]
                dve.tensor_tensor(img, z_ps[:, n % 2, o, :].rearrange("p (a y x) -> p a y x", a=2, x=NB), img,
                                  ALU.add).then_inc(z_taken, 1)

            tables(0, 0)
            fold_low(0, 0, 0)
            fold_low(0, 0, 1)
            reciprocals(0, 0)
            reciprocals(0, 1)
            rec_low(0, 0)
            scale(0, 0, 0)
            scale(0, 0, 1)
            low(0, 0)

            def body(i, last_body):
                for b, par, u, g, nxt in units_of(i, last_body):
                    r = 2 * (u % 2)
                    more = nxt or u < UNITS - 1
                    scale(2 * g + 1, r + 1, 0)
                    if more:
                        reciprocals(g + 1, 0)
                    scale(2 * g + 1, r + 1, 1)
                    low(2 * g + 1, r + 1)
                    if more:
                        reciprocals(g + 1, 1)
                        rec_low(g + 1, (u + 1) % 2)
                    if nxt and u == 0:
                        tables(b + 1, 1 - par)
                    if nxt and u >= 2:
                        fold_low(b + 1, 1 - par, u - 2)
                    if u == 0:
                        dve.wait_ge(x_shifted, 8 * (b + 1))
                    add(2 * g, 2 * u, par, 0)
                    add(2 * g, 2 * u, par, 1)
                    add(2 * g + 1, 2 * u + 1, par, 0)
                    if more:
                        scale(2 * g + 2, 2 - r, 0)
                        scale(2 * g + 2, 2 - r, 1)
                        low(2 * g + 2, 2 - r)
                    add(2 * g + 1, 2 * u + 1, par, 1)
            over_image_pairs(dve, body)


def build(nc, a, out, scratch):
    with ExitStack() as ctx:
        K = {}
        two_phases = ctx.enter_context(ExitStack())
        make_constants(nc, ctx, two_phases, K)
        window_mixing(nc, K, a["x"], a["L0_conv_w"], a["L0_conv_b"], a["L1_conv_w_qkv"], a["L1_conv_w_dw"],
                      scratch["x1"], scratch["taps"])
        projections(nc, K, scratch["x1"], scratch["qkv"], a["L1_conv_w_pw"],
                    {"gamma": a["L1_conv_bn_gamma"], "beta": a["L1_conv_bn_beta"], "mean": a["L1_conv_bn_mean"],
                     "var": a["L1_conv_bn_var"]}, scratch["taps"], scratch["taps_sorted"])
        two_phases.close()
        K["projT"] = ctx.enter_context(nc.sbuf_tensor("projT", [P, KT, C], F32))
        K["spread"] = ctx.enter_context(nc.sbuf_tensor("spread", [P, KT, P], F32R))
        convolved_heads(nc, K, a["L1_conv_w_proj"], scratch["taps_sorted"], scratch["qkv"], scratch["yq"])
        output(nc, K, scratch["x1"], scratch["qkv"], scratch["yq"], out.rearrange("b c h w -> b c (h w)"))



_INS = ["x", "L0_conv_w", "L0_conv_b", "L1_conv_w_qkv", "L1_conv_w_dw", "L1_conv_w_pw", "L1_conv_w_proj",
        "L1_conv_bn_gamma", "L1_conv_bn_beta", "L1_conv_bn_mean", "L1_conv_bn_var"]


def kernel(**inputs):
    import numpy as np
    import concourse.bacc as bacc
    from concourse.bass_utils import run_bass_kernel_spmd

    nc = bacc.Bacc("TRN2", target_bir_lowering=False, num_devices=1)
    arrays, aps = {}, {}
    for name in _INS:
        arr = np.ascontiguousarray(inputs[name])
        arrays[f"in_{name}"] = arr
        aps[name] = nc.dram_tensor(f"in_{name}", arr.shape, mybir.dt.from_np(arr.dtype), kind="ExternalInput").ap()
    out = nc.dram_tensor("out_0", (B, C, H, W), F32, kind="ExternalOutput").ap()
    scratch = {
        "x1": nc.dram_tensor("x1_scratch", (B, C, H * W), F32, kind="Internal").ap(),
        "qkv": nc.dram_tensor("qkv_scratch", (3 * C, NPH, B, PN), F32, kind="Internal").ap(),
        "yq": nc.dram_tensor("yq_scratch", (C, NPH, B, POS), F32, kind="Internal").ap(),
        "taps_sorted": nc.dram_tensor("tap_sorted", (P, QT * HT, TAP * TAP), F32, kind="Internal").ap(),
        "taps": nc.dram_tensor("tap_scratch", (QT, P, NPH, TAP * TAP), F32, kind="Internal").ap(),
    }
    build(nc, aps, out, scratch)
    r = run_bass_kernel_spmd(nc, [arrays], core_ids=[0])
    return r.results[0]["out_0"]
```
